# Optimizing a Trainium2 kernel written in Bass

```python
import numpy as np
import jax
import jax.numpy as jnp

def _softmax(x, axis=-1):
    return jax.nn.softmax(x, axis=axis)

def _gelu(x):
    return jax.nn.gelu(x, approximate=True)

def _silu(x):
    return jax.nn.silu(x)

def _sigmoid(x):
    return jax.nn.sigmoid(x)

def _layernorm(x, axis=-1, eps=1e-05):
    m = jnp.mean(x, axis=axis, keepdims=True)
    v = jnp.var(x, axis=axis, keepdims=True)
    return (x - m) / jnp.sqrt(v + eps)

def _scatter_add(tgt, idx, src, axis=0):
    return tgt.at[idx].add(src)

def _segment_sum(src, seg, n):
    return jax.ops.segment_sum(src, seg, n)
kernel_name = 'mk_hybrid_d1_jaxref_r8_430000'

def setup_inputs(seed: int=0):
    np.random.seed(seed)
    _w = jnp.asarray

    def _L0_attn_a_setup():
        import jax, jax.numpy as jnp
        import numpy as np
        D_MODEL = 128
        N_HEADS = 16
        FEAT_DIM = 16
        V_DIM = 64
        EPS = 1e-12

        def taylor_exp(x):
            d = x.shape[-1]
            rd = jnp.sqrt(jnp.float32(d))
            rrd = jnp.sqrt(rd)
            r2 = jnp.sqrt(jnp.float32(2.0))
            x2 = (x[..., :, None] * x[..., None, :]).reshape(*x.shape[:-1], d * d) / r2
            ones = jnp.ones(x.shape[:-1] + (1,), dtype=x.dtype)
            return jnp.concatenate([ones, x / rrd, x2 / rd], axis=-1)
        key = jax.random.key(seed)
        k0, k1, k2, k3, k4 = jax.random.split(key, 5)
        b, l = (2, 256)
        scale = 1.0 / np.sqrt(D_MODEL)
        return {'hidden_states': jax.random.normal(k0, (b, l, D_MODEL), dtype=jnp.float32), 'Wq': jax.random.normal(k1, (D_MODEL, N_HEADS * FEAT_DIM), dtype=jnp.float32) * scale, 'Wk': jax.random.normal(k2, (D_MODEL, N_HEADS * FEAT_DIM), dtype=jnp.float32) * scale, 'Wv': jax.random.normal(k3, (D_MODEL, N_HEADS * V_DIM), dtype=jnp.float32) * scale, 'Wo': jax.random.normal(k4, (N_HEADS * V_DIM, D_MODEL), dtype=jnp.float32) * scale}
    _L0_attn_a_in = _L0_attn_a_setup()

    def _L0_attn_b_setup():
        import jax, jax.numpy as jnp
        import numpy as np
        B, T, C = (4, 256, 128)

        def wkv(k, v, w, u, reverse):

            def step(carry, kv):
                num, den, mx = carry
                k_t, v_t = kv
                ku = k_t + u
                m = jnp.maximum(mx, ku)
                e1 = jnp.exp(mx - m)
                e2 = jnp.exp(ku - m)
                y = (e1 * num + e2 * v_t) / (e1 * den + e2)
                mw = mx + w
                mn = jnp.maximum(mw, k_t)
                e1s = jnp.exp(mw - mn)
                e2s = jnp.exp(k_t - mn)
                return ((e1s * num + e2s * v_t, e1s * den + e2s, mn), y)
            z = jnp.zeros_like(k[:, 0])
            init = (z, z, jnp.full_like(z, -1e+38))
            ks = jnp.swapaxes(k, 0, 1)
            vs = jnp.swapaxes(v, 0, 1)
            _, ys = jax.lax.scan(step, init, (ks, vs), reverse=reverse)
            return jnp.swapaxes(ys, 0, 1)
        key = jax.random.key(seed)
        k1, k2, k3, k4, k5, k6, k7 = jax.random.split(key, 7)
        x = jax.random.normal(k1, (B, T, C), dtype=jnp.float32)
        rkv_w = jax.random.normal(k2, (6 * C, C), dtype=jnp.float32) / np.sqrt(C)
        out_w = jax.random.normal(k3, (C, 2 * C), dtype=jnp.float32) / np.sqrt(2 * C)
        time_decay = jax.random.uniform(k4, (C,), jnp.float32, -6.0, -5.0)
        time_first = jax.random.uniform(k5, (C,), jnp.float32, -3.0, 0.0)
        time_decay_rev = jax.random.uniform(k6, (C,), jnp.float32, -6.0, -5.0)
        time_first_rev = jax.random.uniform(k7, (C,), jnp.float32, -3.0, 0.0)
        return {'x': x, 'rkv_w': rkv_w, 'out_w': out_w, 'time_decay': time_decay, 'time_first': time_first, 'time_decay_rev': time_decay_rev, 'time_first_rev': time_first_rev}
    _L0_attn_b_in = _L0_attn_b_setup()

    def _L0_ffn_setup():
        import jax, jax.numpy as jnp
        import numpy as np
        DIM = 128
        DEPTH = 2
        HEADS = 8
        DIM_HEAD = 64
        WINDOW = 64
        INNER = HEADS * DIM_HEAD
        HID = int(DIM * 4 * 2 / 3)
        B, N = (2, 1024)
        QK_SCALE = 8.0

        def shift_token(t):
            t1, t2 = jnp.split(t, 2, axis=-1)
            t2 = jnp.pad(t2, ((0, 0), (1, 0), (0, 0)))[:, :-1]
            return jnp.concatenate([t1, t2], axis=-1)

        def l2norm(t):
            return t / jnp.clip(jnp.linalg.norm(t, axis=-1, keepdims=True), 1e-12)

        def rotate_half(x):
            x1, x2 = jnp.split(x, 2, axis=-1)
            return jnp.concatenate([-x2, x1], axis=-1)

        def rotary_xpos(q, k):
            n = q.shape[-2]
            half_idx = jnp.arange(0, DIM_HEAD, 2, dtype=jnp.float32)
            inv_freq = 1.0 / 10000.0 ** (half_idx / DIM_HEAD)
            t = jnp.arange(n, dtype=jnp.float32)
            freqs = t[:, None] * inv_freq[None, :]
            freqs = jnp.concatenate([freqs, freqs], axis=-1)
            base = (half_idx + 0.4 * DIM_HEAD) / (1.4 * DIM_HEAD)
            power = (t - n // 2) / float(WINDOW // 2)
            scale = base[None, :] ** power[:, None]
            scale = jnp.concatenate([scale, scale], axis=-1)
            cos, sin = (jnp.cos(freqs), jnp.sin(freqs))
            q = q * cos * scale + rotate_half(q) * sin * scale
            k = k * cos / scale + rotate_half(k) * sin / scale
            return (q, k)

        def local_attention(q, k, v):
            b, h, n, d = q.shape
            w = n // WINDOW
            bq = q.reshape(b, h, w, WINDOW, d) * QK_SCALE
            bk = k.reshape(b, h, w, WINDOW, d)
            bv = v.reshape(b, h, w, WINDOW, d)

            def look_around(t):
                p = jnp.pad(t, ((0, 0), (0, 0), (1, 0), (0, 0), (0, 0)))
                return jnp.concatenate([p[:, :, :w], p[:, :, 1:]], axis=3)
            bk, bv = (look_around(bk), look_around(bv))
            bt = jnp.arange(n).reshape(w, WINDOW)
            btp = jnp.pad(bt, ((1, 0), (0, 0)), constant_values=-1)
            btk = jnp.concatenate([btp[:w], btp[1:]], axis=1)
            sim = jnp.einsum('bhwid,bhwjd->bhwij', bq, bk)
            i = bt[:, :, None]
            j = btk[:, None, :]
            mask = (i < j) | (i > j + WINDOW) | (j == -1)
            sim = jnp.where(mask, -jnp.finfo(sim.dtype).max, sim)
            attn = jax.nn.softmax(sim, axis=-1)
            out = jnp.einsum('bhwij,bhwjd->bhwid', attn, bv)
            return out.reshape(b, h, n, d)

        def _layer(x, wqkv, qs, ksc, wo, lg, lb, w1, b1, w2, b2):
            b, n, _ = x.shape
            h = shift_token(x)
            qkv = h @ wqkv
            q, k, v = jnp.split(qkv, 3, axis=-1)
            to_heads = lambda t: t.reshape(b, n, HEADS, DIM_HEAD).transpose(0, 2, 1, 3)
            q, k, v = (to_heads(q), to_heads(k), to_heads(v))
            q = l2norm(q) * qs
            k = l2norm(k) * ksc
            q, k = rotary_xpos(q, k)
            o = local_attention(q, k, v)
            o = o.transpose(0, 2, 1, 3).reshape(b, n, INNER)
            x = x + o @ wo
            h = shift_token(x)
            mu = h.mean(-1, keepdims=True)
            var = h.var(-1, keepdims=True)
            h = (h - mu) / jnp.sqrt(var + 1e-05) * lg + lb
            h = h @ w1 + b1
            a, g = jnp.split(h, 2, axis=-1)
            h = a * jax.nn.gelu(g, approximate=False)
            x = x + h @ w2 + b2
            return x
        key = jax.random.key(seed)
        ks = jax.random.split(key, 6)
        return {'x': jax.random.normal(ks[0], (B, N, DIM), jnp.float32), 'wqkv': jax.random.normal(ks[1], (DEPTH, DIM, 3 * INNER), jnp.float32) * 0.02, 'q_scale': jnp.ones((DEPTH, DIM_HEAD), jnp.float32), 'k_scale': jnp.ones((DEPTH, DIM_HEAD), jnp.float32), 'wo': jax.random.normal(ks[2], (DEPTH, INNER, DIM), jnp.float32) * 0.02, 'ln_g': jnp.ones((DEPTH, DIM), jnp.float32), 'ln_b': jnp.zeros((DEPTH, DIM), jnp.float32), 'w1': jax.random.normal(ks[3], (DEPTH, DIM, 2 * HID), jnp.float32) * 0.02, 'b1': jnp.zeros((DEPTH, 2 * HID), jnp.float32), 'w2': jax.random.normal(ks[4], (DEPTH, HID, DIM), jnp.float32) * 0.02, 'b2': jnp.zeros((DEPTH, DIM), jnp.float32)}
    _L0_ffn_in = _L0_ffn_setup()
    _d = {'L0_attn_a_hidden_states': _L0_attn_a_in['hidden_states'], 'L0_attn_a_Wq': _L0_attn_a_in['Wq'], 'L0_attn_a_Wk': _L0_attn_a_in['Wk'], 'L0_attn_a_Wv': _L0_attn_a_in['Wv'], 'L0_attn_a_Wo': _L0_attn_a_in['Wo'], 'L0_attn_b_rkv_w': _L0_attn_b_in['rkv_w'], 'L0_attn_b_out_w': _L0_attn_b_in['out_w'], 'L0_attn_b_time_decay': _L0_attn_b_in['time_decay'], 'L0_attn_b_time_first': _L0_attn_b_in['time_first'], 'L0_attn_b_time_decay_rev': _L0_attn_b_in['time_decay_rev'], 'L0_attn_b_time_first_rev': _L0_attn_b_in['time_first_rev'], 'L0_ffn_wqkv': _L0_ffn_in['wqkv'], 'L0_ffn_q_scale': _L0_ffn_in['q_scale'], 'L0_ffn_k_scale': _L0_ffn_in['k_scale'], 'L0_ffn_wo': _L0_ffn_in['wo'], 'L0_ffn_ln_g': _L0_ffn_in['ln_g'], 'L0_ffn_ln_b': _L0_ffn_in['ln_b'], 'L0_ffn_w1': _L0_ffn_in['w1'], 'L0_ffn_b1': _L0_ffn_in['b1'], 'L0_ffn_w2': _L0_ffn_in['w2'], 'L0_ffn_b2': _L0_ffn_in['b2']}
    _x0 = _d['L0_attn_a_hidden_states']
    _d['L0_attn_a_hidden_states'] = jax.random.normal(jax.random.fold_in(jax.random.key(seed), 1), (2, 1024, 128), dtype=_x0.dtype)
    del _x0
    return _d

def reference(L0_attn_a_hidden_states, L0_attn_a_Wq, L0_attn_a_Wk, L0_attn_a_Wv, L0_attn_a_Wo, L0_attn_b_rkv_w, L0_attn_b_out_w, L0_attn_b_time_decay, L0_attn_b_time_first, L0_attn_b_time_decay_rev, L0_attn_b_time_first_rev, L0_ffn_wqkv, L0_ffn_q_scale, L0_ffn_k_scale, L0_ffn_wo, L0_ffn_ln_g, L0_ffn_ln_b, L0_ffn_w1, L0_ffn_b1, L0_ffn_w2, L0_ffn_b2):

    def _L0_attn_a_ref(hidden_states, Wq, Wk, Wv, Wo):
        import jax, jax.numpy as jnp
        import numpy as np
        D_MODEL = 128
        N_HEADS = 16
        FEAT_DIM = 16
        V_DIM = 64
        EPS = 1e-12

        def taylor_exp(x):
            d = x.shape[-1]
            rd = jnp.sqrt(jnp.float32(d))
            rrd = jnp.sqrt(rd)
            r2 = jnp.sqrt(jnp.float32(2.0))
            x2 = (x[..., :, None] * x[..., None, :]).reshape(*x.shape[:-1], d * d) / r2
            ones = jnp.ones(x.shape[:-1] + (1,), dtype=x.dtype)
            return jnp.concatenate([ones, x / rrd, x2 / rd], axis=-1)
        b, l, _ = hidden_states.shape
        q = (hidden_states @ Wq).reshape(b, l, N_HEADS, FEAT_DIM).transpose(0, 2, 1, 3)
        k = (hidden_states @ Wk).reshape(b, l, N_HEADS, FEAT_DIM).transpose(0, 2, 1, 3)
        v = (hidden_states @ Wv).reshape(b, l, N_HEADS, V_DIM).transpose(0, 2, 1, 3)
        qf = taylor_exp(q)
        kf = taylor_exp(k)
        A = jnp.einsum('bhnf,bhmf->bhnm', qf, kf)
        A = jnp.tril(A)
        y = jnp.einsum('bhnm,bhme->bhne', A, v)
        z = 1.0 / (jnp.einsum('bhlf,bhlf->bhl', qf, jnp.cumsum(kf, axis=2)) + EPS)
        y = y * z[..., None]
        out = y.transpose(0, 2, 1, 3).reshape(b, l, N_HEADS * V_DIM) @ Wo
        return out

    def _L0_attn_b_ref(x, rkv_w, out_w, time_decay, time_first, time_decay_rev, time_first_rev):
        import jax, jax.numpy as jnp
        import numpy as np
        B, T, C = (4, 256, 128)

        def wkv(k, v, w, u, reverse):

            def step(carry, kv):
                num, den, mx = carry
                k_t, v_t = kv
                ku = k_t + u
                m = jnp.maximum(mx, ku)
                e1 = jnp.exp(mx - m)
                e2 = jnp.exp(ku - m)
                y = (e1 * num + e2 * v_t) / (e1 * den + e2)
                mw = mx + w
                mn = jnp.maximum(mw, k_t)
                e1s = jnp.exp(mw - mn)
                e2s = jnp.exp(k_t - mn)
                return ((e1s * num + e2s * v_t, e1s * den + e2s, mn), y)
            z = jnp.zeros_like(k[:, 0])
            init = (z, z, jnp.full_like(z, -1e+38))
            ks = jnp.swapaxes(k, 0, 1)
            vs = jnp.swapaxes(v, 0, 1)
            _, ys = jax.lax.scan(step, init, (ks, vs), reverse=reverse)
            return jnp.swapaxes(ys, 0, 1)
        b, t, c = x.shape
        rkv = jnp.einsum('btc,dc->btd', x, rkv_w).reshape(b, t, 2, 3, c)
        r_f, k_f, v_f = (rkv[:, :, 0, 0], rkv[:, :, 0, 1], rkv[:, :, 0, 2])
        r_b, k_b, v_b = (rkv[:, :, 1, 0], rkv[:, :, 1, 1], rkv[:, :, 1, 2])
        out_f = jax.nn.sigmoid(r_f) * wkv(k_f, v_f, -jnp.exp(time_decay), time_first, False)
        out_b = jax.nn.sigmoid(r_b) * wkv(k_b, v_b, -jnp.exp(time_decay_rev), time_first_rev, True)
        out_cat = jnp.concatenate([out_f, out_b], axis=-1)
        return jnp.einsum('btd,cd->btc', out_cat, out_w)

    def _L0_ffn_ref(x, wqkv, q_scale, k_scale, wo, ln_g, ln_b, w1, b1, w2, b2):
        import jax, jax.numpy as jnp
        import numpy as np
        DIM = 128
        DEPTH = 2
        HEADS = 8
        DIM_HEAD = 64
        WINDOW = 64
        INNER = HEADS * DIM_HEAD
        HID = int(DIM * 4 * 2 / 3)
        B, N = (2, 1024)
        QK_SCALE = 8.0

        def shift_token(t):
            t1, t2 = jnp.split(t, 2, axis=-1)
            t2 = jnp.pad(t2, ((0, 0), (1, 0), (0, 0)))[:, :-1]
            return jnp.concatenate([t1, t2], axis=-1)

        def l2norm(t):
            return t / jnp.clip(jnp.linalg.norm(t, axis=-1, keepdims=True), 1e-12)

        def rotate_half(x):
            x1, x2 = jnp.split(x, 2, axis=-1)
            return jnp.concatenate([-x2, x1], axis=-1)

        def rotary_xpos(q, k):
            n = q.shape[-2]
            half_idx = jnp.arange(0, DIM_HEAD, 2, dtype=jnp.float32)
            inv_freq = 1.0 / 10000.0 ** (half_idx / DIM_HEAD)
            t = jnp.arange(n, dtype=jnp.float32)
            freqs = t[:, None] * inv_freq[None, :]
            freqs = jnp.concatenate([freqs, freqs], axis=-1)
            base = (half_idx + 0.4 * DIM_HEAD) / (1.4 * DIM_HEAD)
            power = (t - n // 2) / float(WINDOW // 2)
            scale = base[None, :] ** power[:, None]
            scale = jnp.concatenate([scale, scale], axis=-1)
            cos, sin = (jnp.cos(freqs), jnp.sin(freqs))
            q = q * cos * scale + rotate_half(q) * sin * scale
            k = k * cos / scale + rotate_half(k) * sin / scale
            return (q, k)

        def local_attention(q, k, v):
            b, h, n, d = q.shape
            w = n // WINDOW
            bq = q.reshape(b, h, w, WINDOW, d) * QK_SCALE
            bk = k.reshape(b, h, w, WINDOW, d)
            bv = v.reshape(b, h, w, WINDOW, d)

            def look_around(t):
                p = jnp.pad(t, ((0, 0), (0, 0), (1, 0), (0, 0), (0, 0)))
                return jnp.concatenate([p[:, :, :w], p[:, :, 1:]], axis=3)
            bk, bv = (look_around(bk), look_around(bv))
            bt = jnp.arange(n).reshape(w, WINDOW)
            btp = jnp.pad(bt, ((1, 0), (0, 0)), constant_values=-1)
            btk = jnp.concatenate([btp[:w], btp[1:]], axis=1)
            sim = jnp.einsum('bhwid,bhwjd->bhwij', bq, bk)
            i = bt[:, :, None]
            j = btk[:, None, :]
            mask = (i < j) | (i > j + WINDOW) | (j == -1)
            sim = jnp.where(mask, -jnp.finfo(sim.dtype).max, sim)
            attn = jax.nn.softmax(sim, axis=-1)
            out = jnp.einsum('bhwij,bhwjd->bhwid', attn, bv)
            return out.reshape(b, h, n, d)

        def _layer(x, wqkv, qs, ksc, wo, lg, lb, w1, b1, w2, b2):
            b, n, _ = x.shape
            h = shift_token(x)
            qkv = h @ wqkv
            q, k, v = jnp.split(qkv, 3, axis=-1)
            to_heads = lambda t: t.reshape(b, n, HEADS, DIM_HEAD).transpose(0, 2, 1, 3)
            q, k, v = (to_heads(q), to_heads(k), to_heads(v))
            q = l2norm(q) * qs
            k = l2norm(k) * ksc
            q, k = rotary_xpos(q, k)
            o = local_attention(q, k, v)
            o = o.transpose(0, 2, 1, 3).reshape(b, n, INNER)
            x = x + o @ wo
            h = shift_token(x)
            mu = h.mean(-1, keepdims=True)
            var = h.var(-1, keepdims=True)
            h = (h - mu) / jnp.sqrt(var + 1e-05) * lg + lb
            h = h @ w1 + b1
            a, g = jnp.split(h, 2, axis=-1)
            h = a * jax.nn.gelu(g, approximate=False)
            x = x + h @ w2 + b2
            return x
        for l in range(DEPTH):
            x = _layer(x, wqkv[l], q_scale[l], k_scale[l], wo[l], ln_g[l], ln_b[l], w1[l], b1[l], w2[l], b2[l])
        return x
    x = L0_attn_a_hidden_states
    x = x + _L0_attn_a_ref(_layernorm(x, axis=-1), L0_attn_a_Wq, L0_attn_a_Wk, L0_attn_a_Wv, L0_attn_a_Wo)
    x = x + _L0_ffn_ref(_layernorm(x, axis=-1), L0_ffn_wqkv, L0_ffn_q_scale, L0_ffn_k_scale, L0_ffn_wo, L0_ffn_ln_g, L0_ffn_ln_b, L0_ffn_w1, L0_ffn_b1, L0_ffn_w2, L0_ffn_b2)
    x = x + _L0_attn_b_ref(_layernorm(x, axis=-1), L0_attn_b_rkv_w, L0_attn_b_out_w, L0_attn_b_time_decay, L0_attn_b_time_first, L0_attn_b_time_decay_rev, L0_attn_b_time_first_rev)
    x = x + _L0_ffn_ref(_layernorm(x, axis=-1), L0_ffn_wqkv, L0_ffn_q_scale, L0_ffn_k_scale, L0_ffn_wo, L0_ffn_ln_g, L0_ffn_ln_b, L0_ffn_w1, L0_ffn_b1, L0_ffn_w2, L0_ffn_b2)
    return x

_drawn_inputs = setup_inputs


def setup_inputs(seed=0):
    import zlib

    import numpy as np

    out = dict(_drawn_inputs(seed))
    spreads = {'L0_ffn_q_scale': (1.0, 0.6),
     'L0_ffn_k_scale': (1.0, 0.6),
     'L0_ffn_ln_g': (1.0, 0.6),
     'L0_ffn_ln_b': (0.0, 0.8),
     'L0_ffn_b1': (0.0, 0.8),
     'L0_ffn_b2': (0.0, 0.1)}
    factors = {'L0_attn_b_time_decay': 8.0,
     'L0_attn_b_time_first': 8.0,
     'L0_attn_b_time_decay_rev': 8.0,
     'L0_attn_b_time_first_rev': 8.0,
     'L0_ffn_w1': 3.874,
     'L0_ffn_w2': 3.804}
    for name, (base, spread) in spreads.items():
        noise = np.random.default_rng([zlib.crc32(name.encode()), seed]).standard_normal(out[name].shape)
        drawn = base * np.exp(spread * noise) if base else spread * noise
        out[name] = jnp.asarray(drawn.astype(out[name].dtype))
    for name, factor in factors.items():
        out[name] = (out[name] * factor).astype(out[name].dtype)
    return out
```

```python
import math
from contextlib import ExitStack

import numpy as np

import concourse.bass as bass
from concourse import mybir

B, N, D = 2, 1024, 128
P = 128
NT = N // P
TOK = B * N
CH = 512
NCH = TOK // CH
LN_EPS = 1e-5

AH, AF, AV = 16, 16, 64
HG = 4
NHG = AH // HG
PAIRS = [(0, 0), (0, 1), (0, 2), (1, 0), (1, 1), (2, 0)]
KROWS = AF * len(PAIRS)
UNITS = [(j, i) for j in range(NT) for i in range(j + 1)]
NU = len(UNITS)

DEPTH, HEADS, DH, WIN = 2, 8, 64, 64
INNER = HEADS * DH
HID = int(D * 4 * 2 / 3)
HC = [(c * P, min(P, HID - c * P)) for c in range(-(-HID // P))]
NG = DEPTH * NT
QK_SCALE = 8.0
NEG = -1e30
SS_SHIFT = 65536.0

F32 = mybir.dt.float32
BF16 = mybir.dt.bfloat16
ALU = mybir.AluOpType
ACT = mybir.ActivationFunctionType
AX = mybir.AxisListType
COL_LN_G, COL_LN_B, COL_B2, COL_B1 = 0, DEPTH, 2 * DEPTH, 3 * DEPTH
COL_R = COL_B1 + DEPTH * 2 * len(HC)
COLS = COL_R + 4
EXP_SET = "natural_log_exp_and_others"


def shape_constants():
    ident = np.eye(P, dtype=np.float32)
    mean = np.full((P, P), 1.0 / D, np.float32)
    ones = np.ones((P, P), np.float32)
    m, n = np.arange(P)[:, None], np.arange(P)[None, :]
    causal = (m <= n).astype(np.float32)
    square = np.stack([ident, ident - mean, mean, ones, causal], axis=1)
    q, k = np.arange(WIN)[:, None], np.arange(WIN)[None, :]
    own = np.where(k <= q, 0.0, NEG)
    prev = np.where(k >= q, 0.0, NEG)
    none = np.full((WIN, WIN), NEG)
    mask = np.zeros((P, NT, P), np.float32)
    for t in range(NT):
        mask[:WIN, t] = np.concatenate([own, prev if t else none], axis=1)
        mask[WIN:, t] = np.concatenate([prev, own], axis=1)
    half = np.arange(0, DH, 2, dtype=np.float32)
    inv_freq = (1.0 / np.float32(10000.0) ** (half / np.float32(DH))).astype(np.float32)
    t = np.arange(N, dtype=np.float32)
    freqs = (t[:, None] * inv_freq[None, :]).astype(np.float32)
    freqs = np.concatenate([freqs, freqs], axis=-1).astype(np.float64)
    base = ((half + 0.4 * DH) / (1.4 * DH)).astype(np.float32)
    power = ((t - N // 2) / float(WIN // 2)).astype(np.float32)
    scale = base[None, :].astype(np.float64) ** power[:, None].astype(np.float64)
    scale = np.concatenate([scale, scale], axis=-1)
    sign = np.where(np.arange(DH) < DH // 2, -1.0, 1.0)
    cos, sin = np.cos(freqs), np.sin(freqs) * sign
    rot = np.stack([cos * scale * QK_SCALE, cos / scale, sin * scale * QK_SCALE, sin / scale])
    rot = rot.reshape(4, NT, P, DH).transpose(2, 0, 1, 3).astype(np.float32)
    return (np.ascontiguousarray(square), np.ascontiguousarray(mask.astype(mybir.dt.np(BF16))),
            ident.astype(mybir.dt.np(BF16)), np.ascontiguousarray(rot))


def build(nc, t_in, out):
    nc.disable_value_cache = True
    ctx = ExitStack()
    with ctx:
        def sem(name):
            return ctx.enter_context(nc.semaphore(name))

        def at_least(eng, s, value):
            if isinstance(value, int) and value <= 0:
                return
            eng.wait_ge(s, value)

        ps = [ctx.enter_context(nc.psum_tensor(f"bank{i}", [P, CH], F32)) for i in range(8)]

        def sb(name, shape, dt=F32, stack=None):
            return (stack or ctx).enter_context(nc.sbuf_tensor(name, shape, dt))

        xT = sb("xT", [P, B, N])
        y0 = sb("y0", [P, B, 1 + N])
        square = sb("square", [P, 5, P])
        identB = sb("identB", [P, P], BF16)
        ident, centre, mean, ones, causal = (square[:, k, :] for k in range(5))
        cols = sb("cols", [P, COLS])
        eps_col = sb("eps_col", [P, 3])
        ln_sqr = sb("ln_sqr", [P, 2, CH])
        ln_log = sb("ln_log", [P, 2, CH])
        ln_inv = sb("ln_inv", [P, 2, CH])

        dram = nc.dram_tensor("parts_dram", [2, 3, AH * AF, TOK], BF16, kind="Internal").ap()

        ld_x, ld_const = sem("ld_x"), sem("ld_const")
        set_up, x_turned, x_in = sem("set_up"), sem("x_turned"), sem("x_in")
        ln_added, ln_centred, ln_squared = sem("ln_added"), sem("ln_centred"), sem("ln_squared")
        ln_var, ln_logged, ln_scaled, ln_done = (sem("ln_var"), sem("ln_logged"), sem("ln_scaled"),
                                                 sem("ln_done"))
        st = sem("stored")

        def y0_chunk(c):
            b, h = divmod(c * CH, N)
            return y0[:, b, 1 + h:1 + h + CH]

        def x_chunk(c):
            b, h = divmod(c * CH, N)
            return xT[:, b, h:h + CH]

        def ln_tensor(pe, n, x_ready):
            base = NCH * n

            def variance(c):
                pe.wait_ge(ln_squared, base + c + 1)
                pe.matmul(ps[6 + c % 2][:, :], mean, ln_sqr[:, c % 2, :],
                          start=True, stop=True).then_inc(ln_var, 1)

            for c in range(NCH):
                x_ready(pe, c)
                if c >= 2:
                    pe.wait_ge(ln_done, base + c - 1)
                pe.matmul(ps[4 + c % 2][:, :], centre, x_chunk(c), start=True, stop=True)\
                    .then_inc(ln_centred, 1)
                if c >= 1:
                    variance(c - 1)
            variance(NCH - 1)

        def ln_scalar(act, n):
            base = NCH * n
            act.preload_act_table_set(EXP_SET)

            def inverse(c):
                act.wait_ge(ln_var, base + c + 1)
                act.activation(ln_log[:, c % 2, :], ps[6 + c % 2][:, :], ACT.Ln, bias=eps_col[:, 0:1])\
                    .then_inc(ln_logged, 1)
                act.wait_ge(ln_logged, base + c + 1)
                at_least(act, ln_done, base + c - 1 if c >= 2 else 0)
                act.activation(ln_inv[:, c % 2, :], ln_log[:, c % 2, :], ACT.Exp, scale=-0.5)\
                    .then_inc(ln_scaled, 1)

            for c in range(NCH):
                act.wait_ge(ln_centred, base + c + 1)
                if c >= 2:
                    act.wait_ge(ln_var, base + c - 1)
                act.activation(ln_sqr[:, c % 2, :], ps[4 + c % 2][:, :], ACT.Square)\
                    .then_inc(ln_squared, 1)
                if c >= 1:
                    inverse(c - 1)
            inverse(NCH - 1)

        def ln_vector(dve, n):
            for c in range(NCH):
                dve.wait_ge(ln_scaled, NCH * n + c + 1)
                dve.tensor_tensor(y0_chunk(c), ps[4 + c % 2][:, :], ln_inv[:, c % 2, :], ALU.mult)\
                    .then_inc(ln_done, 1)

        def add_stream(dve):
            for c in range(NCH):
                dve.tensor_tensor(x_chunk(c), x_chunk(c), y0_chunk(c), ALU.add).then_inc(ln_added, 1)

        y_done = sem("y_done")
        a_x = sem("a_x")
        r_x = sem("r_x")
        x_ready = [lambda e, c: e.wait_ge(x_in, c + 1),
                   lambda e, c: e.wait_ge(a_x, 2 * B * NHG + 2),
                   lambda e, c: e.wait_ge(ln_added, c + 1),
                   lambda e, c: e.wait_ge(r_x, c + 1)]

        with ExitStack() as s0:
            x_tok = sb("x_tok", [P, TOK // P, D], stack=s0)
            with nc.Block() as block:
                @block.sync
                def _(sp):
                    for c in range(NCH):
                        sp.dma_start(x_tok[:, 4 * c:4 * c + 4, :],
                                     t_in["x"].rearrange("b (t p) d -> p (b t) d", p=P)[:, 4 * c:4 * c + 4, :])\
                            .then_inc(ld_x, 16)
                        if c == 0:
                            sp.dma_start(square[:, :, :], t_in["square"]).then_inc(ld_const, 16)
                            sp.dma_start(identB[:, :], t_in["identB"]).then_inc(ld_const, 16)
                            sp.dma_start(cols[:, :], t_in["cols"]).then_inc(ld_const, 16)

                @block.gpsimd
                def _(pool):
                    pool.memset(eps_col[:, 0:1], LN_EPS).then_inc(set_up, 1)
                    pool.memset(eps_col[:, 1:2], 0.5 * math.log(SS_SHIFT)).then_inc(set_up, 1)
                    pool.memset(eps_col[:, 2:3], 1.0).then_inc(set_up, 1)
                    pool.memset(y0[:, :, 0:1], 0.0).then_inc(set_up, 1)

                @block.tensor
                def _(pe):
                    pe.wait_ge(ld_const, 48)
                    pe.wait_ge(ld_x, 16 * NCH)
                    for c in range(NCH):
                        for k in range(4):
                            last = pe.transpose(ps[c][:, k * P:(k + 1) * P], x_tok[:, 4 * c + k, :], ident)
                        last.then_inc(x_turned, 1)
                    ln_tensor(pe, 0, x_ready[0])

                @block.scalar
                def _(act):
                    act.wait_ge(set_up, 4)
                    for c in range(NCH):
                        act.wait_ge(x_turned, c + 1)
                        act.copy(x_chunk(c), ps[c][:, :]).then_inc(x_in, 1)
                    ln_scalar(act, 0)

                @block.vector
                def _(dve):
                    ln_vector(dve, 0)

        linear_attention(nc, t_in, sb, sem, ps, dram, xT, y0, ident, ones, causal, eps_col,
                         a_x, at_least, y0_chunk)

        def normalise(n, eng):
            if eng is nc.tensor:
                ln_tensor(eng, n, x_ready[n])
            elif eng is nc.scalar:
                ln_scalar(eng, n)
            else:
                if n == 2:
                    add_stream(eng)
                ln_vector(eng, n)

        def norm_block(n):
            with nc.Block() as block:
                @block.tensor
                def _(pe):
                    ln_tensor(pe, n, x_ready[n])

                @block.scalar
                def _(act):
                    ln_scalar(act, n)

                @block.vector
                def _(dve):
                    ln_vector(dve, n)

        F = ffn_sems(sem)
        ffn_args = (y0, y_done, ident, centre, mean, identB, eps_col, cols, at_least)
        norm_block(1)
        ffn(nc, t_in, sb, ps, F, 0, *ffn_args)
        rwkv(nc, t_in, sb, sem, ps, xT, y0, cols, r_x,
             lambda eng: normalise(2, eng), lambda eng, c: eng.wait_ge(ln_done, 2 * NCH + c + 1))
        norm_block(3)
        ffn(nc, t_in, sb, ps, F, 1, *ffn_args)
        with nc.Block() as block:
            @block.vector
            def _(dve):
                add_stream(dve)

        store_out(nc, sb, sem, ps, out, xT, ident, st)


def store_out(nc, sb, sem, ps, out, xT, ident, st):
    turned, copied = sem("out_turned"), sem("out_copied")
    with ExitStack() as stack:
        o_tok = sb("o_tok", [P, TOK // P, D], stack=stack)
        with nc.Block() as block:
            @block.tensor
            def _(pe):
                for c in range(NCH):
                    for k in range(4):
                        b, t = divmod(4 * c + k, NT)
                        last = pe.transpose(ps[c][:, k * P:(k + 1) * P], xT[:, b, t * P:(t + 1) * P], ident)
                    last.then_inc(turned, 1)

            @block.scalar
            def _(act):
                for c in range(0, NCH, 2):
                    act.wait_ge(turned, c + 1)
                    act.copy(o_tok[:, 4 * c:4 * c + 4, :], ps[c][:, :]).then_inc(copied, 1)

            copied2 = sem("out_copied2")

            @block.vector
            def _(dve):
                for c in range(1, NCH, 2):
                    dve.wait_ge(turned, c + 1)
                    dve.tensor_copy(o_tok[:, 4 * c:4 * c + 4, :], ps[c][:, :]).then_inc(copied2, 1)

            @block.sync
            def _(sp):
                for c in range(NCH):
                    sp.wait_ge((copied, copied2)[c % 2], c // 2 + 1)
                    sp.dma_start(out.rearrange("b (t p) d -> p (b t) d", p=P)[:, 4 * c:4 * c + 4, :],
                                 o_tok[:, 4 * c:4 * c + 4, :]).then_inc(st, 16)
                sp.wait_ge(st, 16 * NCH)


def linear_attention(nc, t_in, sb, sem, ps, parts, xT, y0, ident, ones, causal, eps_col,
                     a_x, at_least, y0_chunk):
    NV = AV + 1
    NS, NA = 3, 4
    ld_w, ld_wo = sem("a_ld_w"), sem("a_ld_wo")
    proj, p1_done, r1_done, p2_done, p3_done = (sem("a_proj"), sem("a_p1_done"), sem("a_r1_done"),
                                                sem("a_p2_done"), sem("a_p3_done"))
    parts_out, stacked, v_copied = sem("a_parts_out"), sem("a_stacked"), sem("a_v_copied")
    v_proj, v_by_act, v_by_dve, v_ones = sem("a_v_proj"), sem("a_v_by_act"), sem("a_v_by_dve"), sem("a_v_ones")
    scored, squared, weighed, diagonal = sem("a_scored"), sem("a_squared"), sem("a_weighed"), sem("a_diagonal")
    prefixed, prefix_used = sem("a_prefixed"), sem("a_prefix_used")
    z_in, z_inv, y_out = sem("a_z_in"), sem("a_z_inv"), sem("a_y_out")
    y_turned, y_copied, heads_out = sem("a_y_turned"), sem("a_y_copied"), sem("a_heads_out")
    NIT = B * NHG
    with ExitStack() as stack:
        def s(name, shape, dt=F32):
            return sb(name, shape, dt, stack)
        wqk = s("wqk", [P, 2, AH * AF])
        values = s("values", [P, B * NT, AH, NV])
        with ExitStack() as early:
            wv = sb("wv", [P, AH * AV], F32, early)
            part = sb("part", [P, 4, 3, TOK], BF16, early)
            rest = sb("rest", [P, 2, CH], F32, early)

            with nc.Block() as block:
                @block.sync
                def _(sp):
                    sp.dma_start(wqk[:, 0, :], t_in["a_wq"]).then_inc(ld_w, 16)
                    sp.dma_start(wqk[:, 1, :], t_in["a_wk"]).then_inc(ld_w, 16)
                    sp.dma_start(wv[:, :], t_in["a_wv"]).then_inc(ld_w, 16)
                    for c in range(NCH):
                        sp.wait_ge(p3_done, 4 * (c + 1))
                        for g in range(4):
                            sp.dma_start(parts[g // 2, :, (g % 2) * P:(g % 2 + 1) * P, c * CH:(c + 1) * CH]
                                         .rearrange("a p n -> p a n"),
                                         part[:, g, :, c * CH:(c + 1) * CH]).then_inc(parts_out, 16)
                    sp.wait_ge(parts_out, 16 * 4 * NCH)

                @block.gpsimd
                def _(pool):
                    pool.memset(values[:, :, :, AV:NV], 1.0).then_inc(v_ones, 1)

                @block.tensor
                def _(pe):
                    pe.wait_ge(ld_w, 48)
                    for u in range(4 * NCH):
                        c, g = divmod(u, 4)
                        at_least(pe, r1_done, u - 3)
                        pe.matmul(ps[u % 4][:, :], wqk[:, g // 2, (g % 2) * P:(g % 2 + 1) * P], y0_chunk(c),
                                  start=True, stop=True).then_inc(proj, 1)
                        for v in range(2 * u, 2 * u + 2):
                            b, j = divmod(u, NT)
                            at_least(pe, (v_by_act, v_by_dve)[v % 2], v // 2 - 1)
                            pe.matmul(ps[4 + v % 4][:, :], y0[:, b, 1 + j * P:1 + (j + 1) * P],
                                      wv[:, (v % 2) * CH:(v % 2 + 1) * CH], start=True, stop=True)\
                                .then_inc(v_proj, 1)

                def copy_values(eng, v):
                    return (values[:, v // 2, 8 * (v % 2):8 * (v % 2) + 8, 0:AV],
                            ps[4 + v % 4][:, :].rearrange("p (h e) -> p h e", h=8))

                @block.scalar
                def _(act):
                    def second(u):
                        act.wait_ge(r1_done, u + 1)
                        act.copy(part[:, u % 4, 1, (u // 4) * CH:(u // 4 + 1) * CH], rest[:, u % 2, :])\
                            .then_inc(p2_done, 1)
                    for u in range(4 * NCH):
                        act.wait_ge(proj, u + 1)
                        act.copy(part[:, u % 4, 0, (u // 4) * CH:(u // 4 + 1) * CH], ps[u % 4][:, :])\
                            .then_inc(p1_done, 1)
                        if u >= 1:
                            second(u - 1)
                        act.wait_ge(v_proj, 2 * u + 1)
                        act.copy(*copy_values(act, 2 * u)).then_inc(v_by_act, 1)
                    second(4 * NCH - 1)

                @block.vector
                def _(dve):
                    def third(u):
                        dve.wait_ge(p2_done, u + 1)
                        at = slice((u // 4) * CH, (u // 4 + 1) * CH)
                        dve.tensor_tensor(part[:, u % 4, 2, at], rest[:, u % 2, :], part[:, u % 4, 1, at],
                                          ALU.subtract).then_inc(p3_done, 1)
                    for u in range(4 * NCH):
                        dve.wait_ge(p1_done, u + 1)
                        at_least(dve, p3_done, u - 1)
                        at = slice((u // 4) * CH, (u // 4 + 1) * CH)
                        dve.tensor_tensor(rest[:, u % 2, :], ps[u % 4][:, :], part[:, u % 4, 0, at],
                                          ALU.subtract).then_inc(r1_done, 1)
                        if u >= 1:
                            third(u - 1)
                        dve.wait_ge(v_proj, 2 * u + 2)
                        dve.tensor_copy(*copy_values(dve, 2 * u + 1)).then_inc(v_by_dve, 1)
                    third(4 * NCH - 1)

        v_prefix = s("v_prefix", [P, 2, HG, NV])
        v_now = s("v_now", [P, 2, NT, HG, NV])
        q_stack = s("q_stack", [P, 2, HG, N], BF16)
        k_stack = s("k_stack", [P, 2, HG, N], BF16)
        wo_slot = s("wo_slot", [P, 2, D])
        sq = s("sq", [P, NA, HG, P])
        sq_diag = s("sq_diag", [P, 2, HG, P])
        z_sum = s("z_sum", [P, 2, HG])
        z_rec = s("z_rec", [P, 2, HG])
        y_tok = s("y_tok", [P, 2, HG * AV])
        y_feat = s("y_feat", [P, 2, N])
        score_bank = ps[0:NS]
        y_bank = ps[3:5]
        turn_bank = ps[5]
        out_bank = ps[6:8]
        with nc.Block() as block:
            @block.sync
            def _(sp):
                with sp.Fori(0, NIT) as it:
                    b, hg = sp.snap(it // NHG), sp.snap(it % NHG)
                    sp.wait_ge(heads_out, it * 2 + 2)
                    for qk, st_ in enumerate((q_stack, k_stack)):
                        for r, pair in enumerate(PAIRS):
                            src = parts[qk, pair[qk], bass.ds(hg * (HG * AF), HG * AF), bass.ds(b * N, N)]
                            sp.dma_start(st_[r * AF:(r + 1) * AF, bass.ds(it % 2, 1), :, :],
                                         src.rearrange("(h f) n -> f h n", h=HG)).then_inc(stacked, 16)
                    sp.wait_ge(stacked, (it + 1) * (16 * 2 * len(PAIRS)))
                    sp.wait_ge(heads_out, it * 2 + 4)
                    sp.dma_start(wo_slot[:, :, :], t_in["a_wo"][bass.ds(hg * (2 * P), 2 * P), :]
                                 .rearrange("(c p) n -> p c n", p=P)).then_inc(ld_wo, 16)

            @block.gpsimd
            def _(pool):
                with pool.Fori(0, NIT // 2) as pair:
                    for side in range(2):
                        step = pair * 2 + side
                        uses = pool.snap(step * (NT - 2))
                        pool.wait_ge(heads_out, step * 2 + 2)
                        pool.tensor_copy(v_now[:, side], values[:, bass.ds((step // NHG) * NT, NT),
                                                                bass.ds((step % NHG) * HG, HG), :]).then_inc(v_copied, 1)
                        pool.wait_ge(v_copied, step + 1)
                        for j in range(1, NT - 1):
                            pool.wait_ge(prefix_used, uses + j)
                            before = v_now[:, side, 0]
                            if j > 1:
                                before = v_prefix[:, (j - 1) % 2]
                                pool.wait_ge(prefixed, uses + j - 1)
                            pool.tensor_tensor(v_prefix[:, j % 2], before, v_now[:, side, j], ALU.add)\
                                .then_inc(prefixed, 1)

            @block.tensor
            def _(pe):
                pe.sem_inc(heads_out, 4)
                pe.sem_inc(weighed, NA)
                pe.sem_inc(prefix_used, 2)
                pe.sem_inc(y_turned, 2)
                with pe.Fori(0, NIT // 2) as pair:
                    for side in range(2):
                        step = pe.snap(pair * 2 + side)
                        units, tiles, uses = (pe.snap(step * c) for c in (NU, NT, NT - 2))
                        pe.wait_ge(stacked, (step + 1) * (16 * 2 * len(PAIRS)))
                        pe.wait_ge(v_copied, step + 1)

                        def scores(k):
                            j, i = UNITS[k]
                            pe.wait_ge(squared, units + k + 1)
                            for h in range(HG):
                                last = pe.matmul(score_bank[k % NS][:, h * P:(h + 1) * P],
                                                 k_stack[0:KROWS, side, h, i * P:(i + 1) * P],
                                                 q_stack[0:KROWS, side, h, j * P:(j + 1) * P],
                                                 start=True, stop=True, skip_group_check=True)
                            last.then_inc(scored, 1)

                        def turn(j):
                            pe.wait_ge(y_out, tiles + j + 1 + 2)
                            pe.wait_ge(y_copied, tiles + j + 1)
                            for c in range(2):
                                last = pe.transpose(turn_bank[:, (j % 2) * 256 + c * P:(j % 2) * 256 + (c + 1) * P],
                                                    y_tok[:, j % 2, c * P:(c + 1) * P], ident)
                            last.then_inc(y_turned, 1)

                        scores(0)
                        scores(1)
                        for k, (j, i) in enumerate(UNITS):
                            if k + 2 < NU:
                                scores(k + 2)
                            if i == 0:
                                pe.wait_ge(y_out, tiles + j + 1)
                                if j == 1:
                                    pe.matmul(y_bank[1][:, 0:HG * NV], ones, v_now[:, side, 0],
                                              start=True, stop=False, skip_group_check=True)
                                elif j:
                                    pe.wait_ge(prefixed, uses + j - 1)
                                    pe.matmul(y_bank[j % 2][:, 0:HG * NV], ones, v_prefix[:, (j - 1) % 2],
                                              start=True, stop=False, skip_group_check=True).then_inc(prefix_used, 1)
                            if i == j:
                                pe.wait_ge(diagonal, tiles + j + 1)
                            else:
                                pe.wait_ge(squared, units + k + 1 + NS)
                            a = sq_diag[:, j % 2] if i == j else sq[:, k % NA]
                            for h in range(HG):
                                last = pe.matmul(y_bank[j % 2][:, h * NV:(h + 1) * NV], a[:, h, :],
                                                 v_now[:, side, i, h, :],
                                                 start=(j == 0 and h == 0), stop=(i == j), skip_group_check=True)
                            last.then_inc(weighed, 1)
                            if j >= 1 and i == 1:
                                turn(j - 1)
                        turn(NT - 1)
                        pe.wait_ge(ld_wo, (step + 1) * 16)
                        pe.wait_ge(y_copied, tiles + NT + 2)
                        for half in range(2):
                            pe.wait_ge(a_x, step * 2 + half + 1)
                            for c in range(2):
                                last = pe.matmul(out_bank[half][:, :], wo_slot[:, c, :],
                                                 y_feat[:, c, half * CH:(half + 1) * CH], start=(c == 0), stop=(c == 1))
                            last.then_inc(heads_out, 1)

            @block.scalar
            def _(act):
                act.sem_inc(squared, NS)
                act.sem_inc(y_copied, 2)
                with act.Fori(0, NIT) as it:
                    units, tiles, outs = act.snap(it * NU), act.snap(it * NT), act.snap(it * 2)
                    def copy_turned(j):
                        act.wait_ge(y_turned, tiles + j + 1 + 2)
                        act.wait_ge(heads_out, outs + 4)
                        act.copy(y_feat[:, :, j * P:(j + 1) * P],
                                 turn_bank[:, (j % 2) * 256:(j % 2) * 256 + 256]
                                 .rearrange("p (c n) -> p c n", c=2)).then_inc(y_copied, 1)
                    for k, (j, i) in enumerate(UNITS):
                        act.wait_ge(scored, units + k + 1)
                        act.wait_ge(weighed, units + k + 1)
                        act.activation(sq[:, k % NA], score_bank[k % NS][:, :].rearrange("p (h n) -> p h n", h=HG),
                                       ACT.Square, bias=eps_col[:, 2:3], scale=0.25).then_inc(squared, 1)
                        if j >= 1 and i == min(2, j) and not (j == 1):
                            copy_turned(j - 1)
                        if j == 2 and i == 0:
                            copy_turned(0)
                    copy_turned(NT - 1)

            @block.vector
            def _(dve):
                dve.sem_inc(y_out, 2)
                dve.sem_inc(a_x, 2)
                with dve.Fori(0, NIT) as it:
                    units, tiles, outs = dve.snap(it * NU), dve.snap(it * NT), dve.snap(it * 2)
                    b = it // NHG
                    for j in range(NT):
                        k = UNITS.index((j, j))
                        dve.wait_ge(squared, units + k + 1 + NS)
                        dve.scalar_tensor_tensor(sq_diag[:, j % 2], sq[:, k % NA], 1.0,
                                                 causal.unsqueeze(1).to_broadcast([P, HG, P]),
                                                 ALU.add, ALU.mult).then_inc(diagonal, 1)
                        dve.wait_ge(weighed, units + k + 1 + NA)
                        yb = y_bank[j % 2][:, 0:HG * NV].rearrange("p (h e) -> p h e", h=HG)
                        dve.tensor_scalar(z_sum[:, j % 2], yb[:, :, AV], 2e-12, None, ALU.add).then_inc(z_in, 1)
                        dve.wait_ge(z_in, tiles + j + 1)
                        dve.reciprocal(z_rec[:, j % 2], z_sum[:, j % 2]).then_inc(z_inv, 1)
                        dve.wait_ge(z_inv, tiles + j + 1)
                        dve.wait_ge(y_turned, tiles + j + 1)
                        dve.tensor_tensor(y_tok[:, j % 2].rearrange("p (h e) -> p h e", h=HG), yb[:, :, 0:AV],
                                          z_rec[:, j % 2].unsqueeze(2).to_broadcast([P, HG, AV]), ALU.mult)\
                            .then_inc(y_out, 1)
                    for half in range(2):
                        dve.wait_ge(heads_out, outs + half + 1 + 4)
                        dst = xT[:, bass.ds(b, 1), half * CH:(half + 1) * CH]
                        dve.tensor_tensor(dst, dst, out_bank[half][:, :], ALU.add).then_inc(a_x, 1)


def ffn_sems(sem):
    names = """ld_tab ld_qkv ld_mlp set_up tab_done h_in qkv_done qk_squared v_out v_mixed_0 v_mixed_1 ss_in ss_clipped ss_log
        qk_inv qk_rotated qk_summed qk_normed qk_turned q_out k_out sim_done max_done exp_done sum_inv p_normed
        p_turned p_out_lo p_out_hi pv_done o_out_0 o_out_1 wo_done mid_done h2_in centred squared var_done
        var_log var_inv normed affine hid_mm gelu_done hid_done w2_done""".split()
    return {n: sem("f_" + n) for n in names}


def ffn(nc, t_in, sb, ps, S, call, y0, y_done, ident, centre, mean, identB, eps_col, cols, at_least):
    G0 = call * NG
    with ExitStack() as stack:
        def s(name, shape, dt=F32):
            return sb(f"{name}_{call}", shape, dt, stack)
        y1 = s("y1", [P, B, 1 + N])
        wqkv = s("wqkv", [P, DEPTH, 3 * INNER])
        wo = s("wo", [P, INNER // P, D])
        w1 = s("w1", [P, 2 * HID])
        w2 = s("w2", [P, len(HC), D])
        mask = s("mask", [P, NT, P], BF16)
        rot = s("rot", [P, DEPTH, 4, NT, DH])
        gains = s("gains", [P, 2, DEPTH, DH])
        h = s("h", [P, 2, B, P])
        qk_sq = s("qk_sq", [P, 2 * INNER])
        ss = s("ss", [P, B, 3, 2 * HEADS])
        qk_scale = s("qk_scale", [P, B, 2 * HEADS])
        rot_a = s("rot_a", [P, B, 2 * INNER])
        rot_b = s("rot_b", [P, B, 2 * INNER])
        v_nat = s("v_nat", [P, 2, B, INNER])
        v_mix = s("v_mix", [P, 2, B, INNER])
        qT = s("qT", [P, 2, B, HEADS // 2, P])
        kT = s("kT", [P, 2, B, HEADS // 2, P])
        neg_max = s("neg_max", [P, B, 2, HEADS // 2])
        prob = s("prob", [P, B, HEADS, P])
        p_sum = s("p_sum", [P, B, HEADS])
        p_inv = s("p_inv", [P, B, HEADS])
        probT = s("probT", [P, B, HEADS, P])
        oT = s("oT", [P, 2, HEADS // 2, B, P])
        h2 = s("h2", [P, B, P])
        c_sq = s("c_sq", [P, B * P])
        v_log = s("v_log", [P, B * P])
        v_inv = s("v_inv", [P, B * P])
        normed = s("normed", [P, B * P])
        hn = s("hn", [P, B * P])
        gel = s("gel", [P, 2, B * P])
        hid = s("hid", [P, len(HC), B * P])
        BP = B * P
        qk_bank = ps[0:2]
        v_bank = ps[2]
        sim_bank = ps[3:5]
        turn_bank = ps[5:7]
        m_bank = ps[7]
        hid_bank = [ps[2], ps[7], ps[2]]

        def b1_col(l, k, c, m):
            return cols[0:m, bass.ds(l * (2 * len(HC)) + (COL_B1 + k * len(HC) + c), 1)]

        def slots(eng, stage):
            stage(0, 0, True, False, False)
            stage(1, 1, True, True, False)
            stage(2, 0, True, True, True)
            stage(3, 1, True, True, True)
            with eng.Fori(2, NG // 2) as pair:
                stage(eng.snap(pair * 2), 0, True, True, True)
                stage(eng.snap(pair * 2 + 1), 1, True, True, True)
            stage(NG, 0, False, True, True)
            stage(NG + 1, 1, False, False, True)

        def cap(value, most):
            return min(value, most) if isinstance(value, int) else value

        def w(eng, name, value):
            per = {"": 0}
            total = G0 * PER[name] + value
            at_least(eng, S[name], total)

        PER = dict(h_in=2, qkv_done=2, qk_squared=4, v_out=2, v_mixed_0=16, v_mixed_1=16, ss_in=2, ss_clipped=2, ss_log=2,
                   qk_inv=2, qk_rotated=2, qk_summed=2, qk_normed=2, qk_turned=2, q_out=2, k_out=2, sim_done=4,
                   max_done=4, exp_done=4, sum_inv=2, p_normed=2, p_turned=2, p_out_lo=2, p_out_hi=2, pv_done=2,
                   o_out_0=1, o_out_1=1, wo_done=1, mid_done=1, h2_in=2, centred=1, squared=1, var_done=1,
                   var_log=1, var_inv=1, normed=1, affine=1, hid_mm=3, gelu_done=3, hid_done=3, w2_done=1)
        def mixed(eng, g, par):
            if isinstance(g, int) and g < 0:
                return
            w(eng, f"v_mixed_{par}", g * 16 + (32 if par == 0 else 16))

        MLP_LOADS, TAB_LOADS = 4, 3 + 2 * DEPTH

        with nc.Block() as block:
            @block.sync
            def _(sp):
                def mlp(l):
                    sp.dma_start(wo[:, :, :], t_in["wo"][l].rearrange("(c p) n -> p c n", p=P))\
                        .then_inc(S["ld_mlp"], 16)
                    sp.dma_start(w1[:, :], t_in["w1"][l]).then_inc(S["ld_mlp"], 16)
                    full = HID // P
                    sp.dma_start(w2[:, 0:full, :], t_in["w2"][l, 0:full * P, :]
                                 .rearrange("(c p) n -> p c n", p=P)).then_inc(S["ld_mlp"], 16)
                    sp.dma_start(w2[0:HC[-1][1], full, :], t_in["w2"][l, full * P:HID, :]).then_inc(S["ld_mlp"], 16)

                sp.dma_start(wqkv[:, :, :], t_in["wqkv"].rearrange("l p n -> p l n")).then_inc(S["ld_qkv"], 16)
                sp.dma_start(rot[:, 0], t_in["rot"]).then_inc(S["ld_tab"], 16)
                sp.dma_start(rot[:, 1], t_in["rot"]).then_inc(S["ld_tab"], 16)
                sp.dma_start(mask[:, :, :], t_in["mask"]).then_inc(S["ld_tab"], 16)
                for l in range(DEPTH):
                    for k, name in enumerate(("q_scale", "k_scale")):
                        sp.dma_start(gains[:, k, l, :], t_in[name][l:l + 1, :].to_broadcast([P, DH]))\
                            .then_inc(S["ld_tab"], 16)
                mlp(0)

                def stage(g, par, on1, on2, on3):
                    if on1:
                        w(sp, "v_out", 2 * g + 2)
                        w(sp, "pv_done", 2 * g - 2)
                        for rows, src in ((slice(0, WIN), par), (slice(WIN, P), 1 - par)):
                            sp.dma_start(v_mix[rows, par], v_nat[rows, src]).then_inc(S[f"v_mixed_{par}"], 16)

                half_way = NT + 2
                for g in range(4):
                    stage(g, g % 2, True, False, False)
                with sp.Fori(2, half_way // 2) as pair:
                    stage(sp.snap(pair * 2), 0, True, False, False)
                    stage(sp.snap(pair * 2 + 1), 1, True, False, False)
                w(sp, "w2_done", NT)
                sp.wait_ge(S["ld_mlp"], 16 * MLP_LOADS * (2 * call + 1))
                mlp(1)
                with sp.Fori(half_way // 2, NG // 2) as pair:
                    stage(sp.snap(pair * 2), 0, True, False, False)
                    stage(sp.snap(pair * 2 + 1), 1, True, False, False)
            @block.tensor
            def _(pe):
                def stage(g, par, on1, on2, on3):
                    if on2:
                        g2, par2 = g - 1, 1 - par
                    if on3:
                        g3, par3 = g - 2, par
                    if on1:
                        layer1 = g // NT if isinstance(g, int) else pe.snap(g // NT)

                    def project(b):
                        if b == 0:
                            w(pe, "h_in", 2 * g + 2)
                            w(pe, "hid_done", cap(3 * g - 6, 3 * NG))
                        w(pe, "qk_rotated", 2 * g + b)
                        w(pe, "v_out", 2 * g + b)
                        for k, bank in enumerate((*qk_bank, v_bank)):
                            last = pe.matmul(bank[:, :], h[:, par, b, :],
                                             wqkv[:, bass.ds(layer1, 1), k * INNER:(k + 1) * INNER],
                                             start=True, stop=True)
                        last.then_inc(S["qkv_done"], 1)

                    def similar(b):
                        t = g2 % NT
                        w(pe, "q_out", 2 * g2 + b + 1)
                        w(pe, "k_out", 2 * g2 + b + 1)
                        off = t * P
                        w(pe, "exp_done", 4 * g2 + 2 * b)
                        for half in range(2):
                            pe.matmul(sim_bank[half][:, :].rearrange("p (h n) -> p h n", h=4), identB[:, :],
                                      mask.rearrange("p t n -> p (t n)")[:, bass.ds(off, P)].unsqueeze(1)
                                      .to_broadcast([P, 4, P]),
                                      start=True, stop=False, skip_group_check=True)
                        for hh in range(4):
                            o = hh * P
                            q, k_, kp = qT[:, par2, b, hh], kT[:, par2, b, hh], kT[:, 1 - par2, b, hh]
                            for half in range(2):
                                rows, bank = slice(half * DH, half * DH + DH), sim_bank[half]
                                pe.matmul(bank[0:WIN, o:o + WIN], q[rows, 0:WIN], k_[rows, 0:WIN],
                                          start=False, stop=False, skip_group_check=True)
                                pe.matmul(bank[WIN:P, o:o + P], q[rows, WIN:P], k_[rows, 0:P],
                                          start=False, stop=True, skip_group_check=True)
                                last = pe.matmul(bank[0:WIN, o + WIN:o + P], q[rows, 0:WIN], kp[rows, WIN:P],
                                                 start=False, stop=True, skip_group_check=True)
                                if hh == 3:
                                    last.then_inc(S["sim_done"], 1)

                    def turn_qk(b):
                        w(pe, "qk_normed", 2 * g + b + 1)
                        w(pe, "p_out_lo", 2 * g - 2 + b)
                        w(pe, "p_out_hi", 2 * g - 2 + b)
                        w(pe, "q_out", 2 * g + b)
                        w(pe, "k_out", 2 * g + b)
                        for k in range(2):
                            for c in range(INNER // P):
                                last = pe.transpose(turn_bank[k][:, c * P:(c + 1) * P],
                                                    rot_a[:, b, k * INNER + c * P:k * INNER + (c + 1) * P], ident)
                        last.then_inc(S["qk_turned"], 1)

                    def turn_p(b):
                        w(pe, "p_normed", 2 * g2 + b + 1)
                        w(pe, "q_out", cap(2 * g2 + 3 + b, 2 * NG))
                        w(pe, "k_out", cap(2 * g2 + 3 + b, 2 * NG))
                        w(pe, "p_out_lo", 2 * g2 + b)
                        w(pe, "p_out_hi", 2 * g2 + b)
                        for hd in range(HEADS):
                            last = pe.transpose(turn_bank[hd // 4][:, (hd % 4) * P:(hd % 4 + 1) * P],
                                                prob[:, b, hd, :], ident)
                        last.then_inc(S["p_turned"], 1)

                    def attend(b):
                        w(pe, "p_out_lo", 2 * g2 + b + 1)
                        w(pe, "p_out_hi", 2 * g2 + b + 1)
                        mixed(pe, g2, par2)
                        if b == 0:
                            at_least(pe, y_done, G0 + g2)
                        w(pe, "o_out_1", g2)
                        if b == 1:
                            w(pe, "o_out_0", g2 + 1)
                        for pr in range(HEADS // 2):
                            for half, vals in enumerate((v_mix, v_nat)):
                                for sub in range(2):
                                    hd = 2 * pr + sub
                                    last = pe.matmul(
                                        m_bank[sub * DH:(sub + 1) * DH, pr * P + half * WIN:pr * P + (half + 1) * WIN],
                                        vals[:, par2, b, hd * DH:(hd + 1) * DH],
                                        probT[:, b, hd, half * WIN:(half + 1) * WIN],
                                        start=True, stop=True, skip_group_check=True)
                        last.then_inc(S["pv_done"], 1)

                    def out_proj():
                        pe.wait_ge(S["ld_mlp"], (g3 // NT + (2 * call + 1)) * (16 * MLP_LOADS))
                        w(pe, "o_out_0", g3 + 1)
                        w(pe, "o_out_1", g3 + 1)
                        for c in range(INNER // P):
                            last = pe.matmul(m_bank[:, 0:BP], wo[:, c, :], oT[:, par3, c].rearrange("p b n -> p (b n)"),
                                             start=(c == 0), stop=(c == INNER // P - 1), skip_group_check=True)
                        last.then_inc(S["wo_done"], 1)

                    def take_mean_off():
                        w(pe, "h2_in", 2 * g3 + 2)
                        pe.matmul(m_bank[:, BP:2 * BP], centre, h2[:, :, :].rearrange("p b n -> p (b n)"),
                                  start=True, stop=True, skip_group_check=True).then_inc(S["centred"], 1)

                    def variance():
                        w(pe, "squared", g3 + 1)
                        pe.matmul(m_bank[:, 0:BP], mean, c_sq[:, :], start=True, stop=True, skip_group_check=True)\
                            .then_inc(S["var_done"], 1)

                    def hidden(c):
                        w(pe, "affine", g3 + 1)
                        if c == 0:
                            w(pe, "v_out", cap(2 * g3 + 6, 2 * NG))
                        if c == 2:
                            w(pe, "hid_done", 3 * g3 + 1)
                        c0, m = HC[c]
                        for k in range(2):
                            last = pe.matmul(hid_bank[c][0:m, k * BP:(k + 1) * BP],
                                             w1[:, k * HID + c0:k * HID + c0 + m], hn[:, :],
                                             start=True, stop=True, skip_group_check=True)
                        last.then_inc(S["hid_mm"], 1)

                    def down():
                        w(pe, "hid_done", 3 * g3 + 3)
                        for c, (c0, m) in enumerate(HC):
                            last = pe.matmul(m_bank[:, 0:BP], w2[0:m, c, :], hid[0:m, c, :],
                                             start=(c == 0), stop=(c == len(HC) - 1), skip_group_check=True)
                        last.then_inc(S["w2_done"], 1)

                    if on1:
                        project(0)
                    if on2:
                        similar(0)
                    if on3:
                        out_proj()
                    if on1:
                        project(1)
                    if on3:
                        take_mean_off()
                    if on2:
                        similar(1)
                    if on3:
                        variance()
                    if on1:
                        turn_qk(0)
                    if on3:
                        hidden(0)
                        hidden(1)
                    if on2:
                        turn_p(0)
                    if on3:
                        hidden(2)
                    if on1:
                        turn_qk(1)
                    if on3:
                        down()
                    if on2:
                        attend(0)
                        turn_p(1)
                        attend(1)

                pe.wait_ge(S["ld_tab"], 16 * TAB_LOADS * (call + 1))
                pe.wait_ge(S["ld_qkv"], 16 * (call + 1))
                pe.wait_ge(S["set_up"], 3 * (call + 1))
                slots(pe, stage)

            @block.scalar
            def _(act):
                def stage(g, par, on1, on2, on3):
                    if on2:
                        g2, par2 = g - 1, 1 - par
                    if on3:
                        g3, par3 = g - 2, par
                        l3 = g3 // NT

                    def square_qk(b):
                        w(act, "qkv_done", 2 * g + b + 1)
                        w(act, "ss_in", 2 * g + b)
                        for k in range(2):
                            act.activation(qk_sq[:, k * INNER:(k + 1) * INNER], qk_bank[k][:, :], ACT.Square)\
                                .then_inc(S["qk_squared"], 1)
                        w(act, "pv_done", 2 * g - 2)
                        if b == 0:
                            mixed(act, g - 1, 1 - par)
                        act.copy(v_nat[:, par, b, :], v_bank[:, :]).then_inc(S["v_out"], 1)

                    def norms(b):
                        w(act, "ss_clipped", 2 * g + b + 1)
                        act.activation(ss[:, b, 2, :], ss[:, b, 1, :], ACT.Ln, scale=SS_SHIFT).then_inc(S["ss_log"], 1)
                        w(act, "ss_log", 2 * g + b + 1)
                        w(act, "qk_normed", 2 * g + b - 1)
                        act.activation(qk_scale[:, b, :], ss[:, b, 2, :], ACT.Exp, scale=-0.5,
                                       bias=eps_col[:, 1:2]).then_inc(S["qk_inv"], 1)

                    def softmax(b):
                        w(act, "p_turned", 2 * g2 + b - 1)
                        w(act, "sum_inv", 2 * g2 + b - 1)
                        for half in range(2):
                            w(act, "max_done", 4 * g2 + 2 * b + half + 1)
                            for hh in range(4):
                                hd = 2 * hh + half
                                last = act.activation(prob[:, b, hd, :], sim_bank[half][:, hh * P:(hh + 1) * P],
                                                      ACT.Exp, bias=neg_max[:, b, half, hh:hh + 1],
                                                      accum_out=p_sum[:, b, hd:hd + 1])
                            last.then_inc(S["exp_done"], 1)

                    def square_centred():
                        w(act, "centred", g3 + 1)
                        w(act, "var_done", g3)
                        act.activation(c_sq[:, :], m_bank[:, BP:2 * BP], ACT.Square).then_inc(S["squared"], 1)

                    def inverse_std():
                        w(act, "var_done", g3 + 1)
                        act.activation(v_log[:, :], m_bank[:, 0:BP], ACT.Ln, bias=eps_col[:, 0:1])\
                            .then_inc(S["var_log"], 1)
                        w(act, "var_log", g3 + 1)
                        w(act, "normed", g3)
                        act.activation(v_inv[:, :], v_log[:, :], ACT.Exp, scale=-0.5).then_inc(S["var_inv"], 1)

                    def copy_q(b):
                        w(act, "qk_turned", 2 * g + b + 1)
                        w(act, "sim_done", 4 * g - 6 + 2 * b)
                        act.copy(qT[:, par, b, :, :], turn_bank[0][:, :].rearrange("p (c n) -> p c n", n=P))\
                            .then_inc(S["q_out"], 1)

                    def copy_p(b):
                        w(act, "p_turned", 2 * g2 + b + 1)
                        w(act, "pv_done", 2 * g2 + b - 1)
                        act.copy(probT[:, b, 0:4, :], turn_bank[0][:, :].rearrange("p (c n) -> p c n", n=P))\
                            .then_inc(S["p_out_lo"], 1)

                    def gelu(c):
                        w(act, "hid_mm", 3 * g3 + c + 1)
                        w(act, "hid_done", 3 * g3 + c - 1)
                        m = HC[c][1]
                        act.activation(gel[0:m, c % 2, :], hid_bank[c][0:m, BP:2 * BP], ACT.Gelu,
                                       bias=b1_col(l3, 1, c, m))\
                            .then_inc(S["gelu_done"], 1)

                    def copy_o():
                        w(act, "pv_done", 2 * g2 + 1)
                        w(act, "wo_done", g2 - 1)
                        act.copy(oT[:, par2, :, 0, :], m_bank[:, :].rearrange("p (c n) -> p c n", n=P))\
                            .then_inc(S["o_out_0"], 1)

                    act.preload_act_table_set(EXP_SET)
                    if on1:
                        square_qk(0)
                        norms(0)
                    if on2:
                        softmax(0)
                    if on1:
                        square_qk(1)
                        norms(1)
                    if on3:
                        square_centred()
                    if on2:
                        softmax(1)
                    if on3:
                        inverse_std()
                    if on1:
                        copy_q(0)
                    if on3:
                        gelu(0)
                        gelu(1)
                    if on2:
                        copy_p(0)
                    if on3:
                        gelu(2)
                    if on1:
                        copy_q(1)
                    if on2:
                        copy_o()
                        copy_p(1)

                act.wait_ge(S["ld_tab"], 16 * TAB_LOADS * (call + 1))
                slots(act, stage)

            @block.vector
            def _(dve):
                def tok(buf, rows, b, t, ahead):
                    return buf[rows, b, bass.ds(t * P + ahead, P)]

                def shifted(eng, out, buf, t, s_):
                    eng.tensor_copy(out[0:D // 2], buf[0:D // 2, :, bass.ds(t * P + 1, P)]).then_inc(s_, 1)
                    eng.tensor_copy(out[D // 2:D], buf[D // 2:D, :, bass.ds(t * P, P)]).then_inc(s_, 1)

                def stage(g, par, on1, on2, on3):
                    if on2:
                        g2, par2 = g - 1, 1 - par
                    if on3:
                        g3, par3 = g - 2, par
                        t3, l3 = g3 % NT, g3 // NT
                        if not isinstance(g3, int):
                            t3, l3 = dve.snap(t3), dve.snap(l3)
                    if on1:
                        t1, l1 = g % NT, g // NT
                        if not isinstance(g, int):
                            t1, l1 = dve.snap(t1), dve.snap(l1)

                    def take_in():
                        at_least(dve, y_done, G0 + g - 2)
                        w(dve, "qkv_done", 2 * g - 2)
                        shifted(dve, h[:, par], y0, t1, S["h_in"])

                    def rotate(b):
                        w(dve, "qk_summed", 2 * g + b - 1)
                        w(dve, "qk_turned", 2 * g + b - 1)
                        for k in range(2):
                            w(dve, "qk_squared", 4 * g + 2 * b + k + 1)
                            x = qk_bank[k][:, :].rearrange("p (h d) -> p h d", d=DH)
                            ra = rot_a[:, b, k * INNER:(k + 1) * INNER].rearrange("p (h d) -> p h d", d=DH)
                            rb = rot_b[:, b, k * INNER:(k + 1) * INNER].rearrange("p (h d) -> p h d", d=DH)
                            HF = DH // 2

                            def tab(i, lo, hi):
                                return rot[:, bass.ds(l1, 1), i, bass.ds(t1, 1), lo:hi]\
                                    .rearrange("p a b d -> p (a b) d").to_broadcast([P, HEADS, hi - lo])
                            dve.tensor_tensor(ra, x, tab(k, 0, DH), ALU.mult)
                            dve.tensor_tensor(rb[:, :, 0:HF], x[:, :, HF:DH], tab(2 + k, 0, HF), ALU.mult)
                            last = dve.tensor_tensor(rb[:, :, HF:DH], x[:, :, 0:HF], tab(2 + k, HF, DH), ALU.mult)
                        last.then_inc(S["qk_rotated"], 1)

                    def norms(b):
                        w(dve, "qk_squared", 4 * g + 2 * b + 2)
                        w(dve, "ss_clipped", 2 * g + b - 1)
                        dve.tensor_reduce(ss[:, b, 0, :], qk_sq[:, :].rearrange("p (h d) -> p h d", d=DH),
                                          AX.X, ALU.add).then_inc(S["ss_in"], 1)
                        w(dve, "ss_in", 2 * g + b + 1)
                        w(dve, "ss_log", 2 * g + b - 1)
                        dve.tensor_scalar(ss[:, b, 1, :], ss[:, b, 0, :], 1e-24, None, ALU.max)\
                            .then_inc(S["ss_clipped"], 1)

                    def maxima(b):
                        w(dve, "exp_done", 4 * g2 + 2 * b - 2)
                        for half in range(2):
                            w(dve, "sim_done", 4 * g2 + 2 * b + half + 1)
                            dve.tensor_reduce(neg_max[:, b, half, :],
                                              sim_bank[half][:, :].rearrange("p (h n) -> p h n", n=P),
                                              AX.X, ALU.max, negate=True).then_inc(S["max_done"], 1)

                    def invert_sums(b):
                        w(dve, "exp_done", 4 * g2 + 2 * b + 2)
                        w(dve, "p_normed", 2 * g2 + b - 1)
                        dve.reciprocal(p_inv[:, b, :], p_sum[:, b, :]).then_inc(S["sum_inv"], 1)

                    def copy_k(b):
                        w(dve, "qk_turned", 2 * g + b + 1)
                        w(dve, "sim_done", 4 * g - 2 + 2 * b)
                        dve.tensor_copy(kT[:, par, b, :, :], turn_bank[1][:, :].rearrange("p (c n) -> p c n", n=P))\
                            .then_inc(S["k_out"], 1)

                    def copy_p(b):
                        w(dve, "p_turned", 2 * g2 + b + 1)
                        w(dve, "pv_done", 2 * g2 + b - 1)
                        dve.tensor_copy(probT[:, b, 4:8, :], turn_bank[1][:, :].rearrange("p (c n) -> p c n", n=P))\
                            .then_inc(S["p_out_hi"], 1)

                    def copy_o():
                        w(dve, "pv_done", 2 * g2 + 2)
                        w(dve, "wo_done", g2 - 1)
                        dve.tensor_copy(oT[:, par2, :, 1, :], m_bank[:, :].rearrange("p (c n) -> p c n", n=P))\
                            .then_inc(S["o_out_1"], 1)

                    def add_attention():
                        w(dve, "wo_done", g3 + 1)
                        w(dve, "h2_in", 2 * g3)
                        at = bass.ds(t3 * P + 1, P)
                        dve.tensor_tensor(y1[:, :, at], y0[:, :, at],
                                          m_bank[:, 0:BP].rearrange("p (b n) -> p b n", b=B), ALU.add)\
                            .then_inc(S["mid_done"], 1)
                        w(dve, "mid_done", g3 + 1)
                        w(dve, "centred", g3)
                        shifted(dve, h2, y1, t3, S["h2_in"])

                    def normalise():
                        w(dve, "var_inv", g3 + 1)
                        w(dve, "affine", g3)
                        dve.tensor_tensor(normed[:, :], m_bank[:, BP:2 * BP], v_inv[:, :], ALU.mult)\
                            .then_inc(S["normed"], 1)
                        w(dve, "normed", g3 + 1)
                        w(dve, "hid_mm", 3 * g3)
                        dve.tensor_scalar(hn[:, :], normed[:, :], cols[:, bass.ds(l3 + COL_LN_G, 1)],
                                          cols[:, bass.ds(l3 + COL_LN_B, 1)], ALU.mult, ALU.add).then_inc(S["affine"], 1)

                    def gate(c):
                        w(dve, "gelu_done", 3 * g3 + c + 1)
                        if c == 0:
                            w(dve, "w2_done", g3)
                        m = HC[c][1]
                        dve.scalar_tensor_tensor(hid[0:m, c, :], hid_bank[c][0:m, 0:BP],
                                                 b1_col(l3, 0, c, m),
                                                 gel[0:m, c % 2, :], ALU.add, ALU.mult).then_inc(S["hid_done"], 1)

                    def give_out():
                        w(dve, "w2_done", g3 + 1)
                        if on1:
                            w(dve, "h_in", 2 * g + 2)
                        at = bass.ds(t3 * P + 1, P)
                        dve.scalar_tensor_tensor(y0[:, :, at], m_bank[:, 0:BP].rearrange("p (b n) -> p b n", b=B),
                                                 cols[:, bass.ds(l3 + COL_B2, 1)], y1[:, :, at], ALU.add, ALU.add)\
                            .then_inc(y_done, 1)

                    if on1:
                        take_in()
                        rotate(0)
                        norms(0)
                    if on2:
                        maxima(0)
                    if on3:
                        add_attention()
                    if on1:
                        rotate(1)
                        norms(1)
                    if on2:
                        invert_sums(0)
                        maxima(1)
                    if on3:
                        normalise()
                    if on1:
                        copy_k(0)
                    if on3:
                        gate(0)
                        gate(1)
                    if on2:
                        invert_sums(1)
                        copy_p(0)
                    if on3:
                        gate(2)
                    if on1:
                        copy_k(1)
                    if on3:
                        give_out()
                    if on2:
                        copy_p(1)
                        copy_o()

                dve.wait_ge(S["ld_tab"], 16 * TAB_LOADS * (call + 1))
                tabs = 0
                for l in range(DEPTH):
                    for k in range(2):
                        HF = DH // 2
                        for i, lo, hi, g0 in ((k, 0, DH, 0), (2 + k, 0, HF, HF), (2 + k, HF, DH, 0)):
                            t_ = rot[:, l, i, :, lo:hi]
                            dve.tensor_tensor(t_, t_, gains[:, k, l, g0:g0 + hi - lo].unsqueeze(1)
                                              .to_broadcast([P, NT, hi - lo]), ALU.mult).then_inc(S["tab_done"], 1)
                            tabs += 1
                dve.wait_ge(S["tab_done"], tabs * (call + 1))
                dve.wait_ge(S["set_up"], 3 * (call + 1))
                slots(dve, stage)

            @block.gpsimd
            def _(pool):
                def stage(g, par, on1, on2, on3):
                    if on2:
                        g2 = g - 1

                    def sum_and_scale(b):
                        w(pool, "qk_rotated", 2 * g + b + 1)
                        pool.tensor_tensor(rot_b[:, b, :], rot_a[:, b, :], rot_b[:, b, :], ALU.add)\
                            .then_inc(S["qk_summed"], 1)
                        w(pool, "qk_summed", 2 * g + b + 1)
                        w(pool, "qk_inv", 2 * g + b + 1)
                        pool.tensor_tensor(rot_a[:, b, :].rearrange("p (h d) -> p h d", d=DH),
                                           rot_b[:, b, :].rearrange("p (h d) -> p h d", d=DH),
                                           qk_scale[:, b, :].unsqueeze(2).to_broadcast([P, 2 * HEADS, DH]), ALU.mult)\
                            .then_inc(S["qk_normed"], 1)

                    def scale_probs(b):
                        w(pool, "sum_inv", 2 * g2 + b + 1)
                        pool.tensor_tensor(prob[:, b], prob[:, b],
                                           p_inv[:, b, :].unsqueeze(2).to_broadcast([P, HEADS, P]), ALU.mult)\
                            .then_inc(S["p_normed"], 1)

                    if on1:
                        sum_and_scale(0)
                    if on2:
                        scale_probs(0)
                    if on1:
                        sum_and_scale(1)
                    if on2:
                        scale_probs(1)

                pool.memset(kT[:, 1], 0.0).then_inc(S["set_up"], 1)
                pool.memset(v_nat[:, 1], 0.0).then_inc(S["set_up"], 1)
                pool.memset(y1[:, :, 0:1], 0.0).then_inc(S["set_up"], 1)
                pool.wait_ge(S["set_up"], 3 * (call + 1))
                slots(pool, stage)


def rwkv(nc, t_in, sb, sem, ps, xT, y0, cols, r_x, normalise, y_ready):
    NSEQ = 2 * B
    HALVES = N // CH
    R, K, V = range(3)
    chunks = [(K, 0), (V, 0), *((R, s) for s in range(NSEQ)),
              *((what, s) for s in range(1, NSEQ) for what in (K, V))]
    chunks = [(what, s, h) for what, s in chunks for h in range(HALVES)]
    by_dve = [c for c in chunks if c[0] == K]
    by_act = [c for c in chunks if c[0] != K]
    names = """ld_w ld_out projected keys_in rest_in decay_exp decay_in max_scanned kept decayed shifted clipped
        weights_in den_scanned num_scanned values_in den_scaled den_out num_scaled top_in gated log_in inv_in
        mixed out_done""".split()
    S = {n: sem("r_" + n) for n in names}
    with ExitStack() as stack:
        def s(name, shape, dt=F32):
            return sb("r_" + name, shape, dt, stack)
        w_in = s("w_in", [P, 6 * D])
        w_out = s("w_out", [P, 2, D])
        decay = s("decay", [P, 2])
        rkv = s("rkv", [P, 3, NSEQ, N])
        mx = s("mx", [P, 2, 1 + N])
        diff = s("diff", [P, 2, N])
        NX = 3
        ex = s("ex", [P, NX, 4, N])
        E1, E2, E1S, E2S = range(4)
        ev = s("ev", [P, 2, 2, N])
        num = s("num", [P, 2, 1 + N])
        den = s("den", [P, 2, 1 + N])
        mixed = s("mixed", [P, NSEQ, N])

        def first_col(d):
            return cols[:, COL_R + 2 * d + 1:COL_R + 2 * d + 2]

        with nc.Block() as block:
            @block.sync
            def _(sp):
                sp.dma_start(w_in[:, :], t_in["r_w"]).then_inc(S["ld_w"], 16)
                sp.dma_start(w_out[:, :, :], t_in["r_out"].rearrange("(c p) n -> p c n", p=P))\
                    .then_inc(S["ld_out"], 16)

            @block.tensor
            def _(pe):
                normalise(pe)
                pe.wait_ge(S["ld_w"], 16)
                for i, (what, seq, h) in enumerate(chunks):
                    b, d = divmod(seq, 2)
                    if i >= 8:
                        c = chunks[i - 8]
                        if c[0] == K:
                            pe.wait_ge(S["keys_in"], by_dve.index(c) + 1)
                        else:
                            pe.wait_ge(S["rest_in"], by_act.index(c) + 1)
                    y_ready(pe, NCH - 1 if i >= 4 else HALVES * b + h)
                    at = (3 * d + what) * D
                    pe.matmul(ps[i % 8][:, :], w_in[:, at:at + D], y0[:, b, 1 + h * CH:1 + (h + 1) * CH],
                              start=True, stop=True).then_inc(S["projected"], 1)
                pe.wait_ge(S["ld_out"], 16)
                for b in range(B):
                    pe.wait_ge(S["mixed"], 2 * b + 2)
                    for h in range(HALVES):
                        c = HALVES * b + h
                        if b == 0:
                            pe.wait_ge(S["keys_in"], len(by_dve))
                            pe.wait_ge(S["rest_in"], len(by_act))
                        for d in range(2):
                            last = pe.matmul(ps[c][:, :], w_out[:, d, :], mixed[:, 2 * b + d, h * CH:(h + 1) * CH],
                                             start=(d == 0), stop=(d == 1))
                        last.then_inc(S["out_done"], 1)

            @block.scalar
            def _(act):
                normalise(act)

                def take(want):
                    for i, c in enumerate(chunks):
                        if c not in by_act or not want(c):
                            continue
                        what, seq, h = c
                        act.wait_ge(S["projected"], i + 1)
                        hh = h if seq % 2 == 0 else HALVES - 1 - h
                        dst = rkv[:, what, seq, hh * CH:(hh + 1) * CH]
                        if seq % 2:
                            dst = rkv[:, what, seq, hh * CH:(hh + 1) * CH][:, ::-1]
                        act.activation(dst, ps[i % 8][:, :], ACT.Sigmoid if what == R else ACT.Copy)\
                            .then_inc(S["rest_in"], 1)

                def weights(q):
                    for e, name, n in ((E1, "clipped", 2 * q + 1), (E2, "clipped", 2 * q + 2),
                                       (E1S, "decayed", q + 1), (E2S, "kept", q + 1)):
                        act.wait_ge(S[name], n)
                        act.activation(ex[:, q % NX, e, :], ex[:, q % NX, e, :], ACT.Exp)\
                            .then_inc(S["weights_in"], 1)

                def invert(q):
                    bot = ex[:, q % NX, E1S, :]
                    act.wait_ge(S["den_out"], q + 1)
                    act.activation(bot, bot, ACT.Ln).then_inc(S["log_in"], 1)
                    act.wait_ge(S["log_in"], q + 1)
                    act.activation(bot, bot, ACT.Exp, scale=-1.0).then_inc(S["inv_in"], 1)

                take(lambda c: c[0] == V and c[1] == 0)
                take(lambda c: c[0] == R)
                act.preload_act_table_set(EXP_SET)
                act.activation(decay[:, :], cols[:, COL_R:COL_R + 4:2], ACT.Exp).then_inc(S["decay_exp"], 1)
                for seq in range(NSEQ):
                    weights(seq)
                    if seq + 1 < NSEQ:
                        take(lambda c: c[0] == V and c[1] == seq + 1)
                    if seq >= 1:
                        invert(seq - 1)
                invert(NSEQ - 1)

            @block.vector
            def _(dve):
                normalise(dve)

                def take_keys(seq):
                    for i, c in enumerate(chunks):
                        if c[0:2] != (K, seq):
                            continue
                        h = c[2]
                        dve.wait_ge(S["projected"], i + 1)
                        hh = h if seq % 2 == 0 else HALVES - 1 - h
                        dst = rkv[:, K, seq, hh * CH:(hh + 1) * CH]
                        if seq % 2:
                            dst = dst[:, ::-1]
                        dve.tensor_copy(dst, ps[i % 8][:, :]).then_inc(S["keys_in"], 1)

                def stage_a(q):
                    d, k = q % 2, rkv[:, K, q, :]
                    old, new = mx[:, q % 2, 0:N], mx[:, q % 2, 1:1 + N]
                    dve.wait_ge(S["keys_in"], HALVES * (q + 1))
                    if q >= 2:
                        dve.wait_ge(S["kept"], q - 1)
                        dve.wait_ge(S["clipped"], 2 * (q - 1))
                    dve.tensor_tensor_scan(new, decay[:, d:d + 1].to_broadcast([P, N]), k,
                                           -1e38, ALU.add, ALU.max).then_inc(S["max_scanned"], 1)
                    dve.wait_ge(S["max_scanned"], q + 1)
                    dve.scalar_tensor_tensor(diff[:, q % 2, :], k, first_col(d), old, ALU.add, ALU.subtract)\
                        .then_inc(S["shifted"], 1)
                    if q >= NX:
                        dve.wait_ge(S["mixed"], q - NX + 1)
                    dve.scalar_tensor_tensor(ex[:, q % NX, E1S, :], old, decay[:, d:d + 1], new,
                                             ALU.add, ALU.subtract).then_inc(S["decayed"], 1)
                    dve.wait_ge(S["shifted"], q + 1)
                    dve.tensor_scalar(ex[:, q % NX, E1, :], diff[:, q % 2, :], -1.0, 0.0, ALU.mult, ALU.min)\
                        .then_inc(S["clipped"], 1)
                    dve.tensor_scalar(ex[:, q % NX, E2, :], diff[:, q % 2, :], 0.0, None, ALU.min)\
                        .then_inc(S["clipped"], 1)

                def stage_b(q):
                    e1, e2, e1s, e2s = (ex[:, q % NX, e, :] for e in range(4))
                    bot, top = e1s, e2s
                    dve.wait_ge(S["weights_in"], 4 * q + 4)
                    if q >= 2:
                        dve.wait_ge(S["top_in"], q - 1)
                    dve.tensor_tensor_scan(den[:, q % 2, 1:1 + N], e1s, e2s, 0.0, ALU.mult, ALU.add)\
                        .then_inc(S["den_scanned"], 1)
                    dve.wait_ge(S["values_in"], 2 * q + 1)
                    dve.tensor_tensor_scan(num[:, q % 2, 1:1 + N], e1s, ev[:, q % 2, 0, :], 0.0,
                                           ALU.mult, ALU.add).then_inc(S["num_scanned"], 1)
                    dve.wait_ge(S["num_scanned"], q + 1)
                    dve.wait_ge(S["den_scanned"], q + 1)
                    dve.tensor_tensor(bot, den[:, q % 2, 0:N], e1, ALU.mult).then_inc(S["den_scaled"], 1)
                    dve.tensor_tensor(top, num[:, q % 2, 0:N], e1, ALU.mult).then_inc(S["num_scaled"], 1)
                    dve.wait_ge(S["den_scaled"], q + 1)
                    dve.tensor_tensor(bot, bot, e2, ALU.add).then_inc(S["den_out"], 1)
                    dve.wait_ge(S["num_scaled"], q + 1)
                    dve.wait_ge(S["values_in"], 2 * q + 2)
                    dve.tensor_tensor(top, top, ev[:, q % 2, 1, :], ALU.add).then_inc(S["top_in"], 1)

                def stage_c(q):
                    dve.wait_ge(S["inv_in"], q + 1)
                    dve.wait_ge(S["gated"], q + 1)
                    dst = mixed[:, q, :] if q % 2 == 0 else mixed[:, q, ::-1]
                    dve.tensor_tensor(dst, ex[:, q % NX, E2S, :], ex[:, q % NX, E1S, :], ALU.mult)\
                        .then_inc(S["mixed"], 1)

                def add_out(b):
                    for h in range(HALVES):
                        c = HALVES * b + h
                        dve.wait_ge(S["out_done"], c + 1)
                        dst = xT[:, b, h * CH:(h + 1) * CH]
                        dve.tensor_tensor(dst, dst, ps[c][:, :], ALU.add).then_inc(r_x, 1)

                take_keys(0)
                dve.wait_ge(S["decay_exp"], 1)
                dve.tensor_scalar(decay[:, :], decay[:, :], -1.0, None, ALU.mult).then_inc(S["decay_in"], 1)
                dve.memset(mx[:, :, 0:1], -1e38).then_inc(S["decay_in"], 1)
                dve.memset(num[:, :, 0:1], 0.0).then_inc(S["decay_in"], 1)
                dve.memset(den[:, :, 0:1], 0.0).then_inc(S["decay_in"], 1)
                dve.wait_ge(S["decay_in"], 4)
                for q in range(NSEQ + 2):
                    if q < NSEQ:
                        stage_a(q)
                    if q + 1 < NSEQ:
                        take_keys(q + 1)
                    if q >= 2:
                        stage_c(q - 2)
                    if 1 <= q <= NSEQ:
                        stage_b(q - 1)
                    if q == NSEQ:
                        add_out(0)
                add_out(1)

            @block.gpsimd
            def _(pool):
                def keep(q):
                    pool.wait_ge(S["max_scanned"], q + 1)
                    if q >= NX:
                        pool.wait_ge(S["mixed"], q - NX + 1)
                    pool.tensor_tensor(ex[:, q % NX, E2S, :], rkv[:, K, q, :], mx[:, q % 2, 1:1 + N],
                                       ALU.subtract).then_inc(S["kept"], 1)

                def weigh_values(q):
                    pool.wait_ge(S["weights_in"], 4 * q + 4)
                    pool.wait_ge(S["rest_in"], by_act.index((V, q, HALVES - 1)) + 1)
                    if q >= 2:
                        pool.wait_ge(S["top_in"], q - 1)
                    for e, at in ((E2S, 0), (E2, 1)):
                        pool.tensor_tensor(ev[:, q % 2, at, :], ex[:, q % NX, e, :], rkv[:, V, q, :], ALU.mult)\
                            .then_inc(S["values_in"], 1)

                def gate(q):
                    pool.wait_ge(S["top_in"], q + 1)
                    pool.wait_ge(S["rest_in"], by_act.index((R, q, HALVES - 1)) + 1)
                    top = ex[:, q % NX, E2S, :]
                    pool.tensor_tensor(top, top, rkv[:, R, q, :], ALU.mult).then_inc(S["gated"], 1)

                for q in range(NSEQ + 2):
                    if q < NSEQ:
                        keep(q)
                    if q >= 2:
                        gate(q - 2)
                    if q < NSEQ:
                        weigh_values(q)


_NAMES = {
    "x": "L0_attn_a_hidden_states", "a_wq": "L0_attn_a_Wq", "a_wk": "L0_attn_a_Wk", "a_wv": "L0_attn_a_Wv",
    "a_wo": "L0_attn_a_Wo", "wqkv": "L0_ffn_wqkv", "q_scale": "L0_ffn_q_scale", "k_scale": "L0_ffn_k_scale",
    "wo": "L0_ffn_wo", "w1": "L0_ffn_w1", "w2": "L0_ffn_w2",
}


def _columns(inputs):
    cols = np.zeros((P, COLS), np.float32)
    for at, name in ((COL_LN_G, "L0_ffn_ln_g"), (COL_LN_B, "L0_ffn_ln_b"), (COL_B2, "L0_ffn_b2")):
        cols[:, at:at + DEPTH] = np.asarray(inputs[name]).T
    b1 = np.asarray(inputs["L0_ffn_b1"]).reshape(DEPTH, 2, HID)
    for l in range(DEPTH):
        for k in range(2):
            for c, (c0, m) in enumerate(HC):
                cols[:m, COL_B1 + (l * 2 + k) * len(HC) + c] = b1[l, k, c0:c0 + m]
    for n, name in enumerate(("time_decay", "time_first", "time_decay_rev", "time_first_rev")):
        cols[:, COL_R + n] = np.asarray(inputs["L0_attn_b_" + name])
    return cols


def kernel(**inputs):
    import concourse.bacc as bacc
    from concourse.bass_utils import run_bass_kernel_spmd

    nc = bacc.Bacc("TRN2", target_bir_lowering=False, num_devices=1)
    arrays = {k: np.ascontiguousarray(inputs[v]) for k, v in _NAMES.items()}
    arrays["cols"] = _columns(inputs)
    arrays["r_w"] = np.ascontiguousarray(np.asarray(inputs["L0_attn_b_rkv_w"]).T)
    arrays["r_out"] = np.ascontiguousarray(np.asarray(inputs["L0_attn_b_out_w"]).T)
    arrays.update(zip(("square", "mask", "identB", "rot"), shape_constants()))
    t_in = {k: nc.dram_tensor(f"in_{k}", a.shape, mybir.dt.from_np(a.dtype), kind="ExternalInput").ap()
            for k, a in arrays.items()}
    out = nc.dram_tensor("out", (B, N, D), F32, kind="ExternalOutput").ap()
    build(nc, t_in, out)
    r = run_bass_kernel_spmd(nc, [{f"in_{k}": a for k, a in arrays.items()}], core_ids=[0])
    return r.results[0]["out"]
```

```python
import math
from contextlib import ExitStack

import numpy as np

import concourse.bass as bass
from concourse import mybir

B, N, D = 2, 1024, 128
P = 128
NT = N // P
TOK = B * N
CH = 512
NCH = TOK // CH
LN_EPS = 1e-5

AH, AF, AV = 16, 16, 64
HG = 4
NHG = AH // HG
PAIRS = [(0, 0), (0, 1), (0, 2), (1, 0), (1, 1), (2, 0)]
KROWS = AF * len(PAIRS)
UNITS = [(j, i) for j in range(NT) for i in range(j + 1)]
NU = len(UNITS)

DEPTH, HEADS, DH, WIN = 2, 8, 64, 64
INNER = HEADS * DH
HID = int(D * 4 * 2 / 3)
HC = [(c * P, min(P, HID - c * P)) for c in range(-(-HID // P))]
NG = DEPTH * NT
QK_SCALE = 8.0
NEG = -1e30
SS_SHIFT = 65536.0

F32 = mybir.dt.float32
BF16 = mybir.dt.bfloat16
ALU = mybir.AluOpType
ACT = mybir.ActivationFunctionType
AX = mybir.AxisListType
COL_LN_G, COL_LN_B, COL_B2, COL_B1 = 0, DEPTH, 2 * DEPTH, 3 * DEPTH
COL_R = COL_B1 + DEPTH * 2 * len(HC)
COLS = COL_R + 4
GELU_SET = "gelu_and_others"
EXP_SET = "natural_log_exp_and_others"


def shape_constants():
    ident = np.eye(P, dtype=np.float32)
    mean = np.full((P, P), 1.0 / D, np.float32)
    ones = np.ones((P, P), np.float32)
    m, n = np.arange(P)[:, None], np.arange(P)[None, :]
    causal = (m <= n).astype(np.float32)
    square = np.stack([ident, ident - mean, mean, ones, causal], axis=1)
    q, k = np.arange(WIN)[:, None], np.arange(WIN)[None, :]
    own = np.where(k <= q, 0.0, NEG)
    prev = np.where(k >= q, 0.0, NEG)
    none = np.full((WIN, WIN), NEG)
    mask = np.zeros((P, NT, P), np.float32)
    for t in range(NT):
        mask[:WIN, t] = np.concatenate([own, prev if t else none], axis=1)
        mask[WIN:, t] = np.concatenate([prev, own], axis=1)
    half = np.arange(0, DH, 2, dtype=np.float32)
    inv_freq = (1.0 / np.float32(10000.0) ** (half / np.float32(DH))).astype(np.float32)
    t = np.arange(N, dtype=np.float32)
    freqs = (t[:, None] * inv_freq[None, :]).astype(np.float32)
    freqs = np.concatenate([freqs, freqs], axis=-1).astype(np.float64)
    base = ((half + 0.4 * DH) / (1.4 * DH)).astype(np.float32)
    power = ((t - N // 2) / float(WIN // 2)).astype(np.float32)
    scale = base[None, :].astype(np.float64) ** power[:, None].astype(np.float64)
    scale = np.concatenate([scale, scale], axis=-1)
    sign = np.where(np.arange(DH) < DH // 2, -1.0, 1.0)
    cos, sin = np.cos(freqs), np.sin(freqs) * sign
    rot = np.stack([cos * scale * QK_SCALE, cos / scale, sin * scale * QK_SCALE, sin / scale])
    rot = rot.reshape(4, NT, P, DH).transpose(2, 0, 1, 3).astype(np.float32)
    return (np.ascontiguousarray(square), np.ascontiguousarray(mask.astype(mybir.dt.np(BF16))),
            ident.astype(mybir.dt.np(BF16)), np.ascontiguousarray(rot))


def build(nc, t_in, out):
    nc.disable_value_cache = True
    ctx = ExitStack()
    with ctx:
        def sem(name):
            return ctx.enter_context(nc.semaphore(name))

        def at_least(eng, s, value):
            if isinstance(value, int) and value <= 0:
                return
            eng.wait_ge(s, value)

        ps = [ctx.enter_context(nc.psum_tensor(f"bank{i}", [P, CH], F32)) for i in range(8)]

        def sb(name, shape, dt=F32, stack=None):
            return (stack or ctx).enter_context(nc.sbuf_tensor(name, shape, dt))

        xT = sb("xT", [P, B, N])
        y0 = sb("y0", [P, B, 1 + N])
        square = sb("square", [P, 5, P])
        identB = sb("identB", [P, P], BF16)
        ident, centre, mean, ones, causal = (square[:, k, :] for k in range(5))
        cols = sb("cols", [P, COLS])
        eps_col = sb("eps_col", [P, 3])
        ln_sqr = sb("ln_sqr", [P, 2, CH])
        ln_log = sb("ln_log", [P, 2, CH])
        ln_inv = sb("ln_inv", [P, 2, CH])

        dram = nc.dram_tensor("parts_dram", [2, 3, AH * AF, TOK], BF16, kind="Internal").ap()

        ld_x, ld_const = sem("ld_x"), sem("ld_const")
        set_up, x_turned, x_in = sem("set_up"), sem("x_turned"), sem("x_in")
        ln_added, ln_centred, ln_squared = sem("ln_added"), sem("ln_centred"), sem("ln_squared")
        ln_var, ln_logged, ln_scaled, ln_done = (sem("ln_var"), sem("ln_logged"), sem("ln_scaled"),
                                                 sem("ln_done"))
        st = sem("stored")

        def y0_chunk(c):
            b, h = divmod(c * CH, N)
            return y0[:, b, 1 + h:1 + h + CH]

        def x_chunk(c):
            b, h = divmod(c * CH, N)
            return xT[:, b, h:h + CH]

        def ln_tensor(pe, n, x_ready):
            base = NCH * n

            def variance(c):
                pe.wait_ge(ln_squared, base + c + 1)
                pe.matmul(ps[6 + c % 2][:, :], mean, ln_sqr[:, c % 2, :],
                          start=True, stop=True).then_inc(ln_var, 1)

            for c in range(NCH):
                x_ready(pe, c)
                if c >= 2:
                    pe.wait_ge(ln_done, base + c - 1)
                pe.matmul(ps[4 + c % 2][:, :], centre, x_chunk(c), start=True, stop=True)\
                    .then_inc(ln_centred, 1)
                if c >= 1:
                    variance(c - 1)
            variance(NCH - 1)

        def ln_scalar(act, n):
            base = NCH * n
            act.preload_act_table_set(EXP_SET)

            def inverse(c):
                act.wait_ge(ln_var, base + c + 1)
                act.activation(ln_log[:, c % 2, :], ps[6 + c % 2][:, :], ACT.Ln, bias=eps_col[:, 0:1])\
                    .then_inc(ln_logged, 1)
                act.wait_ge(ln_logged, base + c + 1)
                at_least(act, ln_done, base + c - 1 if c >= 2 else 0)
                act.activation(ln_inv[:, c % 2, :], ln_log[:, c % 2, :], ACT.Exp, scale=-0.5)\
                    .then_inc(ln_scaled, 1)

            for c in range(NCH):
                act.wait_ge(ln_centred, base + c + 1)
                if c >= 2:
                    act.wait_ge(ln_var, base + c - 1)
                act.activation(ln_sqr[:, c % 2, :], ps[4 + c % 2][:, :], ACT.Square)\
                    .then_inc(ln_squared, 1)
                if c >= 1:
                    inverse(c - 1)
            inverse(NCH - 1)

        def ln_vector(dve, n):
            for c in range(NCH):
                dve.wait_ge(ln_scaled, NCH * n + c + 1)
                dve.tensor_tensor(y0_chunk(c), ps[4 + c % 2][:, :], ln_inv[:, c % 2, :], ALU.mult)\
                    .then_inc(ln_done, 1)

        def add_stream(dve):
            for c in range(NCH):
                dve.tensor_tensor(x_chunk(c), x_chunk(c), y0_chunk(c), ALU.add).then_inc(ln_added, 1)

        y_done = sem("y_done")
        a_x = sem("a_x")
        r_x = sem("r_x")
        x_ready = [lambda e, c: e.wait_ge(x_in, c + 1),
                   lambda e, c: e.wait_ge(a_x, 2 * B * NHG + 2),
                   lambda e, c: e.wait_ge(ln_added, c + 1),
                   lambda e, c: e.wait_ge(r_x, c + 1)]

        with ExitStack() as s0:
            x_tok = sb("x_tok", [P, TOK // P, D], stack=s0)
            with nc.Block() as block:
                @block.sync
                def _(sp):
                    for c in range(NCH):
                        sp.dma_start(x_tok[:, 4 * c:4 * c + 4, :],
                                     t_in["x"].rearrange("b (t p) d -> p (b t) d", p=P)[:, 4 * c:4 * c + 4, :])\
                            .then_inc(ld_x, 16)
                        if c == 0:
                            sp.dma_start(square[:, :, :], t_in["square"]).then_inc(ld_const, 16)
                            sp.dma_start(identB[:, :], t_in["identB"]).then_inc(ld_const, 16)
                            sp.dma_start(cols[:, :], t_in["cols"]).then_inc(ld_const, 16)

                @block.gpsimd
                def _(pool):
                    pool.memset(eps_col[:, 0:1], LN_EPS).then_inc(set_up, 1)
                    pool.memset(eps_col[:, 1:2], 0.5 * math.log(SS_SHIFT)).then_inc(set_up, 1)
                    pool.memset(eps_col[:, 2:3], 1.0).then_inc(set_up, 1)
                    pool.memset(y0[:, :, 0:1], 0.0).then_inc(set_up, 1)

                @block.tensor
                def _(pe):
                    pe.wait_ge(ld_const, 48)
                    pe.wait_ge(ld_x, 16 * NCH)
                    for c in range(NCH):
                        for k in range(4):
                            last = pe.transpose(ps[c][:, k * P:(k + 1) * P], x_tok[:, 4 * c + k, :], ident)
                        last.then_inc(x_turned, 1)
                    ln_tensor(pe, 0, x_ready[0])

                @block.scalar
                def _(act):
                    act.wait_ge(set_up, 4)
                    for c in range(NCH):
                        act.wait_ge(x_turned, c + 1)
                        act.copy(x_chunk(c), ps[c][:, :]).then_inc(x_in, 1)
                    ln_scalar(act, 0)

                @block.vector
                def _(dve):
                    ln_vector(dve, 0)

        linear_attention(nc, t_in, sb, sem, ps, dram, xT, y0, ident, ones, causal, eps_col,
                         a_x, at_least, y0_chunk)

        def normalise(n, eng):
            if eng is nc.tensor:
                ln_tensor(eng, n, x_ready[n])
            elif eng is nc.scalar:
                ln_scalar(eng, n)
            else:
                if n == 2:
                    add_stream(eng)
                ln_vector(eng, n)

        def norm_block(n):
            with nc.Block() as block:
                @block.tensor
                def _(pe):
                    ln_tensor(pe, n, x_ready[n])

                @block.scalar
                def _(act):
                    ln_scalar(act, n)

                @block.vector
                def _(dve):
                    ln_vector(dve, n)

        F = ffn_sems(sem)
        ffn_args = (y0, y_done, ident, centre, mean, identB, eps_col, cols, at_least)
        norm_block(1)
        ffn(nc, t_in, sb, ps, F, 0, *ffn_args)
        rwkv(nc, t_in, sb, sem, ps, xT, y0, cols, r_x,
             lambda eng: normalise(2, eng), lambda eng, c: eng.wait_ge(ln_done, 2 * NCH + c + 1))
        norm_block(3)
        ffn(nc, t_in, sb, ps, F, 1, *ffn_args)
        with nc.Block() as block:
            @block.vector
            def _(dve):
                add_stream(dve)

        store_out(nc, sb, sem, ps, out, xT, ident, st)


def store_out(nc, sb, sem, ps, out, xT, ident, st):
    turned, copied = sem("out_turned"), sem("out_copied")
    with ExitStack() as stack:
        o_tok = sb("o_tok", [P, TOK // P, D], stack=stack)
        with nc.Block() as block:
            @block.tensor
            def _(pe):
                for c in range(NCH):
                    for k in range(4):
                        b, t = divmod(4 * c + k, NT)
                        last = pe.transpose(ps[c][:, k * P:(k + 1) * P], xT[:, b, t * P:(t + 1) * P], ident)
                    last.then_inc(turned, 1)

            @block.scalar
            def _(act):
                for c in range(0, NCH, 2):
                    act.wait_ge(turned, c + 1)
                    act.copy(o_tok[:, 4 * c:4 * c + 4, :], ps[c][:, :]).then_inc(copied, 1)

            copied2 = sem("out_copied2")

            @block.vector
            def _(dve):
                for c in range(1, NCH, 2):
                    dve.wait_ge(turned, c + 1)
                    dve.tensor_copy(o_tok[:, 4 * c:4 * c + 4, :], ps[c][:, :]).then_inc(copied2, 1)

            @block.sync
            def _(sp):
                for c in range(NCH):
                    sp.wait_ge((copied, copied2)[c % 2], c // 2 + 1)
                    sp.dma_start(out.rearrange("b (t p) d -> p (b t) d", p=P)[:, 4 * c:4 * c + 4, :],
                                 o_tok[:, 4 * c:4 * c + 4, :]).then_inc(st, 16)
                sp.wait_ge(st, 16 * NCH)


def linear_attention(nc, t_in, sb, sem, ps, parts, xT, y0, ident, ones, causal, eps_col,
                     a_x, at_least, y0_chunk):
    NV = AV + 1
    NS, NA = 3, 4
    ld_w, ld_wo = sem("a_ld_w"), sem("a_ld_wo")
    proj, p1_done, r1_done, p2_done, p3_done = (sem("a_proj"), sem("a_p1_done"), sem("a_r1_done"),
                                                sem("a_p2_done"), sem("a_p3_done"))
    parts_out, stacked, v_copied = sem("a_parts_out"), sem("a_stacked"), sem("a_v_copied")
    v_proj, v_by_act, v_by_dve, v_ones = sem("a_v_proj"), sem("a_v_by_act"), sem("a_v_by_dve"), sem("a_v_ones")
    scored, squared, weighed, diagonal = sem("a_scored"), sem("a_squared"), sem("a_weighed"), sem("a_diagonal")
    prefixed, prefix_used = sem("a_prefixed"), sem("a_prefix_used")
    z_in, z_inv, y_out = sem("a_z_in"), sem("a_z_inv"), sem("a_y_out")
    y_turned, y_copied, heads_out = sem("a_y_turned"), sem("a_y_copied"), sem("a_heads_out")
    NIT = B * NHG
    with ExitStack() as stack:
        def s(name, shape, dt=F32):
            return sb(name, shape, dt, stack)
        wqk = s("wqk", [P, 2, AH * AF])
        values = s("values", [P, B * NT, AH, NV])
        with ExitStack() as early:
            wv = sb("wv", [P, AH * AV], F32, early)
            part = sb("part", [P, 4, 3, TOK], BF16, early)
            rest = sb("rest", [P, 2, CH], F32, early)

            with nc.Block() as block:
                @block.sync
                def _(sp):
                    sp.dma_start(wqk[:, 0, :], t_in["a_wq"]).then_inc(ld_w, 16)
                    sp.dma_start(wqk[:, 1, :], t_in["a_wk"]).then_inc(ld_w, 16)
                    sp.dma_start(wv[:, :], t_in["a_wv"]).then_inc(ld_w, 16)
                    for c in range(NCH):
                        sp.wait_ge(p3_done, 4 * (c + 1))
                        for g in range(4):
                            sp.dma_start(parts[g // 2, :, (g % 2) * P:(g % 2 + 1) * P, c * CH:(c + 1) * CH]
                                         .rearrange("a p n -> p a n"),
                                         part[:, g, :, c * CH:(c + 1) * CH]).then_inc(parts_out, 16)
                    sp.wait_ge(parts_out, 16 * 4 * NCH)

                @block.gpsimd
                def _(pool):
                    pool.memset(values[:, :, :, AV:NV], 1.0).then_inc(v_ones, 1)

                @block.tensor
                def _(pe):
                    pe.wait_ge(ld_w, 48)
                    for u in range(4 * NCH):
                        c, g = divmod(u, 4)
                        at_least(pe, r1_done, u - 3)
                        pe.matmul(ps[u % 4][:, :], wqk[:, g // 2, (g % 2) * P:(g % 2 + 1) * P], y0_chunk(c),
                                  start=True, stop=True).then_inc(proj, 1)
                        for v in range(2 * u, 2 * u + 2):
                            b, j = divmod(u, NT)
                            at_least(pe, (v_by_act, v_by_dve)[v % 2], v // 2 - 1)
                            pe.matmul(ps[4 + v % 4][:, :], y0[:, b, 1 + j * P:1 + (j + 1) * P],
                                      wv[:, (v % 2) * CH:(v % 2 + 1) * CH], start=True, stop=True)\
                                .then_inc(v_proj, 1)

                def copy_values(eng, v):
                    return (values[:, v // 2, 8 * (v % 2):8 * (v % 2) + 8, 0:AV],
                            ps[4 + v % 4][:, :].rearrange("p (h e) -> p h e", h=8))

                @block.scalar
                def _(act):
                    def second(u):
                        act.wait_ge(r1_done, u + 1)
                        act.copy(part[:, u % 4, 1, (u // 4) * CH:(u // 4 + 1) * CH], rest[:, u % 2, :])\
                            .then_inc(p2_done, 1)
                    for u in range(4 * NCH):
                        act.wait_ge(proj, u + 1)
                        act.copy(part[:, u % 4, 0, (u // 4) * CH:(u // 4 + 1) * CH], ps[u % 4][:, :])\
                            .then_inc(p1_done, 1)
                        if u >= 1:
                            second(u - 1)
                        act.wait_ge(v_proj, 2 * u + 1)
                        act.copy(*copy_values(act, 2 * u)).then_inc(v_by_act, 1)
                    second(4 * NCH - 1)

                @block.vector
                def _(dve):
                    def third(u):
                        dve.wait_ge(p2_done, u + 1)
                        at = slice((u // 4) * CH, (u // 4 + 1) * CH)
                        dve.tensor_tensor(part[:, u % 4, 2, at], rest[:, u % 2, :], part[:, u % 4, 1, at],
                                          ALU.subtract).then_inc(p3_done, 1)
                    for u in range(4 * NCH):
                        dve.wait_ge(p1_done, u + 1)
                        at_least(dve, p3_done, u - 1)
                        at = slice((u // 4) * CH, (u // 4 + 1) * CH)
                        dve.tensor_tensor(rest[:, u % 2, :], ps[u % 4][:, :], part[:, u % 4, 0, at],
                                          ALU.subtract).then_inc(r1_done, 1)
                        if u >= 1:
                            third(u - 1)
                        dve.wait_ge(v_proj, 2 * u + 2)
                        dve.tensor_copy(*copy_values(dve, 2 * u + 1)).then_inc(v_by_dve, 1)
                    third(4 * NCH - 1)

        v_prefix = s("v_prefix", [P, 2, HG, NV])
        v_now = s("v_now", [P, 2, NT, HG, NV])
        q_stack = s("q_stack", [P, 2, HG, N], BF16)
        k_stack = s("k_stack", [P, 2, HG, N], BF16)
        wo_slot = s("wo_slot", [P, 2, D])
        sq = s("sq", [P, NA, HG, P])
        sq_diag = s("sq_diag", [P, 2, HG, P])
        z_sum = s("z_sum", [P, 2, HG])
        z_rec = s("z_rec", [P, 2, HG])
        y_tok = s("y_tok", [P, 2, HG * AV])
        y_feat = s("y_feat", [P, 2, N])
        score_bank = ps[0:NS]
        y_bank = ps[3:5]
        turn_bank = ps[5]
        out_bank = ps[6:8]
        with nc.Block() as block:
            @block.sync
            def _(sp):
                with sp.Fori(0, NIT) as it:
                    b, hg = sp.snap(it // NHG), sp.snap(it % NHG)
                    sp.wait_ge(heads_out, it * 2 + 2)
                    for qk, st_ in enumerate((q_stack, k_stack)):
                        for r, pair in enumerate(PAIRS):
                            src = parts[qk, pair[qk], bass.ds(hg * (HG * AF), HG * AF), bass.ds(b * N, N)]
                            sp.dma_start(st_[r * AF:(r + 1) * AF, bass.ds(it % 2, 1), :, :],
                                         src.rearrange("(h f) n -> f h n", h=HG)).then_inc(stacked, 16)
                    sp.wait_ge(stacked, (it + 1) * (16 * 2 * len(PAIRS)))
                    sp.wait_ge(heads_out, it * 2 + 4)
                    sp.dma_start(wo_slot[:, :, :], t_in["a_wo"][bass.ds(hg * (2 * P), 2 * P), :]
                                 .rearrange("(c p) n -> p c n", p=P)).then_inc(ld_wo, 16)

            @block.gpsimd
            def _(pool):
                with pool.Fori(0, NIT // 2) as pair:
                    for side in range(2):
                        step = pair * 2 + side
                        uses = pool.snap(step * (NT - 2))
                        pool.wait_ge(heads_out, step * 2 + 2)
                        pool.tensor_copy(v_now[:, side], values[:, bass.ds((step // NHG) * NT, NT),
                                                                bass.ds((step % NHG) * HG, HG), :]).then_inc(v_copied, 1)
                        pool.wait_ge(v_copied, step + 1)
                        for j in range(1, NT - 1):
                            pool.wait_ge(prefix_used, uses + j)
                            before = v_now[:, side, 0]
                            if j > 1:
                                before = v_prefix[:, (j - 1) % 2]
                                pool.wait_ge(prefixed, uses + j - 1)
                            pool.tensor_tensor(v_prefix[:, j % 2], before, v_now[:, side, j], ALU.add)\
                                .then_inc(prefixed, 1)

            @block.tensor
            def _(pe):
                pe.sem_inc(heads_out, 4)
                pe.sem_inc(weighed, NA)
                pe.sem_inc(prefix_used, 2)
                pe.sem_inc(y_turned, 2)
                with pe.Fori(0, NIT // 2) as pair:
                    for side in range(2):
                        step = pe.snap(pair * 2 + side)
                        units, tiles, uses = (pe.snap(step * c) for c in (NU, NT, NT - 2))
                        pe.wait_ge(stacked, (step + 1) * (16 * 2 * len(PAIRS)))
                        pe.wait_ge(v_copied, step + 1)

                        def scores(k):
                            j, i = UNITS[k]
                            pe.wait_ge(squared, units + k + 1)
                            for h in range(HG):
                                last = pe.matmul(score_bank[k % NS][:, h * P:(h + 1) * P],
                                                 k_stack[0:KROWS, side, h, i * P:(i + 1) * P],
                                                 q_stack[0:KROWS, side, h, j * P:(j + 1) * P],
                                                 start=True, stop=True, skip_group_check=True)
                            last.then_inc(scored, 1)

                        def turn(j):
                            pe.wait_ge(y_out, tiles + j + 1 + 2)
                            pe.wait_ge(y_copied, tiles + j + 1)
                            for c in range(2):
                                last = pe.transpose(turn_bank[:, (j % 2) * 256 + c * P:(j % 2) * 256 + (c + 1) * P],
                                                    y_tok[:, j % 2, c * P:(c + 1) * P], ident)
                            last.then_inc(y_turned, 1)

                        scores(0)
                        scores(1)
                        for k, (j, i) in enumerate(UNITS):
                            if k + 2 < NU:
                                scores(k + 2)
                            if i == 0:
                                pe.wait_ge(y_out, tiles + j + 1)
                                if j == 1:
                                    pe.matmul(y_bank[1][:, 0:HG * NV], ones, v_now[:, side, 0],
                                              start=True, stop=False, skip_group_check=True)
                                elif j:
                                    pe.wait_ge(prefixed, uses + j - 1)
                                    pe.matmul(y_bank[j % 2][:, 0:HG * NV], ones, v_prefix[:, (j - 1) % 2],
                                              start=True, stop=False, skip_group_check=True).then_inc(prefix_used, 1)
                            if i == j:
                                pe.wait_ge(diagonal, tiles + j + 1)
                            else:
                                pe.wait_ge(squared, units + k + 1 + NS)
                            a = sq_diag[:, j % 2] if i == j else sq[:, k % NA]
                            for h in range(HG):
                                last = pe.matmul(y_bank[j % 2][:, h * NV:(h + 1) * NV], a[:, h, :],
                                                 v_now[:, side, i, h, :],
                                                 start=(j == 0 and h == 0), stop=(i == j), skip_group_check=True)
                            last.then_inc(weighed, 1)
                            if j >= 1 and i == 1:
                                turn(j - 1)
                        turn(NT - 1)
                        pe.wait_ge(ld_wo, (step + 1) * 16)
                        pe.wait_ge(y_copied, tiles + NT + 2)
                        for half in range(2):
                            pe.wait_ge(a_x, step * 2 + half + 1)
                            for c in range(2):
                                last = pe.matmul(out_bank[half][:, :], wo_slot[:, c, :],
                                                 y_feat[:, c, half * CH:(half + 1) * CH], start=(c == 0), stop=(c == 1))
                            last.then_inc(heads_out, 1)

            @block.scalar
            def _(act):
                act.sem_inc(squared, NS)
                act.sem_inc(y_copied, 2)
                with act.Fori(0, NIT) as it:
                    units, tiles, outs = act.snap(it * NU), act.snap(it * NT), act.snap(it * 2)
                    def copy_turned(j):
                        act.wait_ge(y_turned, tiles + j + 1 + 2)
                        act.wait_ge(heads_out, outs + 4)
                        act.copy(y_feat[:, :, j * P:(j + 1) * P],
                                 turn_bank[:, (j % 2) * 256:(j % 2) * 256 + 256]
                                 .rearrange("p (c n) -> p c n", c=2)).then_inc(y_copied, 1)
                    for k, (j, i) in enumerate(UNITS):
                        act.wait_ge(scored, units + k + 1)
                        act.wait_ge(weighed, units + k + 1)
                        act.activation(sq[:, k % NA], score_bank[k % NS][:, :].rearrange("p (h n) -> p h n", h=HG),
                                       ACT.Square, bias=eps_col[:, 2:3], scale=0.25).then_inc(squared, 1)
                        if j >= 1 and i == min(2, j) and not (j == 1):
                            copy_turned(j - 1)
                        if j == 2 and i == 0:
                            copy_turned(0)
                    copy_turned(NT - 1)

            @block.vector
            def _(dve):
                dve.sem_inc(y_out, 2)
                dve.sem_inc(a_x, 2)
                with dve.Fori(0, NIT) as it:
                    units, tiles, outs = dve.snap(it * NU), dve.snap(it * NT), dve.snap(it * 2)
                    b = it // NHG
                    for j in range(NT):
                        k = UNITS.index((j, j))
                        dve.wait_ge(squared, units + k + 1 + NS)
                        dve.scalar_tensor_tensor(sq_diag[:, j % 2], sq[:, k % NA], 1.0,
                                                 causal.unsqueeze(1).to_broadcast([P, HG, P]),
                                                 ALU.add, ALU.mult).then_inc(diagonal, 1)
                        dve.wait_ge(weighed, units + k + 1 + NA)
                        yb = y_bank[j % 2][:, 0:HG * NV].rearrange("p (h e) -> p h e", h=HG)
                        dve.tensor_scalar(z_sum[:, j % 2], yb[:, :, AV], 2e-12, None, ALU.add).then_inc(z_in, 1)
                        dve.wait_ge(z_in, tiles + j + 1)
                        dve.reciprocal(z_rec[:, j % 2], z_sum[:, j % 2]).then_inc(z_inv, 1)
                        dve.wait_ge(z_inv, tiles + j + 1)
                        dve.wait_ge(y_turned, tiles + j + 1)
                        dve.tensor_tensor(y_tok[:, j % 2].rearrange("p (h e) -> p h e", h=HG), yb[:, :, 0:AV],
                                          z_rec[:, j % 2].unsqueeze(2).to_broadcast([P, HG, AV]), ALU.mult)\
                            .then_inc(y_out, 1)
                    for half in range(2):
                        dve.wait_ge(heads_out, outs + half + 1 + 4)
                        dst = xT[:, bass.ds(b, 1), half * CH:(half + 1) * CH]
                        dve.tensor_tensor(dst, dst, out_bank[half][:, :], ALU.add).then_inc(a_x, 1)


def ffn_sems(sem):
    names = """ld_tab ld_qkv ld_wo ld_w1 ld_w2 set_up tab_done h_in qkv_done qk_squared v_out v_mixed_0 v_mixed_1 ss_in ss_clipped ss_log
        qk_inv qk_rotated qk_summed qk_normed qk_turned q_out k_out sim_done max_done exp_done sum_inv p_normed
        p_turned p_out_lo p_out_hi pv_done o_out_0 o_out_1 wo_done mid_done h2_in centred squared var_done
        var_log var_inv normed affine hid_mm gelu_done hid_done w2_done""".split()
    return {n: sem("f_" + n) for n in names}


def ffn(nc, t_in, sb, ps, S, call, y0, y_done, ident, centre, mean, identB, eps_col, cols, at_least):
    G0 = call * NG
    with ExitStack() as stack:
        def s(name, shape, dt=F32):
            return sb(f"{name}_{call}", shape, dt, stack)
        y1 = s("y1", [P, B, 1 + N])
        wqkv = s("wqkv", [P, DEPTH, 3 * INNER])
        wo = s("wo", [P, INNER // P, D])
        w1 = s("w1", [P, 2 * HID])
        w2 = s("w2", [P, len(HC), D])
        mask = s("mask", [P, NT, P], BF16)
        rot = s("rot", [P, DEPTH, 4, NT, DH])
        gains = s("gains", [P, 2, DEPTH, DH])
        h = s("h", [P, 2, B, P])
        qk_sq = s("qk_sq", [P, 2 * INNER])
        ss = s("ss", [P, B, 3, 2 * HEADS])
        qk_scale = s("qk_scale", [P, B, 2 * HEADS])
        rot_a = s("rot_a", [P, B, 2 * INNER])
        rot_b = s("rot_b", [P, B, 2 * INNER])
        v_nat = s("v_nat", [P, 2, B, INNER])
        v_mix = s("v_mix", [P, 2, B, INNER])
        qT = s("qT", [P, 2, B, HEADS // 2, P])
        kT = s("kT", [P, 2, B, HEADS // 2, P])
        neg_max = s("neg_max", [P, B, 2, HEADS // 2])
        prob = s("prob", [P, B, HEADS, P])
        p_sum = s("p_sum", [P, B, HEADS])
        p_inv = s("p_inv", [P, B, HEADS])
        probT = s("probT", [P, B, HEADS, P])
        oT = s("oT", [P, 2, HEADS // 2, B, P])
        h2 = s("h2", [P, B, P])
        c_sq = s("c_sq", [P, B * P])
        v_log = s("v_log", [P, B * P])
        v_inv = s("v_inv", [P, B * P])
        normed = s("normed", [P, B * P])
        hn = s("hn", [P, B * P])
        gel = s("gel", [P, 2, B * P])
        hid = s("hid", [P, len(HC), B * P])
        BP = B * P
        qk_bank = ps[0:2]
        v_bank = ps[2]
        sim_bank = ps[3:5]
        turn_bank = ps[5:7]
        m_bank = ps[7]
        hid_bank = [ps[2], *turn_bank]
        HORDER = (1, 2, 0)

        def b1_col(l, k, c, m):
            return cols[0:m, bass.ds(l * (2 * len(HC)) + (COL_B1 + k * len(HC) + c), 1)]

        def slots(eng, stage):
            stage(0, 0, True, False, False, False)
            stage(1, 1, True, True, False, False)
            stage(2, 0, True, True, True, False)
            stage(3, 1, True, True, True, True)
            with eng.Fori(2, NG // 2) as pair:
                stage(eng.snap(pair * 2), 0, True, True, True, True)
                stage(eng.snap(pair * 2 + 1), 1, True, True, True, True)
            stage(NG, 0, False, True, True, True)
            stage(NG + 1, 1, False, False, True, True)
            stage(NG + 2, 0, False, False, False, True)

        def run(on, *calls):
            if on:
                for f, *args in calls:
                    f(*args)

        def cap(value, most):
            return min(value, most) if isinstance(value, int) else value

        def w(eng, name, value):
            per = {"": 0}
            total = G0 * PER[name] + value
            at_least(eng, S[name], total)

        PER = dict(h_in=2, qkv_done=2, qk_squared=4, v_out=2, v_mixed_0=16, v_mixed_1=16, ss_in=2, ss_clipped=2, ss_log=2,
                   qk_inv=2, qk_rotated=2, qk_summed=2, qk_normed=2, qk_turned=2, q_out=2, k_out=2, sim_done=4,
                   max_done=4, exp_done=4, sum_inv=2, p_normed=2, p_turned=2, p_out_lo=2, p_out_hi=2, pv_done=2,
                   o_out_0=1, o_out_1=1, wo_done=1, mid_done=1, h2_in=2, centred=1, squared=1, var_done=1,
                   var_log=1, var_inv=1, normed=1, affine=1, hid_mm=3, gelu_done=3, hid_done=3, w2_done=1)
        def mixed(eng, g, par):
            if isinstance(g, int) and g < 0:
                return
            w(eng, f"v_mixed_{par}", g * 16 + (32 if par == 0 else 16))

        TAB_LOADS = 3 + 2 * DEPTH

        with nc.Block() as block:
            @block.sync
            def _(sp):
                def load_wo(l):
                    sp.dma_start(wo[:, :, :], t_in["wo"][l].rearrange("(c p) n -> p c n", p=P))\
                        .then_inc(S["ld_wo"], 16)

                def load_w1(l):
                    sp.dma_start(w1[:, :], t_in["w1"][l]).then_inc(S["ld_w1"], 16)

                def load_w2(l):
                    full = HID // P
                    sp.dma_start(w2[:, 0:full, :], t_in["w2"][l, 0:full * P, :]
                                 .rearrange("(c p) n -> p c n", p=P)).then_inc(S["ld_w2"], 16)
                    sp.dma_start(w2[0:HC[-1][1], full, :], t_in["w2"][l, full * P:HID, :]).then_inc(S["ld_w2"], 16)

                sp.dma_start(wqkv[:, :, :], t_in["wqkv"].rearrange("l p n -> p l n")).then_inc(S["ld_qkv"], 16)
                sp.dma_start(rot[:, 0], t_in["rot"]).then_inc(S["ld_tab"], 16)
                sp.dma_start(rot[:, 1], t_in["rot"]).then_inc(S["ld_tab"], 16)
                sp.dma_start(mask[:, :, :], t_in["mask"]).then_inc(S["ld_tab"], 16)
                for l in range(DEPTH):
                    for k, name in enumerate(("q_scale", "k_scale")):
                        sp.dma_start(gains[:, k, l, :], t_in[name][l:l + 1, :].to_broadcast([P, DH]))\
                            .then_inc(S["ld_tab"], 16)
                load_wo(0)
                load_w1(0)
                load_w2(0)

                def stage(g, par):
                    w(sp, "v_out", 2 * g + 2)
                    w(sp, "pv_done", 2 * g - 2)
                    for rows, src in ((slice(0, WIN), par), (slice(WIN, P), 1 - par)):
                        sp.dma_start(v_mix[rows, par], v_nat[rows, src]).then_inc(S[f"v_mixed_{par}"], 16)

                last = NT + 2
                for g in range(4):
                    stage(g, g % 2)
                with sp.Fori(2, last // 2) as pair:
                    stage(sp.snap(pair * 2), 0)
                    stage(sp.snap(pair * 2 + 1), 1)
                w(sp, "wo_done", NT)
                sp.wait_ge(S["ld_wo"], 16 * (2 * call + 1))
                load_wo(1)
                w(sp, "hid_mm", 3 * NT)
                sp.wait_ge(S["ld_w1"], 16 * (2 * call + 1))
                load_w1(1)
                w(sp, "w2_done", NT)
                sp.wait_ge(S["ld_w2"], 32 * (2 * call + 1))
                load_w2(1)
                with sp.Fori(last // 2, NG // 2) as pair:
                    stage(sp.snap(pair * 2), 0)
                    stage(sp.snap(pair * 2 + 1), 1)

            @block.tensor
            def _(pe):
                def stage(g, par, on1, on2, on3, on4):
                    if on2:
                        g2, par2 = g - 1, 1 - par
                    if on3:
                        g3, par3 = g - 2, par
                    if on4:
                        g4 = g - 3
                    if on1:
                        layer1 = g // NT if isinstance(g, int) else pe.snap(g // NT)

                    def project(b):
                        if b == 0:
                            w(pe, "h_in", 2 * g + 2)
                        w(pe, "qk_rotated", 2 * g + b)
                        for k, bank in enumerate((*qk_bank, v_bank)):
                            if k == 2:
                                w(pe, "v_out", 2 * g + b)
                                if b == 0:
                                    w(pe, "normed", g - 2)
                                else:
                                    w(pe, "hid_done", 3 * g - 6)
                            last = pe.matmul(bank[:, :], h[:, par, b, :],
                                             wqkv[:, bass.ds(layer1, 1), k * INNER:(k + 1) * INNER],
                                             start=True, stop=True)
                        last.then_inc(S["qkv_done"], 1)

                    def similar(b):
                        t = g2 % NT
                        w(pe, "q_out", 2 * g2 + b + 1)
                        w(pe, "k_out", 2 * g2 + b + 1)
                        off = t * P
                        w(pe, "exp_done", 4 * g2 + 2 * b)
                        for half in range(2):
                            pe.matmul(sim_bank[half][:, :].rearrange("p (h n) -> p h n", h=4), identB[:, :],
                                      mask.rearrange("p t n -> p (t n)")[:, bass.ds(off, P)].unsqueeze(1)
                                      .to_broadcast([P, 4, P]),
                                      start=True, stop=False, skip_group_check=True)
                        for hh in range(4):
                            o = hh * P
                            q, k_, kp = qT[:, par2, b, hh], kT[:, par2, b, hh], kT[:, 1 - par2, b, hh]
                            for half in range(2):
                                rows, bank = slice(half * DH, half * DH + DH), sim_bank[half]
                                pe.matmul(bank[0:WIN, o:o + WIN], q[rows, 0:WIN], k_[rows, 0:WIN],
                                          start=False, stop=False, skip_group_check=True)
                                pe.matmul(bank[WIN:P, o:o + P], q[rows, WIN:P], k_[rows, 0:P],
                                          start=False, stop=True, skip_group_check=True)
                                last = pe.matmul(bank[0:WIN, o + WIN:o + P], q[rows, 0:WIN], kp[rows, WIN:P],
                                                 start=False, stop=True, skip_group_check=True)
                                if hh == 3:
                                    last.then_inc(S["sim_done"], 1)

                    def turn_qk(b, m):
                        w(pe, "qk_normed", 2 * m + b + 1)
                        w(pe, "p_out_lo", 2 * m - 1 + b)
                        w(pe, "p_out_hi", 2 * m - 1 + b)
                        w(pe, "q_out", 2 * m + b)
                        w(pe, "k_out", 2 * m + b)
                        for k in range(2):
                            for c in range(INNER // P):
                                last = pe.transpose(turn_bank[k][:, c * P:(c + 1) * P],
                                                    rot_a[:, b, k * INNER + c * P:k * INNER + (c + 1) * P], ident)
                        last.then_inc(S["qk_turned"], 1)

                    def turn_p(b, m):
                        w(pe, "p_normed", 2 * m + b + 1)
                        w(pe, "q_out", cap(2 * m + 2 + b, 2 * NG))
                        w(pe, "k_out", cap(2 * m + 2 + b, 2 * NG))
                        w(pe, "p_out_lo", 2 * m + b)
                        w(pe, "p_out_hi", 2 * m + b)
                        if b == 1 and on4:
                            w(pe, "hid_done", 3 * g4 + 3)
                        for hd in range(HEADS):
                            last = pe.transpose(turn_bank[hd // 4][:, (hd % 4) * P:(hd % 4 + 1) * P],
                                                prob[:, b, hd, :], ident)
                        last.then_inc(S["p_turned"], 1)

                    def attend(b, m, slot):
                        w(pe, "p_out_lo", 2 * m + b + 1)
                        w(pe, "p_out_hi", 2 * m + b + 1)
                        mixed(pe, m, slot)
                        if b == 0:
                            w(pe, "mid_done", m)
                        else:
                            w(pe, "o_out_0", m + 1)
                            if on4:
                                at_least(pe, y_done, G0 + g4 + 1)
                        for pr in range(HEADS // 2):
                            for half, vals in enumerate((v_mix, v_nat)):
                                for sub in range(2):
                                    hd = 2 * pr + sub
                                    last = pe.matmul(
                                        m_bank[sub * DH:(sub + 1) * DH, pr * P + half * WIN:pr * P + (half + 1) * WIN],
                                        vals[:, slot, b, hd * DH:(hd + 1) * DH],
                                        probT[:, b, hd, half * WIN:(half + 1) * WIN],
                                        start=True, stop=True, skip_group_check=True)
                        last.then_inc(S["pv_done"], 1)

                    def out_proj():
                        pe.wait_ge(S["ld_wo"], (g3 // NT + (2 * call + 1)) * 16)
                        w(pe, "o_out_0", g3 + 1)
                        w(pe, "o_out_1", g3 + 1)
                        for c in range(INNER // P):
                            last = pe.matmul(m_bank[:, 0:BP], wo[:, c, :], oT[:, par3, c].rearrange("p b n -> p (b n)"),
                                             start=(c == 0), stop=(c == INNER // P - 1), skip_group_check=True)
                        last.then_inc(S["wo_done"], 1)

                    def take_mean_off():
                        w(pe, "h2_in", 2 * g3 + 2)
                        if on1:
                            w(pe, "v_out", 2 * g + 2)
                        elif on4:
                            w(pe, "hid_done", 3 * g4 + 3)
                        pe.matmul(v_bank[:, BP:2 * BP], centre, h2[:, :, :].rearrange("p b n -> p (b n)"),
                                  start=True, stop=True, skip_group_check=True).then_inc(S["centred"], 1)

                    def variance():
                        w(pe, "squared", g3 + 1)
                        pe.matmul(v_bank[:, 0:BP], mean, c_sq[:, :], start=True, stop=True, skip_group_check=True)\
                            .then_inc(S["var_done"], 1)

                    def hidden(c):
                        w(pe, "affine", g4 + 1)
                        if c == HORDER[0]:
                            pe.wait_ge(S["ld_w1"], (g4 // NT + (2 * call + 1)) * 16)
                        if hid_bank[c] is v_bank:
                            w(pe, "v_out", cap(2 * g4 + 7, 2 * NG))
                        else:
                            w(pe, "q_out", cap(2 * g4 + 5, 2 * NG))
                            w(pe, "k_out", cap(2 * g4 + 5, 2 * NG))
                            w(pe, "p_out_lo", cap(2 * g4 + 3, 2 * NG))
                            w(pe, "p_out_hi", cap(2 * g4 + 3, 2 * NG))
                        c0, m = HC[c]
                        for k in range(2):
                            last = pe.matmul(hid_bank[c][0:m, k * BP:(k + 1) * BP],
                                             w1[:, k * HID + c0:k * HID + c0 + m], hn[:, :],
                                             start=True, stop=True, skip_group_check=True)
                        last.then_inc(S["hid_mm"], 1)

                    def down():
                        w(pe, "hid_done", 3 * g4 + 3)
                        pe.wait_ge(S["ld_w2"], (g4 // NT + (2 * call + 1)) * 32)
                        w(pe, "mid_done", g4 + 1)
                        w(pe, "o_out_0", cap(g4 + 2, NG))
                        for c, (c0, m) in enumerate(HC):
                            last = pe.matmul(m_bank[:, 0:BP], w2[0:m, c, :], hid[0:m, c, :],
                                             start=(c == 0), stop=(c == len(HC) - 1), skip_group_check=True)
                        last.then_inc(S["w2_done"], 1)

                    run(on1, (project, 0))
                    run(on4, *((hidden, c) for c in HORDER))
                    run(on2, (similar, 0))
                    run(on3, (turn_p, 1, g - 2))
                    run(on4, (down,))
                    run(on2, (turn_qk, 1, g - 1))
                    run(on3, (attend, 1, g - 2, par))
                    run(on1, (project, 1))
                    run(on3, (out_proj,))
                    run(on2, (similar, 1), (turn_p, 0, g - 1))
                    run(on3, (take_mean_off,))
                    run(on1, (turn_qk, 0, g))
                    run(on2, (attend, 0, g - 1, 1 - par))
                    run(on3, (variance,))

                pe.wait_ge(S["ld_tab"], 16 * TAB_LOADS * (call + 1))
                pe.wait_ge(S["ld_qkv"], 16 * (call + 1))
                pe.wait_ge(S["set_up"], 3 * (call + 1))
                slots(pe, stage)

            @block.scalar
            def _(act):
                def stage(g, par, on1, on2, on3, on4):
                    if on2:
                        g2, par2 = g - 1, 1 - par
                    if on3:
                        g3, par3 = g - 2, par
                    if on4:
                        g4 = g - 3
                        l4 = g4 // NT

                    def square_qk(b):
                        w(act, "qkv_done", 2 * g + b + 1)
                        w(act, "ss_in", 2 * g + b)
                        for k in range(2):
                            act.activation(qk_sq[:, k * INNER:(k + 1) * INNER], qk_bank[k][:, :], ACT.Square)\
                                .then_inc(S["qk_squared"], 1)
                        w(act, "pv_done", 2 * g - 3 + b)
                        if b == 0:
                            mixed(act, g - 1, 1 - par)
                        act.copy(v_nat[:, par, b, :], v_bank[:, :]).then_inc(S["v_out"], 1)

                    def norms(b, g):
                        w(act, "ss_clipped", 2 * g + b + 1)
                        act.activation(ss[:, b, 2, :], ss[:, b, 1, :], ACT.Ln, scale=SS_SHIFT).then_inc(S["ss_log"], 1)
                        w(act, "ss_log", 2 * g + b + 1)
                        w(act, "qk_normed", 2 * g + b - 1)
                        act.activation(qk_scale[:, b, :], ss[:, b, 2, :], ACT.Exp, scale=-0.5,
                                       bias=eps_col[:, 1:2]).then_inc(S["qk_inv"], 1)

                    def softmax(b, halves):
                        w(act, "p_turned", 2 * g2 + b - 1)
                        w(act, "sum_inv", 2 * g2 + b - 1)
                        for half in halves:
                            w(act, "max_done", 4 * g2 + 2 * b + half + 1)
                            for hh in range(4):
                                hd = 2 * hh + half
                                last = act.activation(prob[:, b, hd, :], sim_bank[half][:, hh * P:(hh + 1) * P],
                                                      ACT.Exp, bias=neg_max[:, b, half, hh:hh + 1],
                                                      accum_out=p_sum[:, b, hd:hd + 1])
                            last.then_inc(S["exp_done"], 1)

                    def square_centred():
                        w(act, "centred", g3 + 1)
                        w(act, "var_done", g3)
                        act.activation(c_sq[:, :], v_bank[:, BP:2 * BP], ACT.Square).then_inc(S["squared"], 1)

                    def inverse_std():
                        w(act, "var_done", g3 + 1)
                        act.activation(v_log[:, :], v_bank[:, 0:BP], ACT.Ln, bias=eps_col[:, 0:1])\
                            .then_inc(S["var_log"], 1)
                        w(act, "var_log", g3 + 1)
                        w(act, "normed", g3)
                        act.activation(v_inv[:, :], v_log[:, :], ACT.Exp, scale=-0.5).then_inc(S["var_inv"], 1)

                    def copy_qk(b, m, slot):
                        w(act, "qk_turned", 2 * m + b + 1)
                        w(act, "sim_done", 4 * m - 6 + 2 * b)
                        act.copy(qT[:, slot, b, :, :], turn_bank[0][:, :].rearrange("p (c n) -> p c n", n=P))\
                            .then_inc(S["q_out"], 1)
                        w(act, "sim_done", 4 * m - 2 + 2 * b)
                        act.copy(kT[:, slot, b, :, :], turn_bank[1][:, :].rearrange("p (c n) -> p c n", n=P))\
                            .then_inc(S["k_out"], 1)

                    def copy_p(b, m):
                        w(act, "p_turned", 2 * m + b + 1)
                        w(act, "pv_done", 2 * m + b - 1)
                        act.copy(probT[:, b, 0:4, :], turn_bank[0][:, :].rearrange("p (c n) -> p c n", n=P))\
                            .then_inc(S["p_out_lo"], 1)

                    def gelu(i):
                        c = HORDER[i]
                        w(act, "hid_mm", 3 * g4 + i + 1)
                        w(act, "hid_done", 3 * g4 + i - 1)
                        m = HC[c][1]
                        act.activation(gel[0:m, i % 2, :], hid_bank[c][0:m, BP:2 * BP], ACT.Gelu,
                                       bias=b1_col(l4, 1, c, m)).then_inc(S["gelu_done"], 1)

                    def copy_o():
                        w(act, "pv_done", 2 * g2 + 1)
                        w(act, "wo_done", g2 - 1)
                        act.copy(oT[:, par2, :, 0, :], m_bank[:, :].rearrange("p (c n) -> p c n", n=P))\
                            .then_inc(S["o_out_0"], 1)

                    run(on2, (norms, 1, g - 1))
                    run(on1, (square_qk, 0))
                    run(on4, (act.preload_act_table_set, GELU_SET), (gelu, 0), (gelu, 1), (gelu, 2),
                        (act.preload_act_table_set, EXP_SET))
                    run(on2, (softmax, 0, (0,)))
                    run(on3, (copy_p, 1, g - 2))
                    run(on2, (softmax, 0, (1,)))
                    run(on1, (norms, 0, g))
                    run(on2, (copy_qk, 1, g - 1, 1 - par))
                    run(on1, (square_qk, 1))
                    run(on2, (copy_p, 0, g - 1))
                    run(on3, (square_centred,))
                    run(on1, (copy_qk, 0, g, par))
                    run(on3, (inverse_std,))
                    run(on2, (softmax, 1, (0, 1)), (copy_o,))

                act.preload_act_table_set(EXP_SET)
                act.wait_ge(S["ld_tab"], 16 * TAB_LOADS * (call + 1))
                slots(act, stage)

            @block.vector
            def _(dve):
                def tok(buf, rows, b, t, ahead):
                    return buf[rows, b, bass.ds(t * P + ahead, P)]

                def shifted(eng, out, buf, t, s_):
                    eng.tensor_copy(out[0:D // 2], buf[0:D // 2, :, bass.ds(t * P + 1, P)]).then_inc(s_, 1)
                    eng.tensor_copy(out[D // 2:D], buf[D // 2:D, :, bass.ds(t * P, P)]).then_inc(s_, 1)

                def stage(g, par, on1, on2, on3, on4):
                    if on2:
                        g2, par2 = g - 1, 1 - par
                    if on3:
                        g3, par3 = g - 2, par
                        t3 = g3 % NT if isinstance(g3, int) else dve.snap(g3 % NT)
                    if on4:
                        g4 = g - 3
                        t4, l4 = g4 % NT, g4 // NT
                        if not isinstance(g4, int):
                            t4, l4 = dve.snap(t4), dve.snap(l4)
                    if on1:
                        t1, l1 = g % NT, g // NT
                        if not isinstance(g, int):
                            t1, l1 = dve.snap(t1), dve.snap(l1)

                    def take_in():
                        at_least(dve, y_done, G0 + g - 3)
                        w(dve, "qkv_done", 2 * g - 2)
                        shifted(dve, h[:, par], y0, t1, S["h_in"])

                    def rotate(b):
                        w(dve, "qk_summed", 2 * g + b - 1)
                        w(dve, "qk_turned", 2 * g + b - 1)
                        for k in range(2):
                            w(dve, "qk_squared", 4 * g + 2 * b + k + 1)
                            x = qk_bank[k][:, :].rearrange("p (h d) -> p h d", d=DH)
                            ra = rot_a[:, b, k * INNER:(k + 1) * INNER].rearrange("p (h d) -> p h d", d=DH)
                            rb = rot_b[:, b, k * INNER:(k + 1) * INNER].rearrange("p (h d) -> p h d", d=DH)
                            HF = DH // 2

                            def tab(i, lo, hi):
                                return rot[:, bass.ds(l1, 1), i, bass.ds(t1, 1), lo:hi]\
                                    .rearrange("p a b d -> p (a b) d").to_broadcast([P, HEADS, hi - lo])
                            dve.tensor_tensor(ra, x, tab(k, 0, DH), ALU.mult)
                            dve.tensor_tensor(rb[:, :, 0:HF], x[:, :, HF:DH], tab(2 + k, 0, HF), ALU.mult)
                            last = dve.tensor_tensor(rb[:, :, HF:DH], x[:, :, 0:HF], tab(2 + k, HF, DH), ALU.mult)
                        last.then_inc(S["qk_rotated"], 1)

                    def norms(b, g):
                        w(dve, "qk_squared", 4 * g + 2 * b + 2)
                        w(dve, "ss_clipped", 2 * g + b - 1)
                        dve.tensor_reduce(ss[:, b, 0, :], qk_sq[:, :].rearrange("p (h d) -> p h d", d=DH),
                                          AX.X, ALU.add).then_inc(S["ss_in"], 1)
                        w(dve, "ss_in", 2 * g + b + 1)
                        w(dve, "ss_log", 2 * g + b - 1)
                        dve.tensor_scalar(ss[:, b, 1, :], ss[:, b, 0, :], 1e-24, None, ALU.max)\
                            .then_inc(S["ss_clipped"], 1)

                    def maxima(b):
                        w(dve, "exp_done", 4 * g2 + 2 * b - 2)
                        for half in range(2):
                            w(dve, "sim_done", 4 * g2 + 2 * b + half + 1)
                            dve.tensor_reduce(neg_max[:, b, half, :],
                                              sim_bank[half][:, :].rearrange("p (h n) -> p h n", n=P),
                                              AX.X, ALU.max, negate=True).then_inc(S["max_done"], 1)

                    def invert_sums(b, m):
                        w(dve, "exp_done", 4 * m + 2 * b + 2)
                        w(dve, "p_normed", 2 * m + b - 1)
                        dve.reciprocal(p_inv[:, b, :], p_sum[:, b, :]).then_inc(S["sum_inv"], 1)

                    def copy_p(b, m):
                        w(dve, "p_turned", 2 * m + b + 1)
                        w(dve, "pv_done", 2 * m + b - 1)
                        dve.tensor_copy(probT[:, b, 4:8, :], turn_bank[1][:, :].rearrange("p (c n) -> p c n", n=P))\
                            .then_inc(S["p_out_hi"], 1)

                    def copy_o():
                        w(dve, "pv_done", 2 * g3 + 2)
                        w(dve, "wo_done", g3 - 1)
                        dve.tensor_copy(oT[:, par3, :, 1, :], m_bank[:, :].rearrange("p (c n) -> p c n", n=P))\
                            .then_inc(S["o_out_1"], 1)

                    def add_attention():
                        w(dve, "wo_done", g3 + 1)
                        w(dve, "h2_in", 2 * g3)
                        at = bass.ds(t3 * P + 1, P)
                        dve.tensor_tensor(y1[:, :, at], y0[:, :, at],
                                          m_bank[:, 0:BP].rearrange("p (b n) -> p b n", b=B), ALU.add)\
                            .then_inc(S["mid_done"], 1)
                        w(dve, "mid_done", g3 + 1)
                        w(dve, "centred", g3)
                        shifted(dve, h2, y1, t3, S["h2_in"])

                    def normalise():
                        w(dve, "var_inv", g4 + 1)
                        w(dve, "affine", g4)
                        dve.tensor_tensor(normed[:, :], v_bank[:, BP:2 * BP], v_inv[:, :], ALU.mult)\
                            .then_inc(S["normed"], 1)
                        w(dve, "normed", g4 + 1)
                        w(dve, "hid_mm", 3 * g4)
                        dve.tensor_scalar(hn[:, :], normed[:, :], cols[:, bass.ds(l4 + COL_LN_G, 1)],
                                          cols[:, bass.ds(l4 + COL_LN_B, 1)], ALU.mult, ALU.add).then_inc(S["affine"], 1)

                    def gate(i):
                        c = HORDER[i]
                        w(dve, "gelu_done", 3 * g4 + i + 1)
                        if i == 0:
                            w(dve, "w2_done", g4)
                        m = HC[c][1]
                        dve.scalar_tensor_tensor(hid[0:m, c, :], hid_bank[c][0:m, 0:BP],
                                                 b1_col(l4, 0, c, m),
                                                 gel[0:m, i % 2, :], ALU.add, ALU.mult).then_inc(S["hid_done"], 1)

                    def give_out():
                        w(dve, "w2_done", g4 + 1)
                        w(dve, "h_in", cap(2 * g4 + 4, 2 * NG))
                        at = bass.ds(t4 * P + 1, P)
                        dve.scalar_tensor_tensor(y0[:, :, at], m_bank[:, 0:BP].rearrange("p (b n) -> p b n", b=B),
                                                 cols[:, bass.ds(l4 + COL_B2, 1)], y1[:, :, at], ALU.add, ALU.add)\
                            .then_inc(y_done, 1)

                    run(on1, (take_in,))
                    run(on2, (norms, 1, g - 1))
                    run(on4, (normalise,))
                    run(on3, (invert_sums, 1, g - 2))
                    run(on1, (rotate, 0))
                    run(on4, (gate, 0), (gate, 1), (gate, 2))
                    run(on2, (maxima, 0))
                    run(on3, (copy_p, 1, g - 2))
                    run(on4, (give_out,))
                    run(on1, (norms, 0, g))
                    run(on3, (copy_o,))
                    run(on2, (invert_sums, 0, g - 1))
                    run(on1, (rotate, 1))
                    run(on3, (add_attention,))
                    run(on2, (copy_p, 0, g - 1), (maxima, 1))

                dve.wait_ge(S["ld_tab"], 16 * TAB_LOADS * (call + 1))
                tabs = 0
                for l in range(DEPTH):
                    for k in range(2):
                        HF = DH // 2
                        for i, lo, hi, g0 in ((k, 0, DH, 0), (2 + k, 0, HF, HF), (2 + k, HF, DH, 0)):
                            t_ = rot[:, l, i, :, lo:hi]
                            dve.tensor_tensor(t_, t_, gains[:, k, l, g0:g0 + hi - lo].unsqueeze(1)
                                              .to_broadcast([P, NT, hi - lo]), ALU.mult).then_inc(S["tab_done"], 1)
                            tabs += 1
                dve.wait_ge(S["tab_done"], tabs * (call + 1))
                dve.wait_ge(S["set_up"], 3 * (call + 1))
                slots(dve, stage)

            @block.gpsimd
            def _(pool):
                def stage(g, par, on1, on2, on3, on4):
                    def sum_and_scale(b):
                        w(pool, "qk_rotated", 2 * g + b + 1)
                        pool.tensor_tensor(rot_b[:, b, :], rot_a[:, b, :], rot_b[:, b, :], ALU.add)\
                            .then_inc(S["qk_summed"], 1)
                        w(pool, "qk_summed", 2 * g + b + 1)
                        w(pool, "qk_inv", 2 * g + b + 1)
                        pool.tensor_tensor(rot_a[:, b, :].rearrange("p (h d) -> p h d", d=DH),
                                           rot_b[:, b, :].rearrange("p (h d) -> p h d", d=DH),
                                           qk_scale[:, b, :].unsqueeze(2).to_broadcast([P, 2 * HEADS, DH]), ALU.mult)\
                            .then_inc(S["qk_normed"], 1)

                    def scale_probs(b, m):
                        w(pool, "sum_inv", 2 * m + b + 1)
                        pool.tensor_tensor(prob[:, b], prob[:, b],
                                           p_inv[:, b, :].unsqueeze(2).to_broadcast([P, HEADS, P]), ALU.mult)\
                            .then_inc(S["p_normed"], 1)

                    run(on3, (scale_probs, 1, g - 2))
                    run(on1, (sum_and_scale, 0))
                    run(on2, (scale_probs, 0, g - 1))
                    run(on1, (sum_and_scale, 1))

                pool.memset(kT[:, 1], 0.0).then_inc(S["set_up"], 1)
                pool.memset(v_nat[:, 1], 0.0).then_inc(S["set_up"], 1)
                pool.memset(y1[:, :, 0:1], 0.0).then_inc(S["set_up"], 1)
                pool.wait_ge(S["set_up"], 3 * (call + 1))
                slots(pool, stage)


def rwkv(nc, t_in, sb, sem, ps, xT, y0, cols, r_x, normalise, y_ready):
    NSEQ = 2 * B
    HALVES = N // CH
    R, K, V = range(3)
    chunks = [(K, 0), (V, 0), *((R, s) for s in range(NSEQ)),
              *((what, s) for s in range(1, NSEQ) for what in (K, V))]
    chunks = [(what, s, h) for what, s in chunks for h in range(HALVES)]
    by_dve = [c for c in chunks if c[0] == K]
    by_act = [c for c in chunks if c[0] != K]
    names = """ld_w ld_out projected keys_in rest_in decay_exp decay_in max_scanned kept decayed shifted clipped
        weights_in den_scanned num_scanned values_in den_scaled den_out num_scaled top_in gated log_in inv_in
        mixed out_done""".split()
    S = {n: sem("r_" + n) for n in names}
    with ExitStack() as stack:
        def s(name, shape, dt=F32):
            return sb("r_" + name, shape, dt, stack)
        w_in = s("w_in", [P, 6 * D])
        w_out = s("w_out", [P, 2, D])
        decay = s("decay", [P, 2])
        rkv = s("rkv", [P, 3, NSEQ, N])
        mx = s("mx", [P, 2, 1 + N])
        diff = s("diff", [P, 2, N])
        NX = 3
        ex = s("ex", [P, NX, 4, N])
        E1, E2, E1S, E2S = range(4)
        ev = s("ev", [P, 2, 2, N])
        num = s("num", [P, 2, 1 + N])
        den = s("den", [P, 2, 1 + N])
        mixed = s("mixed", [P, NSEQ, N])

        def first_col(d):
            return cols[:, COL_R + 2 * d + 1:COL_R + 2 * d + 2]

        with nc.Block() as block:
            @block.sync
            def _(sp):
                sp.dma_start(w_in[:, :], t_in["r_w"]).then_inc(S["ld_w"], 16)
                sp.dma_start(w_out[:, :, :], t_in["r_out"].rearrange("(c p) n -> p c n", p=P))\
                    .then_inc(S["ld_out"], 16)

            @block.tensor
            def _(pe):
                normalise(pe)
                pe.wait_ge(S["ld_w"], 16)
                for i, (what, seq, h) in enumerate(chunks):
                    b, d = divmod(seq, 2)
                    if i >= 8:
                        c = chunks[i - 8]
                        if c[0] == K:
                            pe.wait_ge(S["keys_in"], by_dve.index(c) + 1)
                        else:
                            pe.wait_ge(S["rest_in"], by_act.index(c) + 1)
                    y_ready(pe, NCH - 1 if i >= 4 else HALVES * b + h)
                    at = (3 * d + what) * D
                    pe.matmul(ps[i % 8][:, :], w_in[:, at:at + D], y0[:, b, 1 + h * CH:1 + (h + 1) * CH],
                              start=True, stop=True).then_inc(S["projected"], 1)
                pe.wait_ge(S["ld_out"], 16)
                for b in range(B):
                    pe.wait_ge(S["mixed"], 2 * b + 2)
                    for h in range(HALVES):
                        c = HALVES * b + h
                        if b == 0:
                            pe.wait_ge(S["keys_in"], len(by_dve))
                            pe.wait_ge(S["rest_in"], len(by_act))
                        for d in range(2):
                            last = pe.matmul(ps[c][:, :], w_out[:, d, :], mixed[:, 2 * b + d, h * CH:(h + 1) * CH],
                                             start=(d == 0), stop=(d == 1))
                        last.then_inc(S["out_done"], 1)

            @block.scalar
            def _(act):
                normalise(act)

                def take(want):
                    for i, c in enumerate(chunks):
                        if c not in by_act or not want(c):
                            continue
                        what, seq, h = c
                        act.wait_ge(S["projected"], i + 1)
                        hh = h if seq % 2 == 0 else HALVES - 1 - h
                        dst = rkv[:, what, seq, hh * CH:(hh + 1) * CH]
                        if seq % 2:
                            dst = rkv[:, what, seq, hh * CH:(hh + 1) * CH][:, ::-1]
                        act.activation(dst, ps[i % 8][:, :], ACT.Sigmoid if what == R else ACT.Copy)\
                            .then_inc(S["rest_in"], 1)

                def weights(q):
                    for e, name, n in ((E1, "clipped", 2 * q + 1), (E2, "clipped", 2 * q + 2),
                                       (E1S, "decayed", q + 1), (E2S, "kept", q + 1)):
                        act.wait_ge(S[name], n)
                        act.activation(ex[:, q % NX, e, :], ex[:, q % NX, e, :], ACT.Exp)\
                            .then_inc(S["weights_in"], 1)

                def invert(q):
                    bot = ex[:, q % NX, E1S, :]
                    act.wait_ge(S["den_out"], q + 1)
                    act.activation(bot, bot, ACT.Ln).then_inc(S["log_in"], 1)
                    act.wait_ge(S["log_in"], q + 1)
                    act.activation(bot, bot, ACT.Exp, scale=-1.0).then_inc(S["inv_in"], 1)

                take(lambda c: c[0] == V and c[1] == 0)
                take(lambda c: c[0] == R)
                act.preload_act_table_set(EXP_SET)
                act.activation(decay[:, :], cols[:, COL_R:COL_R + 4:2], ACT.Exp).then_inc(S["decay_exp"], 1)
                for seq in range(NSEQ):
                    weights(seq)
                    if seq + 1 < NSEQ:
                        take(lambda c: c[0] == V and c[1] == seq + 1)
                    if seq >= 1:
                        invert(seq - 1)
                invert(NSEQ - 1)

            @block.vector
            def _(dve):
                normalise(dve)

                def take_keys(seq):
                    for i, c in enumerate(chunks):
                        if c[0:2] != (K, seq):
                            continue
                        h = c[2]
                        dve.wait_ge(S["projected"], i + 1)
                        hh = h if seq % 2 == 0 else HALVES - 1 - h
                        dst = rkv[:, K, seq, hh * CH:(hh + 1) * CH]
                        if seq % 2:
                            dst = dst[:, ::-1]
                        dve.tensor_copy(dst, ps[i % 8][:, :]).then_inc(S["keys_in"], 1)

                def stage_a(q):
                    d, k = q % 2, rkv[:, K, q, :]
                    old, new = mx[:, q % 2, 0:N], mx[:, q % 2, 1:1 + N]
                    dve.wait_ge(S["keys_in"], HALVES * (q + 1))
                    if q >= 2:
                        dve.wait_ge(S["kept"], q - 1)
                        dve.wait_ge(S["clipped"], 2 * (q - 1))
                    dve.tensor_tensor_scan(new, decay[:, d:d + 1].to_broadcast([P, N]), k,
                                           -1e38, ALU.add, ALU.max).then_inc(S["max_scanned"], 1)
                    dve.wait_ge(S["max_scanned"], q + 1)
                    dve.scalar_tensor_tensor(diff[:, q % 2, :], k, first_col(d), old, ALU.add, ALU.subtract)\
                        .then_inc(S["shifted"], 1)
                    if q >= NX:
                        dve.wait_ge(S["mixed"], q - NX + 1)
                    dve.scalar_tensor_tensor(ex[:, q % NX, E1S, :], old, decay[:, d:d + 1], new,
                                             ALU.add, ALU.subtract).then_inc(S["decayed"], 1)
                    dve.wait_ge(S["shifted"], q + 1)
                    dve.tensor_scalar(ex[:, q % NX, E1, :], diff[:, q % 2, :], -1.0, 0.0, ALU.mult, ALU.min)\
                        .then_inc(S["clipped"], 1)
                    dve.tensor_scalar(ex[:, q % NX, E2, :], diff[:, q % 2, :], 0.0, None, ALU.min)\
                        .then_inc(S["clipped"], 1)

                def stage_b(q):
                    e1, e2, e1s, e2s = (ex[:, q % NX, e, :] for e in range(4))
                    bot, top = e1s, e2s
                    dve.wait_ge(S["weights_in"], 4 * q + 4)
                    if q >= 2:
                        dve.wait_ge(S["top_in"], q - 1)
                    dve.tensor_tensor_scan(den[:, q % 2, 1:1 + N], e1s, e2s, 0.0, ALU.mult, ALU.add)\
                        .then_inc(S["den_scanned"], 1)
                    dve.wait_ge(S["values_in"], 2 * q + 1)
                    dve.tensor_tensor_scan(num[:, q % 2, 1:1 + N], e1s, ev[:, q % 2, 0, :], 0.0,
                                           ALU.mult, ALU.add).then_inc(S["num_scanned"], 1)
                    dve.wait_ge(S["num_scanned"], q + 1)
                    dve.wait_ge(S["den_scanned"], q + 1)
                    dve.tensor_tensor(bot, den[:, q % 2, 0:N], e1, ALU.mult).then_inc(S["den_scaled"], 1)
                    dve.tensor_tensor(top, num[:, q % 2, 0:N], e1, ALU.mult).then_inc(S["num_scaled"], 1)
                    dve.wait_ge(S["den_scaled"], q + 1)
                    dve.tensor_tensor(bot, bot, e2, ALU.add).then_inc(S["den_out"], 1)
                    dve.wait_ge(S["num_scaled"], q + 1)
                    dve.wait_ge(S["values_in"], 2 * q + 2)
                    dve.tensor_tensor(top, top, ev[:, q % 2, 1, :], ALU.add).then_inc(S["top_in"], 1)

                def stage_c(q):
                    dve.wait_ge(S["inv_in"], q + 1)
                    dve.wait_ge(S["gated"], q + 1)
                    dst = mixed[:, q, :] if q % 2 == 0 else mixed[:, q, ::-1]
                    dve.tensor_tensor(dst, ex[:, q % NX, E2S, :], ex[:, q % NX, E1S, :], ALU.mult)\
                        .then_inc(S["mixed"], 1)

                def add_out(b):
                    for h in range(HALVES):
                        c = HALVES * b + h
                        dve.wait_ge(S["out_done"], c + 1)
                        dst = xT[:, b, h * CH:(h + 1) * CH]
                        dve.tensor_tensor(dst, dst, ps[c][:, :], ALU.add).then_inc(r_x, 1)

                take_keys(0)
                dve.wait_ge(S["decay_exp"], 1)
                dve.tensor_scalar(decay[:, :], decay[:, :], -1.0, None, ALU.mult).then_inc(S["decay_in"], 1)
                dve.memset(mx[:, :, 0:1], -1e38).then_inc(S["decay_in"], 1)
                dve.memset(num[:, :, 0:1], 0.0).then_inc(S["decay_in"], 1)
                dve.memset(den[:, :, 0:1], 0.0).then_inc(S["decay_in"], 1)
                dve.wait_ge(S["decay_in"], 4)
                for q in range(NSEQ + 2):
                    if q < NSEQ:
                        stage_a(q)
                    if q + 1 < NSEQ:
                        take_keys(q + 1)
                    if q >= 2:
                        stage_c(q - 2)
                    if 1 <= q <= NSEQ:
                        stage_b(q - 1)
                    if q == NSEQ:
                        add_out(0)
                add_out(1)

            @block.gpsimd
            def _(pool):
                def keep(q):
                    pool.wait_ge(S["max_scanned"], q + 1)
                    if q >= NX:
                        pool.wait_ge(S["mixed"], q - NX + 1)
                    pool.tensor_tensor(ex[:, q % NX, E2S, :], rkv[:, K, q, :], mx[:, q % 2, 1:1 + N],
                                       ALU.subtract).then_inc(S["kept"], 1)

                def weigh_values(q):
                    pool.wait_ge(S["weights_in"], 4 * q + 4)
                    pool.wait_ge(S["rest_in"], by_act.index((V, q, HALVES - 1)) + 1)
                    if q >= 2:
                        pool.wait_ge(S["top_in"], q - 1)
                    for e, at in ((E2S, 0), (E2, 1)):
                        pool.tensor_tensor(ev[:, q % 2, at, :], ex[:, q % NX, e, :], rkv[:, V, q, :], ALU.mult)\
                            .then_inc(S["values_in"], 1)

                def gate(q):
                    pool.wait_ge(S["top_in"], q + 1)
                    pool.wait_ge(S["rest_in"], by_act.index((R, q, HALVES - 1)) + 1)
                    top = ex[:, q % NX, E2S, :]
                    pool.tensor_tensor(top, top, rkv[:, R, q, :], ALU.mult).then_inc(S["gated"], 1)

                for q in range(NSEQ + 2):
                    if q < NSEQ:
                        keep(q)
                    if q >= 2:
                        gate(q - 2)
                    if q < NSEQ:
                        weigh_values(q)


_NAMES = {
    "x": "L0_attn_a_hidden_states", "a_wq": "L0_attn_a_Wq", "a_wk": "L0_attn_a_Wk", "a_wv": "L0_attn_a_Wv",
    "a_wo": "L0_attn_a_Wo", "wqkv": "L0_ffn_wqkv", "q_scale": "L0_ffn_q_scale", "k_scale": "L0_ffn_k_scale",
    "wo": "L0_ffn_wo", "w1": "L0_ffn_w1", "w2": "L0_ffn_w2",
}


def _columns(inputs):
    cols = np.zeros((P, COLS), np.float32)
    for at, name in ((COL_LN_G, "L0_ffn_ln_g"), (COL_LN_B, "L0_ffn_ln_b"), (COL_B2, "L0_ffn_b2")):
        cols[:, at:at + DEPTH] = np.asarray(inputs[name]).T
    b1 = np.asarray(inputs["L0_ffn_b1"]).reshape(DEPTH, 2, HID)
    for l in range(DEPTH):
        for k in range(2):
            for c, (c0, m) in enumerate(HC):
                cols[:m, COL_B1 + (l * 2 + k) * len(HC) + c] = b1[l, k, c0:c0 + m]
    for n, name in enumerate(("time_decay", "time_first", "time_decay_rev", "time_first_rev")):
        cols[:, COL_R + n] = np.asarray(inputs["L0_attn_b_" + name])
    return cols


def kernel(**inputs):
    import concourse.bacc as bacc
    from concourse.bass_utils import run_bass_kernel_spmd

    nc = bacc.Bacc("TRN2", target_bir_lowering=False, num_devices=1)
    arrays = {k: np.ascontiguousarray(inputs[v]) for k, v in _NAMES.items()}
    arrays["cols"] = _columns(inputs)
    arrays["r_w"] = np.ascontiguousarray(np.asarray(inputs["L0_attn_b_rkv_w"]).T)
    arrays["r_out"] = np.ascontiguousarray(np.asarray(inputs["L0_attn_b_out_w"]).T)
    arrays.update(zip(("square", "mask", "identB", "rot"), shape_constants()))
    t_in = {k: nc.dram_tensor(f"in_{k}", a.shape, mybir.dt.from_np(a.dtype), kind="ExternalInput").ap()
            for k, a in arrays.items()}
    out = nc.dram_tensor("out", (B, N, D), F32, kind="ExternalOutput").ap()
    build(nc, t_in, out)
    r = run_bass_kernel_spmd(nc, [{f"in_{k}": a for k, a in arrays.items()}], core_ids=[0])
    return r.results[0]["out"]
```

```python
import math
from contextlib import ExitStack

import numpy as np

import concourse.bass as bass
from concourse import mybir

B, N, D = 2, 1024, 128
P = 128
NT = N // P
TOK = B * N
CH = 512
NCH = TOK // CH
LN_EPS = 1e-5

AH, AF, AV = 16, 16, 64
HG = 4
NHG = AH // HG
PAIRS = [(0, 0), (0, 1), (0, 2), (1, 0), (1, 1), (2, 0)]
KROWS = AF * len(PAIRS)
UNITS = [(j, i) for j in range(NT) for i in range(j + 1)]
NU = len(UNITS)

DEPTH, HEADS, DH, WIN = 2, 8, 64, 64
INNER = HEADS * DH
HID = int(D * 4 * 2 / 3)
HC = [(c * P, min(P, HID - c * P)) for c in range(-(-HID // P))]
NG = DEPTH * NT
QK_SCALE = 8.0
NEG = -1e30
SS_SHIFT = 65536.0

F32 = mybir.dt.float32
BF16 = mybir.dt.bfloat16
ALU = mybir.AluOpType
ACT = mybir.ActivationFunctionType
AX = mybir.AxisListType
COL_LN_G, COL_LN_B, COL_B2, COL_B1 = 0, DEPTH, 2 * DEPTH, 3 * DEPTH
COL_R = COL_B1 + DEPTH * 2 * len(HC)
COLS = COL_R + 4
GELU_SET = "gelu_and_others"
EXP_SET = "natural_log_exp_and_others"


def shape_constants():
    ident = np.eye(P, dtype=np.float32)
    mean = np.full((P, P), 1.0 / D, np.float32)
    ones = np.ones((P, P), np.float32)
    m, n = np.arange(P)[:, None], np.arange(P)[None, :]
    causal = (m <= n).astype(np.float32)
    square = np.stack([ident, ident - mean, mean, ones, causal], axis=1)
    q, k = np.arange(WIN)[:, None], np.arange(WIN)[None, :]
    own = np.where(k <= q, 0.0, NEG)
    prev = np.where(k >= q, 0.0, NEG)
    none = np.full((WIN, WIN), NEG)
    mask = np.zeros((P, NT, P), np.float32)
    for t in range(NT):
        mask[:WIN, t] = np.concatenate([own, prev if t else none], axis=1)
        mask[WIN:, t] = np.concatenate([prev, own], axis=1)
    half = np.arange(0, DH, 2, dtype=np.float32)
    inv_freq = (1.0 / np.float32(10000.0) ** (half / np.float32(DH))).astype(np.float32)
    t = np.arange(N, dtype=np.float32)
    freqs = (t[:, None] * inv_freq[None, :]).astype(np.float32)
    freqs = np.concatenate([freqs, freqs], axis=-1).astype(np.float64)
    base = ((half + 0.4 * DH) / (1.4 * DH)).astype(np.float32)
    power = ((t - N // 2) / float(WIN // 2)).astype(np.float32)
    scale = base[None, :].astype(np.float64) ** power[:, None].astype(np.float64)
    scale = np.concatenate([scale, scale], axis=-1)
    sign = np.where(np.arange(DH) < DH // 2, -1.0, 1.0)
    cos, sin = np.cos(freqs), np.sin(freqs) * sign
    rot = np.stack([cos * scale * QK_SCALE, cos / scale, sin * scale * QK_SCALE, sin / scale])
    rot = rot.reshape(4, NT, P, DH).transpose(2, 0, 1, 3).astype(np.float32)
    return (np.ascontiguousarray(square), np.ascontiguousarray(mask.astype(mybir.dt.np(BF16))),
            ident.astype(mybir.dt.np(BF16)), np.ascontiguousarray(rot))


def build(nc, t_in, out):
    nc.disable_value_cache = True
    ctx = ExitStack()
    with ctx:
        def sem(name):
            return ctx.enter_context(nc.semaphore(name))

        def at_least(eng, s, value):
            if isinstance(value, int) and value <= 0:
                return
            eng.wait_ge(s, value)

        ps = [ctx.enter_context(nc.psum_tensor(f"bank{i}", [P, CH], F32)) for i in range(8)]

        def sb(name, shape, dt=F32, stack=None):
            return (stack or ctx).enter_context(nc.sbuf_tensor(name, shape, dt))

        xT = sb("xT", [P, B, N])
        y0 = sb("y0", [P, B, 1 + N])
        square = sb("square", [P, 5, P])
        identB = sb("identB", [P, P], BF16)
        ident, centre, mean, ones, causal = (square[:, k, :] for k in range(5))
        cols = sb("cols", [P, COLS])
        eps_col = sb("eps_col", [P, 3])
        ln_sqr = sb("ln_sqr", [P, 2, CH])
        ln_inv = sb("ln_inv", [P, 2, CH])

        wqkv = sb("wqkv", [P, DEPTH, 3 * INNER])
        mask = sb("mask", [P, NT, P], BF16)
        rot = sb("rot", [P, DEPTH, 4, NT, DH])
        gains = sb("gains", [P, 2, DEPTH, DH])

        dram = nc.dram_tensor("parts_dram", [2, 3, AH * AF, TOK], BF16, kind="Internal").ap()

        ld_x, ld_const = sem("ld_x"), sem("ld_const")
        ld_tab, ld_qkv, tab_done = sem("ld_tab"), sem("ld_qkv"), sem("tab_done")
        set_up, x_turned, x_in = sem("set_up"), sem("x_turned"), sem("x_in")
        ln_added, ln_centred, ln_squared = sem("ln_added"), sem("ln_centred"), sem("ln_squared")
        ln_var, ln_logged, ln_scaled, ln_done = (sem("ln_var"), sem("ln_logged"), sem("ln_scaled"),
                                                 sem("ln_done"))
        st = sem("stored")

        def y0_chunk(c):
            b, h = divmod(c * CH, N)
            return y0[:, b, 1 + h:1 + h + CH]

        def x_chunk(c):
            b, h = divmod(c * CH, N)
            return xT[:, b, h:h + CH]

        def ln_tensor(pe, n):
            base = NCH * n

            def variance(c):
                pe.wait_ge(ln_squared, base + c + 1)
                pe.matmul(ps[c][:, :], mean, ln_sqr[:, c % 2, :], start=True, stop=True).then_inc(ln_var, 1)

            for c in range(NCH):
                x_ready[n](pe, c)
                pe.matmul(ps[4 + c][:, :], centre, x_chunk(c), start=True, stop=True).then_inc(ln_centred, 1)
                if c >= 1:
                    variance(c - 1)
            variance(NCH - 1)

        def ln_scalar(act, n):
            base = NCH * n
            act.preload_act_table_set(EXP_SET)

            def inverse(c):
                act.wait_ge(ln_var, base + c + 1)
                if c >= 2:
                    act.wait_ge(ln_done, base + c - 1)
                act.activation(ln_inv[:, c % 2, :], ps[c][:, :], ACT.Ln, bias=eps_col[:, 0:1])\
                    .then_inc(ln_logged, 1)
                act.wait_ge(ln_logged, base + c + 1)
                act.activation(ln_inv[:, c % 2, :], ln_inv[:, c % 2, :], ACT.Exp, scale=-0.5)\
                    .then_inc(ln_scaled, 1)

            for c in range(NCH):
                act.wait_ge(ln_centred, base + c + 1)
                if c >= 2:
                    act.wait_ge(ln_var, base + c - 1)
                act.activation(ln_sqr[:, c % 2, :], ps[4 + c][:, :], ACT.Square).then_inc(ln_squared, 1)
                if c >= 1:
                    inverse(c - 1)
            inverse(NCH - 1)

        def ln_vector(dve, n):
            if n == 2:
                add_stream(dve)
            for c in range(NCH):
                dve.wait_ge(ln_scaled, NCH * n + c + 1)
                dve.tensor_tensor(y0_chunk(c), ps[4 + c][:, :], ln_inv[:, c % 2, :], ALU.mult)\
                    .then_inc(ln_done, 1)
            dve.wait_ge(ln_done, NCH * (n + 1))

        def normalise(n, eng):
            {nc.tensor: ln_tensor, nc.scalar: ln_scalar, nc.vector: ln_vector}[eng](eng, n)

        def add_stream(dve):
            for c in range(NCH):
                dve.tensor_tensor(x_chunk(c), x_chunk(c), y0_chunk(c), ALU.add).then_inc(ln_added, 1)

        y_done = sem("y_done")
        a_x = sem("a_x")
        r_x = sem("r_x")
        x_ready = [lambda e, c: e.wait_ge(x_in, c + 1),
                   lambda e, c: e.wait_ge(a_x, 2 * B * NHG + 2),
                   lambda e, c: e.wait_ge(ln_added, c + 1),
                   lambda e, c: e.wait_ge(r_x, c + 1)]

        def load_first(sp):
            for c in range(NCH):
                sp.dma_start(x_tok[:, 4 * c:4 * c + 4, :],
                             t_in["x"].rearrange("b (t p) d -> p (b t) d", p=P)[:, 4 * c:4 * c + 4, :])\
                    .then_inc(ld_x, 16)
                if c == 0:
                    sp.dma_start(square[:, :, :], t_in["square"]).then_inc(ld_const, 16)
                    sp.dma_start(identB[:, :], t_in["identB"]).then_inc(ld_const, 16)
                    sp.dma_start(cols[:, :], t_in["cols"]).then_inc(ld_const, 16)

        def load_tables(sp):
            sp.dma_start(rot[:, 0], t_in["rot"]).then_inc(ld_tab, 16)
            sp.dma_start(rot[:, 1], t_in["rot"]).then_inc(ld_tab, 16)
            sp.dma_start(mask[:, :, :], t_in["mask"]).then_inc(ld_tab, 16)
            for l in range(DEPTH):
                for k, name in enumerate(("q_scale", "k_scale")):
                    sp.dma_start(gains[:, k, l, :], t_in[name][l:l + 1, :].to_broadcast([P, DH]))\
                        .then_inc(ld_tab, 16)
            sp.dma_start(wqkv[:, :, :], t_in["wqkv"].rearrange("l p n -> p l n")).then_inc(ld_qkv, 16)

        def set_constants(pool):
            pool.memset(eps_col[:, 0:1], LN_EPS).then_inc(set_up, 1)
            pool.memset(eps_col[:, 1:2], 0.5 * math.log(SS_SHIFT)).then_inc(set_up, 1)
            pool.memset(eps_col[:, 2:3], 1.0).then_inc(set_up, 1)
            pool.memset(y0[:, :, 0:1], 0.0).then_inc(set_up, 1)

        def scale_tables(pool):
            pool.wait_ge(ld_tab, 16 * (3 + 2 * DEPTH))
            HF = DH // 2
            for l in range(DEPTH):
                for k in range(2):
                    for i, lo, hi, g0 in ((k, 0, DH, 0), (2 + k, 0, HF, HF), (2 + k, HF, DH, 0)):
                        t_ = rot[:, l, i, :, lo:hi]
                        pool.tensor_tensor(t_, t_, gains[:, k, l, g0:g0 + hi - lo].unsqueeze(1)
                                           .to_broadcast([P, NT, hi - lo]), ALU.mult).then_inc(tab_done, 1)

        def turn_input(pe):
            pe.wait_ge(ld_const, 48)
            pe.wait_ge(ld_x, 16 * NCH)
            for c in range(NCH):
                for k in range(4):
                    last = pe.transpose(ps[c][:, k * P:(k + 1) * P], x_tok[:, 4 * c + k, :], ident)
                last.then_inc(x_turned, 1)

        def copy_input(act):
            act.wait_ge(set_up, 4)
            for c in range(NCH):
                act.wait_ge(x_turned, c + 1)
                act.copy(x_chunk(c), ps[c][:, :]).then_inc(x_in, 1)

        with ExitStack() as s0:
            x_tok = sb("x_tok", [P, TOK // P, D], stack=s0)
        start = dict(load_first=load_first, load_tables=load_tables, set_constants=set_constants,
                     scale_tables=scale_tables, turn_input=turn_input, copy_input=copy_input)
        linear_attention(nc, t_in, sb, sem, ps, dram, xT, y0, ident, ones, causal, eps_col,
                         a_x, at_least, y0_chunk, ln_done, lambda eng: normalise(0, eng), start)

        F = ffn_sems(sem)

        def run_ffn(call, n):
            ffn(nc, t_in, sb, ps, F, call, y0, y_done, ident, centre, mean, identB, eps_col, cols, at_least,
                wqkv, mask, rot, ld_tab, ld_qkv, tab_done,
                lambda eng: normalise(n, eng))

        run_ffn(0, 1)
        rwkv(nc, t_in, sb, sem, ps, xT, y0, cols, r_x,
             lambda eng: normalise(2, eng), lambda eng, c: eng.wait_ge(ln_done, 2 * NCH + c + 1))
        run_ffn(1, 3)
        store_out(nc, sb, sem, ps, out, xT, ident, st, add_stream,
                  lambda e, c: e.wait_ge(ln_added, NCH + c + 1))


def store_out(nc, sb, sem, ps, out, xT, ident, st, add_stream, x_ready):
    turned, copied = sem("out_turned"), sem("out_copied")
    with ExitStack() as stack:
        o_tok = sb("o_tok", [P, TOK // P, D], stack=stack)
        with nc.Block() as block:
            @block.tensor
            def _(pe):
                for c in range(NCH):
                    x_ready(pe, c)
                    for k in range(4):
                        b, t = divmod(4 * c + k, NT)
                        last = pe.transpose(ps[c][:, k * P:(k + 1) * P], xT[:, b, t * P:(t + 1) * P], ident)
                    last.then_inc(turned, 1)

            @block.scalar
            def _(act):
                for c in range(0, NCH, 2):
                    act.wait_ge(turned, c + 1)
                    act.copy(o_tok[:, 4 * c:4 * c + 4, :], ps[c][:, :]).then_inc(copied, 1)

            copied2 = sem("out_copied2")

            @block.vector
            def _(dve):
                add_stream(dve)
                for c in range(1, NCH, 2):
                    dve.wait_ge(turned, c + 1)
                    dve.tensor_copy(o_tok[:, 4 * c:4 * c + 4, :], ps[c][:, :]).then_inc(copied2, 1)

            @block.sync
            def _(sp):
                for c in range(NCH):
                    sp.wait_ge((copied, copied2)[c % 2], c // 2 + 1)
                    sp.dma_start(out.rearrange("b (t p) d -> p (b t) d", p=P)[:, 4 * c:4 * c + 4, :],
                                 o_tok[:, 4 * c:4 * c + 4, :]).then_inc(st, 16)
                sp.wait_ge(st, 16 * NCH)


def linear_attention(nc, t_in, sb, sem, ps, parts, xT, y0, ident, ones, causal, eps_col,
                     a_x, at_least, y0_chunk, ln_done, normalise, start):
    NV = AV + 1
    NS, NA = 3, 4
    ld_w, ld_wo = sem("a_ld_w"), sem("a_ld_wo")
    proj, p1_done, r1_done, p2_done, p3_done = (sem("a_proj"), sem("a_p1_done"), sem("a_r1_done"),
                                                sem("a_p2_done"), sem("a_p3_done"))
    parts_out = [sem("a_parts_out_0"), sem("a_parts_out_1")]
    stacked, v_copied = sem("a_stacked"), sem("a_v_copied")
    v_proj, v_by_act, v_by_dve, v_ones = sem("a_v_proj"), sem("a_v_by_act"), sem("a_v_by_dve"), sem("a_v_ones")
    scored, squared, weighed, diagonal = sem("a_scored"), sem("a_squared"), sem("a_weighed"), sem("a_diagonal")
    prefixed, prefix_used = sem("a_prefixed"), sem("a_prefix_used")
    z_in, z_inv, y_out = sem("a_z_in"), sem("a_z_inv"), sem("a_y_out")
    y_turned, y_copied, heads_out = sem("a_y_turned"), sem("a_y_copied"), sem("a_heads_out")
    NIT = B * NHG
    with ExitStack() as stack:
        def s(name, shape, dt=F32):
            return sb(name, shape, dt, stack)
        v_now = s("v_now", [P, 2, NT, HG, NV])
        values = s("values", [P, B * NT, AH, NV])
        q_stack = s("q_stack", [P, 2, HG, N], BF16)
        k_stack = s("k_stack", [P, 2, HG, N], BF16)

        def gather(sp, it):
            b, hg, side = it // NHG, it % NHG, it % 2
            if not isinstance(it, int):
                b, hg, side = sp.snap(b), sp.snap(hg), sp.snap(side)
            for qk, st_ in enumerate((q_stack, k_stack)):
                for r, pair in enumerate(PAIRS):
                    src = parts[qk, pair[qk], bass.ds(hg * (HG * AF), HG * AF), bass.ds(b * N, N)]
                    sp.dma_start(st_[r * AF:(r + 1) * AF, bass.ds(side, 1), :, :],
                                 src.rearrange("(h f) n -> f h n", h=HG)).then_inc(stacked, 16)

        def copy_values_of(pool, step, side):
            b, hg = step // NHG, step % NHG
            pool.tensor_copy(v_now[:, side], values[:, bass.ds(b * NT, NT), bass.ds(hg * HG, HG), :])\
                .then_inc(v_copied, 1)

        wv = s("wv", [P, AH * AV])
        late_by = ["act", "dve", "act", "dve"]
        LATE = len(late_by)
        v_late = {eng: sem("a_v_late_" + eng) for eng in sorted(set(late_by))}

        def take_late(eng, name):
            for n, by in enumerate(late_by):
                if by == name:
                    take_values(eng, 2 * B * NT - LATE + n, ps[3 + n][:, :], v_late[name])

        def project_values(pe, v, bank):
            b, j = divmod(v // 2, NT)
            pe.matmul(bank, y0[:, b, 1 + j * P:1 + (j + 1) * P], wv[:, (v % 2) * CH:(v % 2 + 1) * CH],
                      start=True, stop=True).then_inc(v_proj, 1)

        def take_values(eng, v, bank, done):
            eng.wait_ge(v_proj, v + 1)
            copy = eng.copy if eng is nc.scalar else eng.tensor_copy
            copy(values[:, v // 2, 8 * (v % 2):8 * (v % 2) + 8, 0:AV],
                 bank.rearrange("p (h e) -> p h e", h=8)).then_inc(done, 1)

        with ExitStack() as early:
            wqk = sb("wqk", [P, 2, AH * AF], F32, early)
            part = sb("part", [P, 4, 3, 2, CH], BF16, early)
            rest = sb("rest", [P, 2, CH], F32, early)
            NQK, NVU = 4 * NCH, 2 * B * NT - LATE

            with nc.Block() as block:
                @block.sync
                def _(sp):
                    def put_out(c):
                        sp.wait_ge(p3_done, 4 * (c + 1))
                        for g in range(4):
                            sp.dma_start(parts[g // 2, :, (g % 2) * P:(g % 2 + 1) * P, c * CH:(c + 1) * CH]
                                         .rearrange("a p n -> p a n"), part[:, g, :, c % 2, :])\
                                .then_inc(parts_out[c % 2], 16)

                    start["load_first"](sp)
                    sp.dma_start(wqk[:, 0, :], t_in["a_wq"]).then_inc(ld_w, 16)
                    sp.dma_start(wqk[:, 1, :], t_in["a_wk"]).then_inc(ld_w, 16)
                    sp.dma_start(wv[:, :], t_in["a_wv"]).then_inc(ld_w, 16)
                    put_out(0)
                    put_out(1)
                    sp.wait_ge(parts_out[0], 64)
                    sp.wait_ge(parts_out[1], 64)
                    gather(sp, 0)
                    put_out(2)
                    put_out(3)
                    sp.wait_ge(parts_out[0], 128)
                    sp.wait_ge(parts_out[1], 128)

                @block.gpsimd
                def _(pool):
                    start["set_constants"](pool)
                    pool.memset(values[:, :, :, AV:NV], 1.0).then_inc(v_ones, 1)
                    pool.wait_ge(v_ones, 1)
                    pool.wait_ge(v_by_act, NT)
                    pool.wait_ge(v_by_dve, NT)
                    copy_values_of(pool, 0, 0)

                @block.tensor
                def _(pe):
                    start["turn_input"](pe)
                    normalise(pe)
                    pe.wait_ge(ld_w, 48)
                    pe.wait_ge(ln_done, NCH)

                    def values_of(v):
                        at_least(pe, (v_by_act, v_by_dve)[v % 2], v // 2 - 1)
                        project_values(pe, v, ps[4 + v % 4][:, :])

                    for u in range(NQK):
                        c, g = divmod(u, 4)
                        at_least(pe, r1_done, u - 3)
                        pe.matmul(ps[u % 4][:, :], wqk[:, g // 2, (g % 2) * P:(g % 2 + 1) * P], y0_chunk(c),
                                  start=True, stop=True).then_inc(proj, 1)
                        values_of(u)
                    for v in range(NQK, NVU):
                        values_of(v)

                @block.scalar
                def _(act):
                    def second(u):
                        act.wait_ge(r1_done, u + 1)
                        act.copy(part[:, u % 4, 1, (u // 4) % 2, :], rest[:, u % 2, :]).then_inc(p2_done, 1)

                    start["copy_input"](act)
                    normalise(act)
                    for u in range(NQK):
                        act.wait_ge(proj, u + 1)
                        if u // 4 >= 2:
                            act.wait_ge(parts_out[(u // 4) % 2], 64)
                        act.copy(part[:, u % 4, 0, (u // 4) % 2, :], ps[u % 4][:, :]).then_inc(p1_done, 1)
                        if u >= 1:
                            second(u - 1)
                        if u % 2 == 0:
                            take_values(act, u, ps[4 + u % 4][:, :], v_by_act)
                    second(NQK - 1)
                    for v in range(NQK, NVU, 2):
                        take_values(act, v, ps[4 + v % 4][:, :], v_by_act)

                @block.vector
                def _(dve):
                    def third(u):
                        dve.wait_ge(p2_done, u + 1)
                        dve.tensor_tensor(part[:, u % 4, 2, (u // 4) % 2, :], rest[:, u % 2, :],
                                          part[:, u % 4, 1, (u // 4) % 2, :], ALU.subtract).then_inc(p3_done, 1)

                    normalise(dve)
                    for u in range(NQK):
                        dve.wait_ge(p1_done, u + 1)
                        at_least(dve, p3_done, u - 1)
                        dve.tensor_tensor(rest[:, u % 2, :], ps[u % 4][:, :], part[:, u % 4, 0, (u // 4) % 2, :],
                                          ALU.subtract).then_inc(r1_done, 1)
                        if u >= 1:
                            third(u - 1)
                        if u % 2:
                            take_values(dve, u, ps[4 + u % 4][:, :], v_by_dve)
                    third(NQK - 1)
                    for v in range(NQK + 1, NVU, 2):
                        take_values(dve, v, ps[4 + v % 4][:, :], v_by_dve)

        v_prefix = s("v_prefix", [P, 2, HG, NV])
        wo_slot = s("wo_slot", [P, 2, D])
        sq = s("sq", [P, NA, HG, P])
        sq_diag = s("sq_diag", [P, 2, HG, P])
        z_sum = s("z_sum", [P, 2, HG])
        z_rec = s("z_rec", [P, 2, HG])
        y_tok = s("y_tok", [P, 2, HG * AV])
        y_feat = s("y_feat", [P, 2, N])
        score_bank = ps[0:NS]
        y_bank = ps[3:5]
        turn_bank = ps[5]
        out_bank = ps[6:8]
        with nc.Block() as block:
            @block.sync
            def _(sp):
                def load_wo(it):
                    sp.wait_ge(stacked, (it + 1) * (16 * 2 * len(PAIRS)))
                    sp.wait_ge(heads_out, it * 2 + 4)
                    hg = it % NHG if isinstance(it, int) else sp.snap(it % NHG)
                    sp.dma_start(wo_slot[:, :, :], t_in["a_wo"][bass.ds(hg * (2 * P), 2 * P), :]
                                 .rearrange("(c p) n -> p c n", p=P)).then_inc(ld_wo, 16)

                load_wo(0)
                start["load_tables"](sp)
                with sp.Fori(1, NIT) as it:
                    sp.wait_ge(heads_out, it * 2 + 2)
                    gather(sp, it)
                    load_wo(it)

            @block.gpsimd
            def _(pool):
                def prefix_sums(step, side):
                    uses = step * (NT - 2)
                    if not isinstance(step, int):
                        uses = pool.snap(uses)
                    pool.wait_ge(v_copied, step + 1)
                    for j in range(1, NT - 1):
                        pool.wait_ge(prefix_used, uses + j)
                        before = v_now[:, side, 0]
                        if j > 1:
                            before = v_prefix[:, (j - 1) % 2]
                            pool.wait_ge(prefixed, uses + j - 1)
                        pool.tensor_tensor(v_prefix[:, j % 2], before, v_now[:, side, j], ALU.add)\
                            .then_inc(prefixed, 1)

                def next_values(step, side):
                    pool.wait_ge(heads_out, step * 2 + 2)
                    copy_values_of(pool, step, side)

                prefix_sums(0, 0)
                next_values(1, 1)
                prefix_sums(1, 1)
                with pool.Fori(1, NIT // 2) as pair:
                    for side in range(2):
                        step = pair * 2 + side
                        next_values(step, side)
                        prefix_sums(step, side)
                start["scale_tables"](pool)

            @block.tensor
            def _(pe):
                pe.sem_inc(heads_out, 4)
                pe.sem_inc(weighed, NA)
                pe.sem_inc(prefix_used, 2)
                pe.sem_inc(y_turned, 2)

                def known(value):
                    return value if isinstance(value, int) else pe.snap(value)

                def scores(step, units, side, k):
                    j, i = UNITS[k]
                    if k == 0:
                        pe.wait_ge(stacked, (step + 1) * (16 * 2 * len(PAIRS)))
                    pe.wait_ge(squared, units + k + 1)
                    for h in range(HG):
                        last = pe.matmul(score_bank[k % NS][:, h * P:(h + 1) * P],
                                         k_stack[0:KROWS, side, h, i * P:(i + 1) * P],
                                         q_stack[0:KROWS, side, h, j * P:(j + 1) * P],
                                         start=True, stop=True, skip_group_check=True)
                    last.then_inc(scored, 1)

                def attend(step, side, last_step):
                    units, tiles, uses = (known(step * c) for c in (NU, NT, NT - 2))

                    def turn(j):
                        pe.wait_ge(y_out, tiles + j + 1 + 2)
                        pe.wait_ge(y_copied, tiles + j + 1)
                        for c in range(2):
                            last = pe.transpose(turn_bank[:, (j % 2) * 256 + c * P:(j % 2) * 256 + (c + 1) * P],
                                                y_tok[:, j % 2, c * P:(c + 1) * P], ident)
                        last.then_inc(y_turned, 1)

                    def output(half, c):
                        pe.wait_ge(y_copied, tiles + (half + 1) * (NT // 2) + 2)
                        pe.wait_ge(a_x, step * 2 + half + 1)
                        last = pe.matmul(out_bank[half][:, :], wo_slot[:, c, :],
                                         y_feat[:, c, half * CH:(half + 1) * CH], start=(c == 0), stop=(c == 1))
                        if c == 1:
                            last.then_inc(heads_out, 1)

                    pe.wait_ge(v_copied, step + 1)
                    for k, (j, i) in enumerate(UNITS):
                        if i == 0:
                            pe.wait_ge(y_out, tiles + j + 1)
                            if j == 1:
                                pe.matmul(y_bank[1][:, 0:HG * NV], ones, v_now[:, side, 0],
                                          start=True, stop=False, skip_group_check=True)
                            elif j:
                                pe.wait_ge(prefixed, uses + j - 1)
                                pe.matmul(y_bank[j % 2][:, 0:HG * NV], ones, v_prefix[:, (j - 1) % 2],
                                          start=True, stop=False, skip_group_check=True).then_inc(prefix_used, 1)
                        if k + NS < NU:
                            scores(step, units, side, k + NS)
                        elif not last_step:
                            scores(step + 1, units + NU, 1 - side, k + NS - NU)
                        if i == j:
                            pe.wait_ge(diagonal, tiles + j + 1)
                        else:
                            pe.wait_ge(squared, units + k + 1 + NS)
                        a = sq_diag[:, j % 2] if i == j else sq[:, k % NA]
                        for h in range(HG):
                            last = pe.matmul(y_bank[j % 2][:, h * NV:(h + 1) * NV], a[:, h, :],
                                             v_now[:, side, i, h, :],
                                             start=(j == 0 and h == 0), stop=(i == j), skip_group_check=True)
                        last.then_inc(weighed, 1)
                        if j >= 1 and i == 1:
                            turn(j - 1)
                    pe.wait_ge(ld_wo, (step + 1) * 16)
                    output(0, 0)
                    turn(NT - 1)
                    output(0, 1)
                    output(1, 0)
                    output(1, 1)

                for n in range(LATE):
                    if n == 3:
                        for k in range(NS):
                            scores(0, 0, 0, k)
                    project_values(pe, 2 * B * NT - LATE + n, ps[3 + n][:, :])
                for name in sorted(v_late):
                    pe.wait_ge(v_late[name], late_by.count(name))
                with pe.Fori(0, NIT // 2 - 1) as pair:
                    for side in range(2):
                        attend(pe.snap(pair * 2 + side), side, False)
                attend(NIT - 2, 0, False)
                attend(NIT - 1, 1, True)

            @block.scalar
            def _(act):
                act.sem_inc(squared, NS)
                act.sem_inc(y_copied, 2)
                take_late(act, "act")
                with act.Fori(0, NIT) as it:
                    units, tiles, outs = act.snap(it * NU), act.snap(it * NT), act.snap(it * 2)
                    def copy_turned(j):
                        act.wait_ge(y_turned, tiles + j + 1 + 2)
                        act.wait_ge(heads_out, outs + 4)
                        act.copy(y_feat[:, :, j * P:(j + 1) * P],
                                 turn_bank[:, (j % 2) * 256:(j % 2) * 256 + 256]
                                 .rearrange("p (c n) -> p c n", c=2)).then_inc(y_copied, 1)
                    for k, (j, i) in enumerate(UNITS):
                        act.wait_ge(scored, units + k + 1)
                        act.wait_ge(weighed, units + k + 1)
                        act.activation(sq[:, k % NA], score_bank[k % NS][:, :].rearrange("p (h n) -> p h n", h=HG),
                                       ACT.Square, bias=eps_col[:, 2:3], scale=0.25).then_inc(squared, 1)
                        if j >= 1 and i == min(2, j) and not (j == 1):
                            copy_turned(j - 1)
                        if j == 2 and i == 0:
                            copy_turned(0)
                    copy_turned(NT - 1)

            @block.vector
            def _(dve):
                dve.sem_inc(y_out, 2)
                dve.sem_inc(a_x, 2)

                def known(value):
                    return value if isinstance(value, int) else dve.snap(value)

                def add_heads(it, half):
                    dve.wait_ge(heads_out, it * 2 + half + 1 + 4)
                    dst = xT[:, bass.ds(known(it // NHG), 1), half * CH:(half + 1) * CH]
                    dve.tensor_tensor(dst, dst, out_bank[half][:, :], ALU.add).then_inc(a_x, 1)

                def normalise_step(it, first):
                    units, tiles = known(it * NU), known(it * NT)
                    for j in range(NT):
                        k = UNITS.index((j, j))
                        dve.wait_ge(squared, units + k + 1 + NS)
                        dve.scalar_tensor_tensor(sq_diag[:, j % 2], sq[:, k % NA], 1.0,
                                                 causal.unsqueeze(1).to_broadcast([P, HG, P]),
                                                 ALU.add, ALU.mult).then_inc(diagonal, 1)
                        dve.wait_ge(weighed, units + k + 1 + NA)
                        yb = y_bank[j % 2][:, 0:HG * NV].rearrange("p (h e) -> p h e", h=HG)
                        dve.tensor_scalar(z_sum[:, j % 2], yb[:, :, AV], 2e-12, None, ALU.add).then_inc(z_in, 1)
                        dve.wait_ge(z_in, tiles + j + 1)
                        dve.reciprocal(z_rec[:, j % 2], z_sum[:, j % 2]).then_inc(z_inv, 1)
                        dve.wait_ge(z_inv, tiles + j + 1)
                        dve.wait_ge(y_turned, tiles + j + 1)
                        dve.tensor_tensor(y_tok[:, j % 2].rearrange("p (h e) -> p h e", h=HG), yb[:, :, 0:AV],
                                          z_rec[:, j % 2].unsqueeze(2).to_broadcast([P, HG, AV]), ALU.mult)\
                            .then_inc(y_out, 1)
                        if j == 1 and not first:
                            add_heads(known(it - 1), 1)
                    add_heads(it, 0)

                take_late(dve, "dve")
                normalise_step(0, True)
                with dve.Fori(1, NIT) as it:
                    normalise_step(it, False)
                add_heads(NIT - 1, 1)


def ffn_sems(sem):
    names = """ld_wo ld_w1 ld_w2 set_up h_in qkv_done qk_squared v_out v_mixed_0 v_mixed_1 ss_in ss_clipped ss_log
        qk_inv qk_rotated qk_summed qk_normed qk_turned q_out k_out sim_done max_done exp_done sum_inv p_normed
        p_turned p_out_lo p_out_hi pv_done o_out_0 o_out_1 wo_done mid_done h2_in centred squared var_done
        var_log var_inv normed affine hid_mm gelu_done hid_done w2_done""".split()
    return {n: sem("f_" + n) for n in names}


def ffn(nc, t_in, sb, ps, S, call, y0, y_done, ident, centre, mean, identB, eps_col, cols, at_least,
        wqkv, mask, rot, ld_tab, ld_qkv, tab_done, normalise):
    G0 = call * NG
    with ExitStack() as stack:
        def s(name, shape, dt=F32):
            return sb(f"{name}_{call}", shape, dt, stack)
        y1 = s("y1", [P, B, 1 + N])
        wo = s("wo", [P, INNER // P, D])
        w1 = s("w1", [P, 2 * HID])
        w2 = s("w2", [P, len(HC), D])
        h = s("h", [P, 2, B, P])
        qk_sq = s("qk_sq", [P, 2 * INNER])
        ss = s("ss", [P, B, 3, 2 * HEADS])
        qk_scale = s("qk_scale", [P, B, 2 * HEADS])
        rot_a = s("rot_a", [P, B, 2 * INNER])
        rot_b = s("rot_b", [P, B, 2 * INNER])
        v_nat = s("v_nat", [P, 2, B, INNER])
        v_mix = s("v_mix", [P, 2, B, INNER])
        qT = s("qT", [P, 2, B, HEADS // 2, P])
        kT = s("kT", [P, 2, B, HEADS // 2, P])
        neg_max = s("neg_max", [P, B, 2, HEADS // 2])
        prob = s("prob", [P, B, HEADS, P])
        p_sum = s("p_sum", [P, B, HEADS])
        p_inv = s("p_inv", [P, B, HEADS])
        probT = s("probT", [P, B, HEADS, P])
        oT = s("oT", [P, 2, HEADS // 2, B, P])
        h2 = s("h2", [P, B, P])
        c_sq = s("c_sq", [P, B * P])
        v_log = s("v_log", [P, B * P])
        v_inv = s("v_inv", [P, B * P])
        normed = s("normed", [P, B * P])
        hn = s("hn", [P, B * P])
        gel = s("gel", [P, len(HC), B * P])
        hid = s("hid", [P, len(HC), B * P])
        BP = B * P
        wqkv_flat = wqkv.rearrange("p l n -> p (l n)")
        rot_flat = rot.rearrange("p l i t d -> p (l i t d)")
        qk_bank = ps[0:2]
        v_bank = ps[2]
        sim_bank = ps[3:5]
        turn_bank = ps[5:7]
        m_bank = ps[7]
        hid_bank = [ps[2], *turn_bank]
        HORDER = (1, 2, 0)

        def slots(eng, stage):
            stage(0, 0, True, False, False, False)
            stage(1, 1, True, True, False, False)
            stage(2, 0, True, True, True, False)
            stage(3, 1, True, True, True, True)
            with eng.Fori(2, NG // 2) as pair:
                stage(eng.snap(pair * 2), 0, True, True, True, True)
                stage(eng.snap(pair * 2 + 1), 1, True, True, True, True)
            stage(NG, 0, False, True, True, True)
            stage(NG + 1, 1, False, False, True, True)
            stage(NG + 2, 0, False, False, False, True)

        def run(on, *calls):
            if on:
                for f, *args in calls:
                    f(*args)

        def known(eng, value):
            return value if isinstance(value, int) else eng.snap(value)

        def cap(value, most):
            return min(value, most) if isinstance(value, int) else value

        def w(eng, name, value):
            total = G0 * PER[name] + value
            at_least(eng, S[name], total)

        PER = dict(h_in=2, qkv_done=2, qk_squared=4, v_out=2, v_mixed_0=16, v_mixed_1=16, ss_in=2, ss_clipped=2, ss_log=2,
                   qk_inv=2, qk_rotated=2, qk_summed=2, qk_normed=2, qk_turned=4, q_out=2, k_out=2, sim_done=4,
                   max_done=4, exp_done=4, sum_inv=2, p_normed=2, p_turned=4, p_out_lo=2, p_out_hi=2, pv_done=2,
                   o_out_0=1, o_out_1=1, wo_done=1, mid_done=1, h2_in=2, centred=1, squared=1, var_done=1,
                   var_log=1, var_inv=1, normed=1, affine=1, hid_mm=3, gelu_done=3, hid_done=3, w2_done=1)

        def mixed(eng, g, par):
            if isinstance(g, int) and g < 0:
                return
            w(eng, f"v_mixed_{par}", g * 16 + (32 if par == 0 else 16))

        with nc.Block() as block:
            @block.sync
            def _(sp):
                def load_wo(l):
                    sp.dma_start(wo[:, :, :], t_in["wo"][l].rearrange("(c p) n -> p c n", p=P))\
                        .then_inc(S["ld_wo"], 16)

                def load_w1(l):
                    sp.dma_start(w1[:, :], t_in["w1"][l]).then_inc(S["ld_w1"], 16)

                def load_w2(l):
                    full = HID // P
                    sp.dma_start(w2[:, 0:full, :], t_in["w2"][l, 0:full * P, :]
                                 .rearrange("(c p) n -> p c n", p=P)).then_inc(S["ld_w2"], 16)
                    sp.dma_start(w2[0:HC[-1][1], full, :], t_in["w2"][l, full * P:HID, :]).then_inc(S["ld_w2"], 16)

                load_wo(0)
                load_w1(0)
                load_w2(0)

                def stage(g, par):
                    w(sp, "v_out", 2 * g + 2)
                    w(sp, "pv_done", 2 * g - 2)
                    for rows, src in ((slice(0, WIN), par), (slice(WIN, P), 1 - par)):
                        sp.dma_start(v_mix[rows, par], v_nat[rows, src]).then_inc(S[f"v_mixed_{par}"], 16)

                last = NT + 2
                for g in range(4):
                    stage(g, g % 2)
                with sp.Fori(2, last // 2) as pair:
                    stage(sp.snap(pair * 2), 0)
                    stage(sp.snap(pair * 2 + 1), 1)
                w(sp, "wo_done", NT)
                sp.wait_ge(S["ld_wo"], 16 * (2 * call + 1))
                load_wo(1)
                w(sp, "hid_mm", 3 * NT)
                sp.wait_ge(S["ld_w1"], 16 * (2 * call + 1))
                load_w1(1)
                w(sp, "w2_done", NT)
                sp.wait_ge(S["ld_w2"], 32 * (2 * call + 1))
                load_w2(1)
                with sp.Fori(last // 2, NG // 2) as pair:
                    stage(sp.snap(pair * 2), 0)
                    stage(sp.snap(pair * 2 + 1), 1)

            @block.tensor
            def _(pe):
                def stage(g, par, on1, on2, on3, on4):
                    if on2:
                        g2, par2 = g - 1, 1 - par
                    if on3:
                        g3, par3 = g - 2, par
                    if on4:
                        g4 = g - 3
                    if on1:
                        layer1 = known(pe, g // NT * (3 * INNER))

                    def project(b, parts=(0, 1, 2)):
                        if b == 0:
                            w(pe, "h_in", 2 * g + 2)
                        if 0 in parts:
                            w(pe, "qk_rotated", 2 * g + b)
                        for k in parts:
                            bank = (*qk_bank, v_bank)[k]
                            if k == 2:
                                w(pe, "v_out", 2 * g + b)
                                if b == 0:
                                    w(pe, "normed", g - 2)
                                else:
                                    w(pe, "hid_done", 3 * g - 6)
                            last = pe.matmul(bank[:, :], h[:, par, b, :],
                                             wqkv_flat[:, bass.ds(layer1 + k * INNER, INNER)],
                                             start=True, stop=True)
                        if 2 in parts:
                            last.then_inc(S["qkv_done"], 1)

                    def similar(b):
                        t = g2 % NT
                        w(pe, "q_out", 2 * g2 + b + 1)
                        w(pe, "k_out", 2 * g2 + b + 1)
                        off = t * P
                        w(pe, "exp_done", 4 * g2 + 2 * b)
                        for half in range(2):
                            pe.matmul(sim_bank[half][:, :].rearrange("p (h n) -> p h n", h=4), identB[:, :],
                                      mask.rearrange("p t n -> p (t n)")[:, bass.ds(off, P)].unsqueeze(1)
                                      .to_broadcast([P, 4, P]),
                                      start=True, stop=False, skip_group_check=True)
                        for hh in range(4):
                            o = hh * P
                            q, k_, kp = qT[:, par2, b, hh], kT[:, par2, b, hh], kT[:, 1 - par2, b, hh]
                            for half in range(2):
                                rows, bank = slice(half * DH, half * DH + DH), sim_bank[half]
                                pe.matmul(bank[0:WIN, o:o + WIN], q[rows, 0:WIN], k_[rows, 0:WIN],
                                          start=False, stop=False, skip_group_check=True)
                                pe.matmul(bank[WIN:P, o:o + P], q[rows, WIN:P], k_[rows, 0:P],
                                          start=False, stop=True, skip_group_check=True)
                                last = pe.matmul(bank[0:WIN, o + WIN:o + P], q[rows, 0:WIN], kp[rows, WIN:P],
                                                 start=False, stop=True, skip_group_check=True)
                                if hh == 3:
                                    last.then_inc(S["sim_done"], 1)

                    def turn_qk(b, m):
                        w(pe, "qk_normed", 2 * m + b + 1)
                        for k in range(2):
                            w(pe, ("p_out_lo", "p_out_hi")[k], 2 * m - 1 + b)
                            w(pe, ("q_out", "k_out")[k], 2 * m + b)
                            for c in range(INNER // P):
                                last = pe.transpose(turn_bank[k][:, c * P:(c + 1) * P],
                                                    rot_a[:, b, k * INNER + c * P:k * INNER + (c + 1) * P], ident)
                            last.then_inc(S["qk_turned"], 1)

                    def turn_p(b, m):
                        w(pe, "p_normed", 2 * m + b + 1)
                        for hd in range(HEADS):
                            if hd % 4 == 0:
                                if b == 1 and on4:
                                    w(pe, "hid_done", 3 * g4 + 1 + hd // 4)
                                w(pe, ("q_out", "k_out")[hd // 4], cap(2 * m + 2 + b, 2 * NG))
                                w(pe, ("p_out_lo", "p_out_hi")[hd // 4], 2 * m + b)
                            last = pe.transpose(turn_bank[hd // 4][:, (hd % 4) * P:(hd % 4 + 1) * P],
                                                prob[:, b, hd, :], ident)
                            if hd % 4 == 3:
                                last.then_inc(S["p_turned"], 1)

                    def attend(b, m, slot):
                        w(pe, "p_out_lo", 2 * m + b + 1)
                        mixed(pe, m, slot)
                        if b == 0:
                            w(pe, "mid_done", m)
                        else:
                            w(pe, "o_out_0", m + 1)
                            if on4:
                                at_least(pe, y_done, G0 + g4 + 1)
                        for pr in range(HEADS // 2):
                            if pr == HEADS // 4:
                                w(pe, "p_out_hi", 2 * m + b + 1)
                            for half, vals in enumerate((v_mix, v_nat)):
                                for sub in range(2):
                                    hd = 2 * pr + sub
                                    last = pe.matmul(
                                        m_bank[sub * DH:(sub + 1) * DH, pr * P + half * WIN:pr * P + (half + 1) * WIN],
                                        vals[:, slot, b, hd * DH:(hd + 1) * DH],
                                        probT[:, b, hd, half * WIN:(half + 1) * WIN],
                                        start=True, stop=True, skip_group_check=True)
                        last.then_inc(S["pv_done"], 1)

                    def out_proj():
                        pe.wait_ge(S["ld_wo"], (g3 // NT + (2 * call + 1)) * 16)
                        w(pe, "o_out_0", g3 + 1)
                        w(pe, "o_out_1", g3 + 1)
                        for c in range(INNER // P):
                            last = pe.matmul(m_bank[:, 0:BP], wo[:, c, :], oT[:, par3, c].rearrange("p b n -> p (b n)"),
                                             start=(c == 0), stop=(c == INNER // P - 1), skip_group_check=True)
                        last.then_inc(S["wo_done"], 1)

                    def take_mean_off():
                        w(pe, "h2_in", 2 * g3 + 2)
                        if on1:
                            w(pe, "v_out", 2 * g + 2)
                        elif on4:
                            w(pe, "hid_done", 3 * g4 + 3)
                        pe.matmul(v_bank[:, BP:2 * BP], centre, h2[:, :, :].rearrange("p b n -> p (b n)"),
                                  start=True, stop=True, skip_group_check=True).then_inc(S["centred"], 1)

                    def variance():
                        w(pe, "squared", g3 + 1)
                        pe.matmul(v_bank[:, 0:BP], mean, c_sq[:, :], start=True, stop=True, skip_group_check=True)\
                            .then_inc(S["var_done"], 1)

                    def hidden(c):
                        w(pe, "affine", g4 + 1)
                        if c == HORDER[0]:
                            pe.wait_ge(S["ld_w1"], (g4 // NT + (2 * call + 1)) * 16)
                        if hid_bank[c] is v_bank:
                            w(pe, "v_out", cap(2 * g4 + 7, 2 * NG))
                        else:
                            k = turn_bank.index(hid_bank[c])
                            w(pe, ("q_out", "k_out")[k], cap(2 * g4 + 5, 2 * NG))
                            w(pe, ("p_out_lo", "p_out_hi")[k], cap(2 * g4 + 3, 2 * NG))
                        c0, m = HC[c]
                        for k in range(2):
                            last = pe.matmul(hid_bank[c][0:m, k * BP:(k + 1) * BP],
                                             w1[:, k * HID + c0:k * HID + c0 + m], hn[:, :],
                                             start=True, stop=True, skip_group_check=True)
                        last.then_inc(S["hid_mm"], 1)

                    def down():
                        w(pe, "hid_done", 3 * g4 + 3)
                        pe.wait_ge(S["ld_w2"], (g4 // NT + (2 * call + 1)) * 32)
                        w(pe, "mid_done", g4 + 1)
                        w(pe, "o_out_0", cap(g4 + 2, NG))
                        for c, (c0, m) in enumerate(HC):
                            last = pe.matmul(m_bank[:, 0:BP], w2[0:m, c, :], hid[0:m, c, :],
                                             start=(c == 0), stop=(c == len(HC) - 1), skip_group_check=True)
                        last.then_inc(S["w2_done"], 1)

                    run(on1, (project, 0))
                    run(on4, *((hidden, c) for c in HORDER))
                    run(on2, (similar, 0))
                    run(on3, (turn_p, 1, g - 2))
                    run(on4, (down,))
                    run(on2, (turn_qk, 1, g - 1))
                    run(on1, (project, 1, (0, 1)))
                    run(on3, (attend, 1, g - 2, par))
                    run(on1, (project, 1, (2,)))
                    run(on3, (out_proj,))
                    run(on2, (similar, 1))
                    run(on3, (take_mean_off,))
                    run(on2, (turn_p, 0, g - 1))
                    run(on3, (variance,))
                    run(on1, (turn_qk, 0, g))
                    run(on2, (attend, 0, g - 1, 1 - par))

                normalise(pe)
                pe.wait_ge(ld_qkv, 16)
                pe.wait_ge(ld_tab, 16 * (3 + 2 * DEPTH))
                pe.wait_ge(S["set_up"], 3 * (call + 1))
                slots(pe, stage)

            @block.scalar
            def _(act):
                def stage(g, par, on1, on2, on3, on4):
                    if on2:
                        g2, par2 = g - 1, 1 - par
                    if on3:
                        g3, par3 = g - 2, par
                    if on4:
                        g4 = g - 3
                        cols_b1 = [known(act, g4 // NT * (2 * len(HC)) + (COL_B1 + len(HC) + c)) for c in HORDER]

                    def square_qk(b):
                        w(act, "qkv_done", 2 * g + b + 1)
                        w(act, "ss_in", 2 * g + b)
                        for k in range(2):
                            act.activation(qk_sq[:, k * INNER:(k + 1) * INNER], qk_bank[k][:, :], ACT.Square)\
                                .then_inc(S["qk_squared"], 1)

                    def norms(b, g):
                        w(act, "ss_clipped", 2 * g + b + 1)
                        act.activation(ss[:, b, 2, :], ss[:, b, 1, :], ACT.Ln, scale=SS_SHIFT).then_inc(S["ss_log"], 1)
                        w(act, "ss_log", 2 * g + b + 1)
                        w(act, "qk_normed", 2 * g + b - 1)
                        act.activation(qk_scale[:, b, :], ss[:, b, 2, :], ACT.Exp, scale=-0.5,
                                       bias=eps_col[:, 1:2]).then_inc(S["qk_inv"], 1)

                    def softmax(b, halves):
                        w(act, "p_turned", 4 * g2 + 2 * b - 2)
                        w(act, "sum_inv", 2 * g2 + b - 1)
                        for half in halves:
                            w(act, "max_done", 4 * g2 + 2 * b + half + 1)
                            for hh in range(4):
                                hd = 2 * hh + half
                                last = act.activation(prob[:, b, hd, :], sim_bank[half][:, hh * P:(hh + 1) * P],
                                                      ACT.Exp, bias=neg_max[:, b, half, hh:hh + 1],
                                                      accum_out=p_sum[:, b, hd:hd + 1])
                            last.then_inc(S["exp_done"], 1)

                    def square_centred():
                        w(act, "centred", g3 + 1)
                        w(act, "var_done", g3)
                        act.activation(c_sq[:, :], v_bank[:, BP:2 * BP], ACT.Square).then_inc(S["squared"], 1)

                    def inverse_std():
                        w(act, "var_done", g3 + 1)
                        act.activation(v_log[:, :], v_bank[:, 0:BP], ACT.Ln, bias=eps_col[:, 0:1])\
                            .then_inc(S["var_log"], 1)
                        w(act, "var_log", g3 + 1)
                        w(act, "normed", g3)
                        act.activation(v_inv[:, :], v_log[:, :], ACT.Exp, scale=-0.5).then_inc(S["var_inv"], 1)

                    def copy_qk(b, m, slot):
                        w(act, "qk_turned", 4 * m + 2 * b + 1)
                        w(act, "sim_done", 4 * m - 6 + 2 * b)
                        act.copy(qT[:, slot, b, :, :], turn_bank[0][:, :].rearrange("p (c n) -> p c n", n=P))\
                            .then_inc(S["q_out"], 1)
                        w(act, "qk_turned", 4 * m + 2 * b + 2)
                        w(act, "sim_done", 4 * m - 2 + 2 * b)
                        act.copy(kT[:, slot, b, :, :], turn_bank[1][:, :].rearrange("p (c n) -> p c n", n=P))\
                            .then_inc(S["k_out"], 1)

                    def copy_p(b, m):
                        w(act, "p_turned", 4 * m + 2 * b + 1)
                        w(act, "pv_done", 2 * m + b - 1)
                        act.copy(probT[:, b, 0:4, :], turn_bank[0][:, :].rearrange("p (c n) -> p c n", n=P))\
                            .then_inc(S["p_out_lo"], 1)

                    def gelu(i):
                        c = HORDER[i]
                        w(act, "hid_mm", 3 * g4 + i + 1)
                        w(act, "hid_done", 3 * g4 - 2 + i)
                        m = HC[c][1]
                        act.activation(gel[0:m, i, :], hid_bank[c][0:m, BP:2 * BP], ACT.Gelu,
                                       bias=cols[0:m, bass.ds(cols_b1[i], 1)]).then_inc(S["gelu_done"], 1)

                    def copy_o():
                        w(act, "pv_done", 2 * g3 + 1)
                        w(act, "wo_done", g3 - 1)
                        act.copy(oT[:, par3, :, 0, :], m_bank[:, :].rearrange("p (c n) -> p c n", n=P))\
                            .then_inc(S["o_out_0"], 1)

                    run(on1, (square_qk, 0))
                    run(on2, (norms, 1, g - 1))
                    run(on4, (act.preload_act_table_set, GELU_SET), (gelu, 0), (gelu, 1), (gelu, 2))
                    run(on3, (copy_o,))
                    run(on4, (act.preload_act_table_set, EXP_SET))
                    run(on3, (copy_p, 1, g - 2))
                    run(on2, (softmax, 0, (0, 1)))
                    run(on2, (copy_qk, 1, g - 1, 1 - par))
                    run(on1, (square_qk, 1), (norms, 0, g))
                    run(on3, (square_centred,))
                    run(on2, (copy_p, 0, g - 1))
                    run(on3, (inverse_std,))
                    run(on1, (copy_qk, 0, g, par))
                    run(on2, (softmax, 1, (0, 1)))

                normalise(act)
                slots(act, stage)

            @block.vector
            def _(dve):
                def shifted(eng, out, buf, at, s_):
                    eng.tensor_copy(out[0:D // 2], buf[0:D // 2, :, bass.ds(at + 1, P)]).then_inc(s_, 1)
                    eng.tensor_copy(out[D // 2:D], buf[D // 2:D, :, bass.ds(at, P)]).then_inc(s_, 1)

                def stage(g, par, on1, on2, on3, on4):
                    if on2:
                        g2, par2 = g - 1, 1 - par
                    if on1:
                        at1 = known(dve, g % NT * P)
                        tab1 = known(dve, g // NT * (4 * NT * DH) + g % NT * DH)
                    if on4:
                        g4 = g - 3
                        at4 = known(dve, g4 % NT * P + 1)
                        col_g, col_b, col_b2 = (known(dve, g4 // NT + c) for c in (COL_LN_G, COL_LN_B, COL_B2))
                        cols_b1 = [known(dve, g4 // NT * (2 * len(HC)) + (COL_B1 + c)) for c in HORDER]
                    if on3:
                        g3, par3 = g - 2, par
                        at3 = known(dve, g3 % NT * P)
                        at3_1 = known(dve, at3 + 1)

                    def take_in():
                        at_least(dve, y_done, G0 + g - 3)
                        w(dve, "qkv_done", 2 * g - 2)
                        shifted(dve, h[:, par], y0, at1, S["h_in"])

                    def copy_values(b):
                        w(dve, "qkv_done", 2 * g + b + 1)
                        w(dve, "pv_done", 2 * g - 3 + b)
                        if b == 0:
                            mixed(dve, g - 1, 1 - par)
                        dve.tensor_copy(v_nat[:, par, b, :], v_bank[:, :]).then_inc(S["v_out"], 1)

                    def rotate(b, k):
                        w(dve, "qk_summed", 2 * g + b - 1)
                        w(dve, "qk_turned", 4 * g + 2 * b - 2)
                        w(dve, "qk_squared", 4 * g + 2 * b + k + 1)
                        x = qk_bank[k][:, :].rearrange("p (h d) -> p h d", d=DH)
                        ra = rot_a[:, b, k * INNER:(k + 1) * INNER].rearrange("p (h d) -> p h d", d=DH)
                        rb = rot_b[:, b, k * INNER:(k + 1) * INNER].rearrange("p (h d) -> p h d", d=DH)
                        HF = DH // 2

                        def tab(i, lo, hi):
                            return rot_flat[:, bass.ds(tab1 + (i * NT * DH + lo), hi - lo)]\
                                .unsqueeze(1).to_broadcast([P, HEADS, hi - lo])
                        dve.tensor_tensor(ra, x, tab(k, 0, DH), ALU.mult)
                        dve.tensor_tensor(rb[:, :, 0:HF], x[:, :, HF:DH], tab(2 + k, 0, HF), ALU.mult)
                        last = dve.tensor_tensor(rb[:, :, HF:DH], x[:, :, 0:HF], tab(2 + k, HF, DH), ALU.mult)
                        if k == 1:
                            last.then_inc(S["qk_rotated"], 1)

                    def norms(b, g):
                        w(dve, "qk_squared", 4 * g + 2 * b + 2)
                        w(dve, "ss_clipped", 2 * g + b - 1)
                        dve.tensor_reduce(ss[:, b, 0, :], qk_sq[:, :].rearrange("p (h d) -> p h d", d=DH),
                                          AX.X, ALU.add).then_inc(S["ss_in"], 1)
                        w(dve, "ss_in", 2 * g + b + 1)
                        w(dve, "ss_log", 2 * g + b - 1)
                        dve.tensor_scalar(ss[:, b, 1, :], ss[:, b, 0, :], 1e-24, None, ALU.max)\
                            .then_inc(S["ss_clipped"], 1)

                    def maxima(b):
                        w(dve, "exp_done", 4 * g2 + 2 * b - 2)
                        for half in range(2):
                            w(dve, "sim_done", 4 * g2 + 2 * b + half + 1)
                            dve.tensor_reduce(neg_max[:, b, half, :],
                                              sim_bank[half][:, :].rearrange("p (h n) -> p h n", n=P),
                                              AX.X, ALU.max, negate=True).then_inc(S["max_done"], 1)

                    def invert_sums(b, m):
                        w(dve, "exp_done", 4 * m + 2 * b + 2)
                        w(dve, "p_normed", 2 * m + b - 1)
                        dve.reciprocal(p_inv[:, b, :], p_sum[:, b, :]).then_inc(S["sum_inv"], 1)

                    def copy_p(b, m):
                        w(dve, "p_turned", 4 * m + 2 * b + 2)
                        w(dve, "pv_done", 2 * m + b - 1)
                        dve.tensor_copy(probT[:, b, 4:8, :], turn_bank[1][:, :].rearrange("p (c n) -> p c n", n=P))\
                            .then_inc(S["p_out_hi"], 1)

                    def copy_o():
                        w(dve, "pv_done", 2 * g3 + 2)
                        w(dve, "wo_done", g3 - 1)
                        dve.tensor_copy(oT[:, par3, :, 1, :], m_bank[:, :].rearrange("p (c n) -> p c n", n=P))\
                            .then_inc(S["o_out_1"], 1)

                    def add_attention():
                        w(dve, "h2_in", 2 * g3)
                        w(dve, "wo_done", g3 + 1)
                        at = bass.ds(at3_1, P)
                        dve.tensor_tensor(y1[:, :, at], y0[:, :, at],
                                          m_bank[:, 0:BP].rearrange("p (b n) -> p b n", b=B), ALU.add)\
                            .then_inc(S["mid_done"], 1)
                        w(dve, "mid_done", g3 + 1)
                        w(dve, "centred", g3)
                        shifted(dve, h2, y1, at3, S["h2_in"])

                    def normalise_mid():
                        w(dve, "var_inv", g4 + 1)
                        w(dve, "affine", g4)
                        dve.tensor_tensor(normed[:, :], v_bank[:, BP:2 * BP], v_inv[:, :], ALU.mult)\
                            .then_inc(S["normed"], 1)
                        w(dve, "normed", g4 + 1)
                        w(dve, "hid_mm", 3 * g4)
                        dve.tensor_scalar(hn[:, :], normed[:, :], cols[:, bass.ds(col_g, 1)],
                                          cols[:, bass.ds(col_b, 1)], ALU.mult, ALU.add).then_inc(S["affine"], 1)

                    def gate(i):
                        c = HORDER[i]
                        if i == 0:
                            w(dve, "w2_done", g4)
                        w(dve, "gelu_done", 3 * g4 + i + 1)
                        m = HC[c][1]
                        dve.scalar_tensor_tensor(hid[0:m, c, :], hid_bank[c][0:m, 0:BP],
                                                 cols[0:m, bass.ds(cols_b1[i], 1)],
                                                 gel[0:m, i, :], ALU.add, ALU.mult).then_inc(S["hid_done"], 1)

                    def give_out():
                        w(dve, "h_in", cap(2 * g4 + 4, 2 * NG))
                        w(dve, "w2_done", g4 + 1)
                        at = bass.ds(at4, P)
                        dve.scalar_tensor_tensor(y0[:, :, at], m_bank[:, 0:BP].rearrange("p (b n) -> p b n", b=B),
                                                 cols[:, bass.ds(col_b2, 1)], y1[:, :, at], ALU.add, ALU.add)\
                            .then_inc(y_done, 1)

                    run(on1, (take_in,))
                    run(on4, (normalise_mid,))
                    run(on2, (norms, 1, g - 1))
                    run(on1, (copy_values, 0))
                    run(on3, (invert_sums, 1, g - 2))
                    run(on1, (rotate, 0, 0))
                    run(on4, (gate, 0), (gate, 1), (gate, 2))
                    run(on1, (rotate, 0, 1))
                    run(on3, (copy_p, 1, g - 2))
                    run(on4, (give_out,))
                    run(on2, (maxima, 0))
                    run(on1, (norms, 0, g))
                    run(on3, (copy_o,))
                    run(on2, (invert_sums, 0, g - 1))
                    run(on1, (copy_values, 1), (rotate, 1, 0))
                    run(on3, (add_attention,))
                    run(on1, (rotate, 1, 1))
                    run(on2, (copy_p, 0, g - 1), (maxima, 1))
                normalise(dve)
                dve.wait_ge(S["set_up"], 3 * (call + 1))
                dve.wait_ge(tab_done, 6 * DEPTH)
                slots(dve, stage)

            @block.gpsimd
            def _(pool):
                def stage(g, par, on1, on2, on3, on4):
                    def sum_halves(b):
                        w(pool, "qk_rotated", 2 * g + b + 1)
                        pool.tensor_tensor(rot_b[:, b, :], rot_a[:, b, :], rot_b[:, b, :], ALU.add)\
                            .then_inc(S["qk_summed"], 1)

                    def scale_qk(b, g):
                        w(pool, "qk_summed", 2 * g + b + 1)
                        w(pool, "qk_inv", 2 * g + b + 1)
                        pool.tensor_tensor(rot_a[:, b, :].rearrange("p (h d) -> p h d", d=DH),
                                           rot_b[:, b, :].rearrange("p (h d) -> p h d", d=DH),
                                           qk_scale[:, b, :].unsqueeze(2).to_broadcast([P, 2 * HEADS, DH]), ALU.mult)\
                            .then_inc(S["qk_normed"], 1)

                    def scale_probs(b, m):
                        w(pool, "sum_inv", 2 * m + b + 1)
                        pool.tensor_tensor(prob[:, b], prob[:, b],
                                           p_inv[:, b, :].unsqueeze(2).to_broadcast([P, HEADS, P]), ALU.mult)\
                            .then_inc(S["p_normed"], 1)

                    run(on3, (scale_probs, 1, g - 2))
                    run(on2, (scale_qk, 1, g - 1))
                    run(on1, (sum_halves, 0))
                    run(on2, (scale_probs, 0, g - 1))
                    run(on1, (scale_qk, 0, g), (sum_halves, 1))

                pool.memset(kT[:, 1], 0.0).then_inc(S["set_up"], 1)
                pool.memset(v_nat[:, 1], 0.0).then_inc(S["set_up"], 1)
                pool.memset(y1[:, :, 0:1], 0.0).then_inc(S["set_up"], 1)
                pool.wait_ge(S["set_up"], 3 * (call + 1))
                slots(pool, stage)


def rwkv(nc, t_in, sb, sem, ps, xT, y0, cols, r_x, normalise, y_ready):
    NSEQ = 2 * B
    HALVES = N // CH
    R, K, V = range(3)
    chunks = [(K, 0), (K, 1), (V, 0), *((R, s) for s in range(NSEQ)), (V, 1),
              *((what, s) for s in range(2, NSEQ) for what in (K, V))]
    chunks = [(what, s, h) for what, s in chunks for h in range(HALVES)]
    keys = [c for c in chunks if c[0] == K]
    others = [c for c in chunks if c[0] != K]
    names = """ld_w ld_out projected keys_in rest_in decay_exp decay_in max_scanned kept decayed shifted clipped
        weights_in den_scanned num_scanned values_in den_scaled den_out num_scaled top_in gated log_in inv_in
        mixed out_done""".split()
    S = {n: sem("r_" + n) for n in names}
    with ExitStack() as stack:
        def s(name, shape, dt=F32):
            return sb("r_" + name, shape, dt, stack)
        w_in = s("w_in", [P, 6 * D])
        w_out = s("w_out", [P, 2, D])
        decay = s("decay", [P, 2])
        rkv = s("rkv", [P, 3, NSEQ, N])
        mx = s("mx", [P, 2, 1 + N])
        diff = s("diff", [P, 2, N])
        NX = 3
        ex = s("ex", [P, NX, 4, N])
        E1, E2, E1S, E2S = range(4)
        ev = s("ev", [P, 2, 2, N])
        num = s("num", [P, 2, 1 + N])
        den = s("den", [P, 2, 1 + N])
        mixed = rkv[:, K]

        def first_col(d):
            return cols[:, COL_R + 2 * d + 1:COL_R + 2 * d + 2]

        with nc.Block() as block:
            @block.sync
            def _(sp):
                sp.dma_start(w_in[:, :], t_in["r_w"]).then_inc(S["ld_w"], 16)
                sp.dma_start(w_out[:, :, :], t_in["r_out"].rearrange("(c p) n -> p c n", p=P))\
                    .then_inc(S["ld_out"], 16)

            @block.tensor
            def _(pe):
                normalise(pe)
                pe.wait_ge(S["ld_w"], 16)
                for i, (what, seq, h) in enumerate(chunks):
                    b, d = divmod(seq, 2)
                    if i >= 8:
                        c = chunks[i - 8]
                        if c[0] == K:
                            pe.wait_ge(S["keys_in"], keys.index(c) + 1)
                        else:
                            pe.wait_ge(S["rest_in"], others.index(c) + 1)
                    y_ready(pe, NCH - 1 if i >= 2 else HALVES * b + h)
                    at = (3 * d + what) * D
                    pe.matmul(ps[i % 8][:, :], w_in[:, at:at + D], y0[:, b, 1 + h * CH:1 + (h + 1) * CH],
                              start=True, stop=True).then_inc(S["projected"], 1)
                pe.wait_ge(S["ld_out"], 16)
                for b in range(B):
                    pe.wait_ge(S["mixed"], 2 * b + 2)
                    for h in range(HALVES):
                        c = HALVES * b + h
                        if b == 0:
                            pe.wait_ge(S["keys_in"], len(keys))
                            pe.wait_ge(S["rest_in"], len(others))
                        for d in range(2):
                            last = pe.matmul(ps[c][:, :], w_out[:, d, :], mixed[:, 2 * b + d, h * CH:(h + 1) * CH],
                                             start=(d == 0), stop=(d == 1))
                        last.then_inc(S["out_done"], 1)

            @block.scalar
            def _(act):
                normalise(act)

                def take(want):
                    for i, c in enumerate(chunks):
                        if not want(*c[:2]):
                            continue
                        what, seq, h = c
                        act.wait_ge(S["projected"], i + 1)
                        hh = h if seq % 2 == 0 else HALVES - 1 - h
                        dst = rkv[:, what, seq, hh * CH:(hh + 1) * CH]
                        if seq % 2:
                            dst = rkv[:, what, seq, hh * CH:(hh + 1) * CH][:, ::-1]
                        act.activation(dst, ps[i % 8][:, :], ACT.Sigmoid if what == R else ACT.Copy)\
                            .then_inc(S["keys_in" if what == K else "rest_in"], 1)

                def weights(q):
                    act.wait_ge(S["shifted"], q + 1)
                    if q >= NX:
                        act.wait_ge(S["mixed"], q - NX + 1)
                    for e, sign in ((E1, 1.0), (E2, -1.0)):
                        act.activation(ex[:, q % NX, e, :], diff[:, q % 2, :], ACT.Relu, scale=sign)\
                            .then_inc(S["clipped"], 1)
                    for e, name, n in ((E1, "clipped", 2 * q + 1), (E2, "clipped", 2 * q + 2),
                                       (E1S, "decayed", q + 1), (E2S, "kept", q + 1)):
                        act.wait_ge(S[name], n)
                        act.activation(ex[:, q % NX, e, :], ex[:, q % NX, e, :], ACT.Exp,
                                       scale=-1.0 if e in (E1, E2) else 1.0)\
                            .then_inc(S["weights_in"], 1)

                def invert(q):
                    bot = ex[:, q % NX, E1S, :]
                    act.wait_ge(S["den_out"], q + 1)
                    act.activation(bot, bot, ACT.Ln).then_inc(S["log_in"], 1)
                    act.wait_ge(S["log_in"], q + 1)
                    act.activation(bot, bot, ACT.Exp, scale=-1.0).then_inc(S["inv_in"], 1)

                act.activation(decay[:, :], cols[:, COL_R:COL_R + 4:2], ACT.Exp).then_inc(S["decay_exp"], 1)
                take(lambda what, seq: what == K and seq <= 1)
                take(lambda what, seq: what == V and seq == 0)
                for q in range(NSEQ):
                    if q >= 1:
                        take(lambda what, seq: what == K and seq == q + 1)
                    weights(q)
                    if q == 0:
                        take(lambda what, seq: what == R)
                        act.preload_act_table_set(EXP_SET)
                    take(lambda what, seq: what == V and seq == q + 1)
                    if q >= 1:
                        invert(q - 1)
                invert(NSEQ - 1)

            @block.vector
            def _(dve):
                normalise(dve)

                def stage_a(q):
                    d, k = q % 2, rkv[:, K, q, :]
                    old, new = mx[:, q % 2, 0:N], mx[:, q % 2, 1:1 + N]
                    dve.wait_ge(S["keys_in"], HALVES * (q + 1))
                    if q >= 2:
                        dve.wait_ge(S["kept"], q - 1)
                        dve.wait_ge(S["decayed"], q - 1)
                        dve.wait_ge(S["clipped"], 2 * (q - 1))
                    dve.tensor_tensor_scan(new, decay[:, d:d + 1].to_broadcast([P, N]), k,
                                           -1e38, ALU.add, ALU.max).then_inc(S["max_scanned"], 1)
                    dve.wait_ge(S["max_scanned"], q + 1)
                    dve.scalar_tensor_tensor(diff[:, q % 2, :], k, first_col(d), old, ALU.add, ALU.subtract)\
                        .then_inc(S["shifted"], 1)
                    if q >= NX:
                        dve.wait_ge(S["mixed"], q - NX + 1)
                    dve.scalar_tensor_tensor(ex[:, q % NX, E1S, :], old, decay[:, d:d + 1], new,
                                             ALU.add, ALU.subtract).then_inc(S["decayed"], 1)

                def stage_b(q):
                    e1, e2, e1s, e2s = (ex[:, q % NX, e, :] for e in range(4))
                    bot, top = e1s, e2s
                    dve.wait_ge(S["weights_in"], 4 * q + 4)
                    if q >= 2:
                        dve.wait_ge(S["top_in"], q - 1)
                    dve.tensor_tensor_scan(den[:, q % 2, 1:1 + N], e1s, e2s, 0.0, ALU.mult, ALU.add)\
                        .then_inc(S["den_scanned"], 1)
                    dve.wait_ge(S["values_in"], 2 * q + 1)
                    dve.tensor_tensor_scan(num[:, q % 2, 1:1 + N], e1s, ev[:, q % 2, 0, :], 0.0,
                                           ALU.mult, ALU.add).then_inc(S["num_scanned"], 1)
                    dve.wait_ge(S["num_scanned"], q + 1)
                    dve.wait_ge(S["den_scanned"], q + 1)
                    dve.tensor_tensor(bot, den[:, q % 2, 0:N], e1, ALU.mult).then_inc(S["den_scaled"], 1)
                    dve.tensor_tensor(top, num[:, q % 2, 0:N], e1, ALU.mult).then_inc(S["num_scaled"], 1)
                    dve.wait_ge(S["den_scaled"], q + 1)
                    dve.tensor_tensor(bot, bot, e2, ALU.add).then_inc(S["den_out"], 1)
                    dve.wait_ge(S["num_scaled"], q + 1)
                    dve.wait_ge(S["values_in"], 2 * q + 2)
                    dve.tensor_tensor(top, top, ev[:, q % 2, 1, :], ALU.add).then_inc(S["top_in"], 1)

                def stage_c(q):
                    dve.wait_ge(S["inv_in"], q + 1)
                    dve.wait_ge(S["gated"], q + 1)
                    dst = mixed[:, q, :] if q % 2 == 0 else mixed[:, q, ::-1]
                    dve.tensor_tensor(dst, ex[:, q % NX, E2S, :], ex[:, q % NX, E1S, :], ALU.mult)\
                        .then_inc(S["mixed"], 1)

                def add_out(b):
                    for h in range(HALVES):
                        c = HALVES * b + h
                        dve.wait_ge(S["out_done"], c + 1)
                        dst = xT[:, b, h * CH:(h + 1) * CH]
                        dve.tensor_tensor(dst, dst, ps[c][:, :], ALU.add).then_inc(r_x, 1)

                dve.wait_ge(S["decay_exp"], 1)
                dve.tensor_scalar(decay[:, :], decay[:, :], -1.0, None, ALU.mult).then_inc(S["decay_in"], 1)
                dve.memset(mx[:, :, 0:1], -1e38).then_inc(S["decay_in"], 1)
                dve.memset(num[:, :, 0:1], 0.0).then_inc(S["decay_in"], 1)
                dve.memset(den[:, :, 0:1], 0.0).then_inc(S["decay_in"], 1)
                dve.wait_ge(S["decay_in"], 4)
                for q in range(NSEQ + 2):
                    if q < NSEQ:
                        stage_a(q)
                    if 1 <= q <= NSEQ:
                        stage_b(q - 1)
                    if q >= 2:
                        stage_c(q - 2)
                    if q == NSEQ:
                        add_out(0)
                add_out(1)

            @block.gpsimd
            def _(pool):
                def keep(q):
                    pool.wait_ge(S["max_scanned"], q + 1)
                    if q >= NX:
                        pool.wait_ge(S["mixed"], q - NX + 1)
                    pool.tensor_tensor(ex[:, q % NX, E2S, :], rkv[:, K, q, :], mx[:, q % 2, 1:1 + N],
                                       ALU.subtract).then_inc(S["kept"], 1)

                def weigh_values(q):
                    pool.wait_ge(S["weights_in"], 4 * q + 4)
                    pool.wait_ge(S["rest_in"], others.index((V, q, HALVES - 1)) + 1)
                    if q >= 2:
                        pool.wait_ge(S["top_in"], q - 1)
                    for e, at in ((E2S, 0), (E2, 1)):
                        pool.tensor_tensor(ev[:, q % 2, at, :], ex[:, q % NX, e, :], rkv[:, V, q, :], ALU.mult)\
                            .then_inc(S["values_in"], 1)

                def gate(q):
                    pool.wait_ge(S["top_in"], q + 1)
                    pool.wait_ge(S["rest_in"], others.index((R, q, HALVES - 1)) + 1)
                    top = ex[:, q % NX, E2S, :]
                    pool.tensor_tensor(top, top, rkv[:, R, q, :], ALU.mult).then_inc(S["gated"], 1)

                for q in range(NSEQ + 2):
                    if q >= 2:
                        gate(q - 2)
                    if q < NSEQ:
                        keep(q)
                    if q < NSEQ:
                        weigh_values(q)


_NAMES = {
    "x": "L0_attn_a_hidden_states", "a_wq": "L0_attn_a_Wq", "a_wk": "L0_attn_a_Wk", "a_wv": "L0_attn_a_Wv",
    "a_wo": "L0_attn_a_Wo", "wqkv": "L0_ffn_wqkv", "q_scale": "L0_ffn_q_scale", "k_scale": "L0_ffn_k_scale",
    "wo": "L0_ffn_wo", "w1": "L0_ffn_w1", "w2": "L0_ffn_w2",
}


def _columns(inputs):
    cols = np.zeros((P, COLS), np.float32)
    for at, name in ((COL_LN_G, "L0_ffn_ln_g"), (COL_LN_B, "L0_ffn_ln_b"), (COL_B2, "L0_ffn_b2")):
        cols[:, at:at + DEPTH] = np.asarray(inputs[name]).T
    b1 = np.asarray(inputs["L0_ffn_b1"]).reshape(DEPTH, 2, HID)
    for l in range(DEPTH):
        for k in range(2):
            for c, (c0, m) in enumerate(HC):
                cols[:m, COL_B1 + (l * 2 + k) * len(HC) + c] = b1[l, k, c0:c0 + m]
    for n, name in enumerate(("time_decay", "time_first", "time_decay_rev", "time_first_rev")):
        cols[:, COL_R + n] = np.asarray(inputs["L0_attn_b_" + name])
    return cols


def kernel(**inputs):
    import concourse.bacc as bacc
    from concourse.bass_utils import run_bass_kernel_spmd

    nc = bacc.Bacc("TRN2", target_bir_lowering=False, num_devices=1)
    arrays = {k: np.ascontiguousarray(inputs[v]) for k, v in _NAMES.items()}
    arrays["cols"] = _columns(inputs)
    arrays["r_w"] = np.ascontiguousarray(np.asarray(inputs["L0_attn_b_rkv_w"]).T)
    arrays["r_out"] = np.ascontiguousarray(np.asarray(inputs["L0_attn_b_out_w"]).T)
    arrays.update(zip(("square", "mask", "identB", "rot"), shape_constants()))
    t_in = {k: nc.dram_tensor(f"in_{k}", a.shape, mybir.dt.from_np(a.dtype), kind="ExternalInput").ap()
            for k, a in arrays.items()}
    out = nc.dram_tensor("out", (B, N, D), F32, kind="ExternalOutput").ap()
    build(nc, t_in, out)
    r = run_bass_kernel_spmd(nc, [{f"in_{k}": a for k, a in arrays.items()}], core_ids=[0])
    return r.results[0]["out"]
```
